# Optimizing a Trainium2 kernel written in Bass

```python
import numpy as np
import jax
import jax.numpy as jnp

def _softmax(x, axis=-1):
    return jax.nn.softmax(x, axis=axis)

def _gelu(x):
    return jax.nn.gelu(x, approximate=True)

def _silu(x):
    return jax.nn.silu(x)

def _sigmoid(x):
    return jax.nn.sigmoid(x)

def _layernorm(x, axis=-1, eps=1e-05):
    m = jnp.mean(x, axis=axis, keepdims=True)
    v = jnp.var(x, axis=axis, keepdims=True)
    return (x - m) / jnp.sqrt(v + eps)

def _scatter_add(tgt, idx, src, axis=0):
    return tgt.at[idx].add(src)

def _segment_sum(src, seg, n):
    return jax.ops.segment_sum(src, seg, n)
kernel_name = 'mk_gnn_ffn_d1_gnn_r32_80f084'

def setup_inputs(seed: int=0):
    np.random.seed(seed)
    _w = jnp.asarray

    def _rec_inputs():
        import jax
        import jax.numpy as jnp
        _gk = jax.random.key(seed)
        x = -8.776e-05 + 1 * jax.random.normal(jax.random.fold_in(_gk, 1), (3125, 256), jnp.float32)
        _s = jax.random.randint(jax.random.fold_in(_gk, 2), (25000,), 0, 3125, jnp.int32)
        _d = jax.random.randint(jax.random.fold_in(_gk, 3), (25000,), 0, 3125, jnp.int32)
        _loop = jnp.arange(3125, dtype=jnp.int32)
        src = jnp.concatenate([_s, _d, _loop])
        dst = jnp.concatenate([_d, _s, _loop])
        _o = jnp.argsort(dst, stable=True)
        src = src[_o]
        dst = dst[_o]
        edge_attr_16 = 0.000130101 + 1.00012 * jax.random.normal(jax.random.fold_in(_gk, 11), (53125, 16), jnp.float32)
        return (x, src, dst, edge_attr_16)
    x, src, dst, edge_attr_16 = _rec_inputs()

    def _L0_gnn_setup():
        import jax, jax.numpy as jnp
        import numpy as np
        L = 5
        D = 256
        ED = 16
        N = 625
        E = 10000
        BN_EPS = 1e-05

        def _batchnorm(h, g, b):
            m = jnp.mean(h, axis=0)
            v = jnp.mean((h - m) ** 2, axis=0)
            return g * (h - m) * jax.lax.rsqrt(v + BN_EPS) + b
        key = jax.random.key(seed)
        ks = jax.random.split(key, 16)
        s1 = 1.0 / np.sqrt(ED)
        s2 = 1.0 / np.sqrt(D)
        s3 = 1.0 / np.sqrt(2 * D)
        return {'x': jax.random.normal(ks[0], (N, D), dtype=jnp.float32), 'edge_index': jax.random.randint(ks[1], (2, E), 0, N, dtype=jnp.int32), 'edge_attr': jax.random.normal(ks[2], (E, ED), dtype=jnp.float32), 'ee_w1': jax.random.uniform(ks[3], (L, ED, D), jnp.float32, -s1, s1), 'ee_b1': jax.random.uniform(ks[4], (L, D), jnp.float32, -s1, s1), 'ee_w2': jax.random.uniform(ks[5], (L, D, D), jnp.float32, -s2, s2), 'ee_b2': jax.random.uniform(ks[6], (L, D), jnp.float32, -s2, s2), 'eps': jnp.zeros((L,), jnp.float32), 'mlp_w1': jax.random.uniform(ks[7], (L, D, 2 * D), jnp.float32, -s2, s2), 'mlp_b1': jax.random.uniform(ks[8], (L, 2 * D), jnp.float32, -s2, s2), 'bn1_g': jnp.ones((L, 2 * D), jnp.float32), 'bn1_b': jnp.zeros((L, 2 * D), jnp.float32), 'mlp_w2': jax.random.uniform(ks[9], (L, 2 * D, D), jnp.float32, -s3, s3), 'mlp_b2': jax.random.uniform(ks[10], (L, D), jnp.float32, -s3, s3), 'bn_g': jnp.ones((L, D), jnp.float32), 'bn_b': jnp.zeros((L, D), jnp.float32)}
    _L0_gnn_all = _L0_gnn_setup()
    _L0_gnn_in = {k: v for k, v in _L0_gnn_all.items() if k in ('ee_w1', 'ee_b1', 'ee_w2', 'ee_b2', 'eps', 'mlp_w1', 'mlp_b1', 'bn1_g', 'bn1_b', 'mlp_w2', 'mlp_b2', 'bn_g', 'bn_b')}
    del _L0_gnn_all

    def _L0_ffn_setup():
        import jax, jax.numpy as jnp
        import numpy as np
        B, A = (128, 8)
        IN, OUT = (256, 256)
        SH1, SH2 = (256, 128)
        EH1, EH2 = (128, 64)
        E, TOPK = (4, 2)

        def _shared_mlp(x, W1, b1, W2, b2, W3, b3):
            h = jax.nn.relu(x @ W1 + b1)
            h = jax.nn.relu(h @ W2 + b2)
            return h @ W3 + b3

        def _experts_mlp(x, eW1, eb1, eW2, eb2, eW3, eb3):
            h = jax.nn.relu(jnp.einsum('baf,efh->ebah', x, eW1) + eb1[:, None, None, :])
            h = jax.nn.relu(jnp.einsum('ebah,ehg->ebag', h, eW2) + eb2[:, None, None, :])
            o = jnp.einsum('ebag,ego->ebao', h, eW3) + eb3[:, None, None, :]
            return jnp.moveaxis(o, 0, -1)
        key = jax.random.key(seed)
        ks = jax.random.split(key, 16)
        s = 0.05
        return {'x': jax.random.normal(ks[0], (B, A, IN), jnp.float32), 'sW1': jax.random.normal(ks[1], (IN, SH1), jnp.float32) * s, 'sb1': jnp.zeros((SH1,), jnp.float32), 'sW2': jax.random.normal(ks[2], (SH1, SH2), jnp.float32) * s, 'sb2': jnp.zeros((SH2,), jnp.float32), 'sW3': jax.random.normal(ks[3], (SH2, OUT), jnp.float32) * s, 'sb3': jnp.zeros((OUT,), jnp.float32), 'eW1': jax.random.normal(ks[4], (E, IN, EH1), jnp.float32) * s, 'eb1': jnp.zeros((E, EH1), jnp.float32), 'eW2': jax.random.normal(ks[5], (E, EH1, EH2), jnp.float32) * s, 'eb2': jnp.zeros((E, EH2), jnp.float32), 'eW3': jax.random.normal(ks[6], (E, EH2, OUT), jnp.float32) * s, 'eb3': jnp.zeros((E, OUT), jnp.float32), 'gW': jax.random.normal(ks[7], (IN, E), jnp.float32) * s, 'gb': jnp.zeros((E,), jnp.float32)}
    _L0_ffn_all = _L0_ffn_setup()
    _L0_ffn_in = {k: v for k, v in _L0_ffn_all.items() if k in ('sW1', 'sb1', 'sW2', 'sb2', 'sW3', 'sb3', 'eW1', 'eb1', 'eW2', 'eb2', 'eW3', 'eb3', 'gW', 'gb')}
    del _L0_ffn_all
    return {'x': x, 'src': src, 'dst': dst, 'edge_attr_16': edge_attr_16, 'L0_gnn_ee_w1': _L0_gnn_in['ee_w1'], 'L0_gnn_ee_b1': _L0_gnn_in['ee_b1'], 'L0_gnn_ee_w2': _L0_gnn_in['ee_w2'], 'L0_gnn_ee_b2': _L0_gnn_in['ee_b2'], 'L0_gnn_eps': _L0_gnn_in['eps'], 'L0_gnn_mlp_w1': _L0_gnn_in['mlp_w1'], 'L0_gnn_mlp_b1': _L0_gnn_in['mlp_b1'], 'L0_gnn_bn1_g': _L0_gnn_in['bn1_g'], 'L0_gnn_bn1_b': _L0_gnn_in['bn1_b'], 'L0_gnn_mlp_w2': _L0_gnn_in['mlp_w2'], 'L0_gnn_mlp_b2': _L0_gnn_in['mlp_b2'], 'L0_gnn_bn_g': _L0_gnn_in['bn_g'], 'L0_gnn_bn_b': _L0_gnn_in['bn_b'], 'L0_ffn_sW1': _L0_ffn_in['sW1'], 'L0_ffn_sb1': _L0_ffn_in['sb1'], 'L0_ffn_sW2': _L0_ffn_in['sW2'], 'L0_ffn_sb2': _L0_ffn_in['sb2'], 'L0_ffn_sW3': _L0_ffn_in['sW3'], 'L0_ffn_sb3': _L0_ffn_in['sb3'], 'L0_ffn_eW1': _L0_ffn_in['eW1'], 'L0_ffn_eb1': _L0_ffn_in['eb1'], 'L0_ffn_eW2': _L0_ffn_in['eW2'], 'L0_ffn_eb2': _L0_ffn_in['eb2'], 'L0_ffn_eW3': _L0_ffn_in['eW3'], 'L0_ffn_eb3': _L0_ffn_in['eb3'], 'L0_ffn_gW': _L0_ffn_in['gW'], 'L0_ffn_gb': _L0_ffn_in['gb']}

def reference(x, src, dst, edge_attr_16, L0_gnn_ee_w1, L0_gnn_ee_b1, L0_gnn_ee_w2, L0_gnn_ee_b2, L0_gnn_eps, L0_gnn_mlp_w1, L0_gnn_mlp_b1, L0_gnn_bn1_g, L0_gnn_bn1_b, L0_gnn_mlp_w2, L0_gnn_mlp_b2, L0_gnn_bn_g, L0_gnn_bn_b, L0_ffn_sW1, L0_ffn_sb1, L0_ffn_sW2, L0_ffn_sb2, L0_ffn_sW3, L0_ffn_sb3, L0_ffn_eW1, L0_ffn_eb1, L0_ffn_eW2, L0_ffn_eb2, L0_ffn_eW3, L0_ffn_eb3, L0_ffn_gW, L0_ffn_gb):
    import jax
    import jax.numpy as jnp

    def _L0_gnn_ref(x, edge_index, edge_attr, ee_w1, ee_b1, ee_w2, ee_b2, eps, mlp_w1, mlp_b1, bn1_g, bn1_b, mlp_w2, mlp_b2, bn_g, bn_b):
        import jax, jax.numpy as jnp
        import numpy as np
        L = 5
        D = 256
        ED = 16
        N = 625
        E = 10000
        BN_EPS = 1e-05

        def _batchnorm(h, g, b):
            m = jnp.mean(h, axis=0)
            v = jnp.mean((h - m) ** 2, axis=0)
            return g * (h - m) * jax.lax.rsqrt(v + BN_EPS) + b
        n = x.shape[0]
        src, dst = (edge_index[0], edge_index[1])
        h = x
        for l in range(L):
            e = jax.nn.relu(edge_attr @ ee_w1[l] + ee_b1[l]) @ ee_w2[l] + ee_b2[l]
            msg = jax.nn.relu(h[src] + e)
            agg = jax.ops.segment_sum(msg, dst, num_segments=n)
            z = (1.0 + eps[l]) * h + agg
            z = z @ mlp_w1[l] + mlp_b1[l]
            z = jax.nn.relu(_batchnorm(z, bn1_g[l], bn1_b[l]))
            z = z @ mlp_w2[l] + mlp_b2[l]
            z = _batchnorm(z, bn_g[l], bn_b[l])
            if l < L - 1:
                z = jax.nn.relu(z)
            h = z + h
        return h

    def _L0_ffn_ref(x, sW1, sb1, sW2, sb2, sW3, sb3, eW1, eb1, eW2, eb2, eW3, eb3, gW, gb):
        import jax, jax.numpy as jnp
        import numpy as np
        B, A = (128, 8)
        IN, OUT = (256, 256)
        SH1, SH2 = (256, 128)
        EH1, EH2 = (128, 64)
        E, TOPK = (4, 2)

        def _shared_mlp(x, W1, b1, W2, b2, W3, b3):
            h = jax.nn.relu(x @ W1 + b1)
            h = jax.nn.relu(h @ W2 + b2)
            return h @ W3 + b3

        def _experts_mlp(x, eW1, eb1, eW2, eb2, eW3, eb3):
            h = jax.nn.relu(jnp.einsum('baf,efh->ebah', x, eW1) + eb1[:, None, None, :])
            h = jax.nn.relu(jnp.einsum('ebah,ehg->ebag', h, eW2) + eb2[:, None, None, :])
            o = jnp.einsum('ebag,ego->ebao', h, eW3) + eb3[:, None, None, :]
            return jnp.moveaxis(o, 0, -1)
        all_out = _experts_mlp(x, eW1, eb1, eW2, eb2, eW3, eb3)
        shared = _shared_mlp(x, sW1, sb1, sW2, sb2, sW3, sb3)
        gates = jax.nn.softmax(x @ gW + gb, axis=-1)
        topv, topi = jax.lax.top_k(gates, TOPK)
        topw = jax.nn.softmax(topv, axis=-1)
        sel = jnp.take_along_axis(all_out, topi[:, :, None, :], axis=-1)
        gated = jnp.sum(sel * topw[:, :, None, :], axis=-1)
        return shared + gated
    edge_index = jnp.stack([src, dst])
    x = x + _L0_gnn_ref(_layernorm(x, axis=-1), edge_index, edge_attr_16, L0_gnn_ee_w1, L0_gnn_ee_b1, L0_gnn_ee_w2, L0_gnn_ee_b2, L0_gnn_eps, L0_gnn_mlp_w1, L0_gnn_mlp_b1, L0_gnn_bn1_g, L0_gnn_bn1_b, L0_gnn_mlp_w2, L0_gnn_mlp_b2, L0_gnn_bn_g, L0_gnn_bn_b)
    x = x + _L0_ffn_ref(_layernorm(x, axis=-1)[None], L0_ffn_sW1, L0_ffn_sb1, L0_ffn_sW2, L0_ffn_sb2, L0_ffn_sW3, L0_ffn_sb3, L0_ffn_eW1, L0_ffn_eb1, L0_ffn_eW2, L0_ffn_eb2, L0_ffn_eW3, L0_ffn_eb3, L0_ffn_gW, L0_ffn_gb)[0]
    return x

_drawn_inputs = setup_inputs


def setup_inputs(seed=0):
    import zlib

    import numpy as np

    out = dict(_drawn_inputs(seed))
    spreads = {'L0_gnn_eps': (0.0, 0.515),
     'L0_gnn_bn1_g': (1.0, 0.2),
     'L0_gnn_bn1_b': (0.0, 0.1),
     'L0_gnn_bn_g': (1.0, 0.2),
     'L0_gnn_bn_b': (0.0, 0.1),
     'L0_ffn_sb1': (0.0, 0.8),
     'L0_ffn_sb2': (0.0, 0.57),
     'L0_ffn_sb3': (0.0, 0.322),
     'L0_ffn_eb1': (0.0, 0.8),
     'L0_ffn_eb2': (0.0, 0.8),
     'L0_ffn_eb3': (0.0, 0.359),
     'L0_ffn_gb': (0.0, 0.8)}
    factors = {'L0_gnn_mlp_b1': 64.0,
     'L0_gnn_mlp_b2': 64.0,
     'L0_ffn_eW1': 3.939,
     'L0_ffn_eW2': 3.447,
     'L0_ffn_eW3': 2.771}
    for name, (base, spread) in spreads.items():
        noise = np.random.default_rng([zlib.crc32(name.encode()), seed]).standard_normal(out[name].shape)
        drawn = base * np.exp(spread * noise) if base else spread * noise
        out[name] = jnp.asarray(drawn.astype(out[name].dtype))
    for name, factor in factors.items():
        out[name] = (out[name] * factor).astype(out[name].dtype)
    return out
```

```python
import concourse.bass as bass
from concourse import mybir
from contextlib import ExitStack

F32 = mybir.dt.float32
F32R = mybir.dt.float32r
I32 = mybir.dt.int32
ALU = mybir.AluOpType
ACT = mybir.ActivationFunctionType
AX = mybir.AxisListType.X
ds = bass.ds

N, D, DE, L, E = 3125, 256, 16, 5, 53125
D2 = 2 * D
TP = 125
NT = N // TP
EC = E // TP
GS = 256
NG = (E + NT * (GS - 1)) // GS
SLOTS = NG * GS
UN = 8
NIT = NG // UN
assert NG % UN == 0 and N == NT * TP and E == EC * TP
RW = 2 + DE
SRC, DLOC, ATT = 0, 1, 2
EPS = 1e-5
BIG = 3.0e38
CH = [(t, min(4, NT - t)) for t in range(0, NT, 4)]
NCH = len(CH)
SB = 17
NSB = EC // SB
assert EC == SB * NSB
FILL = 58
NFILL = SLOTS // (128 * FILL)
assert SLOTS == NFILL * 128 * FILL
PK = 4
NPK = NG // PK
assert NG == PK * NPK and NPK % 2 == 0
V_B1, V_G1, V_BB1, V_B2, V_G2, V_BB2, V_EPS, V_FLOOR, NV = 0, 4, 8, 12, 14, 16, 18, 19, 20
NE, EH1, EH2, SH1, SH2 = 4, 128, 64, 256, 128


class Link:

    def __init__(self, eng, sem, base=0):
        self.eng, self.sem, self.base, self.n = eng, sem, base, 0

    def __call__(self, ins):
        self.n += 1
        ins.then_inc(self.sem, 1)
        self.eng.wait_ge(self.sem, self.base + self.n)


def gnn_moe_kernel(nc, x, src, dst, edge_attr, ee_w1, ee_b1, ee_w2, ee_b2, eps, mlp_w1, mlp_b1,
                   bn1_g, bn1_b, mlp_w2, mlp_b2, bn_g, bn_b, sW1, sb1, sW2, sb2, sW3, sb3,
                   eW1, eb1, eW2, eb2, eW3, eb3, gW, gb, out):
    ctx = ExitStack()
    with ctx:
        def sb(name, shape, dt=F32):
            return ctx.enter_context(nc.sbuf_tensor(name, shape, dt))

        def sem(name):
            return ctx.enter_context(nc.semaphore(name))

        rec = nc.dram_tensor("slot_records", [SLOTS, RW], F32, kind="Internal").ap()
        attr_t = nc.dram_tensor("attributes_t", [4 * DE, SLOTS], F32, kind="Internal").ap()
        table = nc.dram_tensor("node_table", [N, D], F32, kind="Internal").ap()

        h = sb("h", [128, NT, D])
        agg = sb("agg", [128, NT, D])
        u = sb("u", [128, 4, N])
        u_flat = u[:, :, :].rearrange("p f n -> p (f n)")
        agg_flat = agg[:, :, :].rearrange("p t d -> p (t d)")
        z2 = agg_flat[:, 0:2 * N].rearrange("p (f n) -> p f n", f=2)
        node_tab = u_flat[:, 0:NT * D].rearrange("p (t d) -> p t d", d=D)
        yT = u_flat[:, 0:2 * N].rearrange("p (f n) -> p f n", f=2)
        attr_raw = u_flat[0:TP, 0:EC * DE].rearrange("p (c w) -> p c w", w=DE)
        scratch = [u_flat[0:TP, EC * DE + k * EC:EC * DE + (k + 1) * EC] for k in range(11)]
        dst_f, bucket, mask, prefix, rank, part, ones_c, dloc = scratch[:8]
        src_i, dst_i, slot_i = (s.bitcast(I32) for s in scratch[8:])

        ident = sb("ident", [128, 128])
        iota_n = sb("iota_n", [128, TP])
        lower = sb("lower", [128, 128])
        ones = sb("ones", [128, 128])
        part_id = sb("part_id", [128, 1])
        w1_high = sb("w1_high", [128, 1])
        w1_low = sb("w1_low", [128, 1])
        vec_all = sb("vec_all", [128, L, NV])
        vec = sb("vec", [128, NV])
        counts = sb("counts", [128, NT])
        cnt_i = sb("cnt_i", [128, NT], I32)
        groups = sb("groups", [128, NT])
        groups_end = sb("groups_end", [128, NT])
        offset = sb("offset", [128, NT])
        gt_f = sb("gt_f", [1, NG])
        g_iota = sb("g_iota", [1, NG])
        group_tile = sb("group_tile", [1, NG], I32)
        def carve(*shape):
            start = carve.at
            size = 1
            for k in shape:
                size *= k
            carve.at = start + size
            assert carve.at <= NT * D
            letters = "abcd"[:len(shape)]
            return agg_flat[:, start:carve.at].rearrange(
                f"p ({' '.join(letters)}) -> p {' '.join(letters)}", **dict(zip(letters, shape)))

        carve.at = 0
        clear = carve(FILL, RW)
        stage = carve(2, SB, RW)
        stage_ix = carve(2, SB).bitcast(I32)
        att_in = carve(2, 2 * PK, RW)
        att_hl = carve(2, 2 * PK, 2 * DE)
        att_t = carve(2, PK * GS)[0:2 * DE, :, :]

        KA = 4 * DE + 2
        w1_raw = sb("w1_raw", [KA, D])
        w1_h = sb("w1_h", [KA, D], F32R)
        w1_l = sb("w1_l", [KA, D], F32R)
        w1_s = sb("w1_s", [KA, D], F32R)
        w2_raw = sb("w2_raw", [128, 2, D])
        w2_h = sb("w2_h", [128, 2, D], F32R)
        w2_l = sb("w2_l", [128, 2, D], F32R)
        b2_all = sb("b2_all", [128, D])
        m1 = sb("m1", [128, 2, D2])
        m2 = sb("m2", [128, 4, D])

        at = sb("at", [KA, UN, GS], F32R)
        meta = sb("meta", [128, UN, 2, 2], I32)
        meta_f = meta[:, :, :, :].bitcast(F32)
        hid_h = sb("hid_h", [128, 2, 2, GS], F32R)
        hid_l = sb("hid_l", [128, 2, 2, GS], F32R)
        e_sb = sb("e_sb", [128, 4, 2, D])
        msg_h = sb("msg_h", [128, 2, 2, D], F32R)
        msg_l = sb("msg_l", [128, 2, 2, D], F32R)
        pick = sb("pick", [128, 2, 2, TP + 1], F32R)

        zT = sb("zT", [128, 2, 2, 500])
        v = sb("v", [128, 2, 4, 500])
        st1 = sb("st1", [128, 4, NCH, 6])
        st2 = sb("st2", [128, 2, NCH, 6])
        mv = sb("mv", [128, NT, 2])
        st_ln = sb("st_ln", [128, NT, 6])
        r_a, r_b, r_y, r_t, r_s, r_o = (sb(f"r{k}", [128, NT]) for k in range(6))

        sW1_s = sb("sW1_s", [128, 2, SH1])
        sW2_s = sb("sW2_s", [128, 2, SH2])
        sW3_s = sb("sW3_s", [128, D])
        eW1_s = sb("eW1_s", [128, NE, 2, EH1])
        eW2_s = sb("eW2_s", [128, NE, 2 * EH2])
        eW3_s = sb("eW3_s", [128, 2, D])
        gW_s = sb("gW_s", [128, 2, NE])
        gb_s = sb("gb_s", [128, NE])
        sb1_s = sb("sb1_s", [128, 2])
        sb2_s = sb("sb2_s", [128, 1])
        eb1_s = sb("eb1_s", [128, NE])
        eb2_s = sb("eb2_s", [128, 2])
        b_out = sb("b_out", [1 + NE, D])
        lg = sb("lg", [128, NT, NE])
        pr = sb("pr", [128, NT, NE])
        rk = sb("rk", [128, NE, NT])
        cmp = sb("cmp", [128, NT])
        w5 = sb("w5", [128, NT, 1 + NE])
        sel = sb("sel", [1 + NE, 2, 128])
        wT = sb("wT", [1 + NE, 2, 500])

        ps = ctx.enter_context(nc.psum_tensor("ps", [128, 8, 512], F32))

        edges_in, x_in, vec_in, moe_in = sem("edges_in"), sem("x_in"), sem("vec_in"), sem("moe_in")
        consts, pool_own = sem("consts"), sem("pool_own")
        zeros_made, filled = sem("zeros_made"), sem("filled")
        counts_made, sums_made, slots_made = sem("counts_made"), sem("sums_made"), sem("slots_made")
        pool_pace, dve_pace = sem("pool_pace"), sem("dve_pace")
        staged = sem("staged")
        scattered = [sem(f"scattered{b}") for b in range(2)]
        d_pre, d_lay, d_moe = sem("d_pre"), sem("d_lay"), sem("d_moe")
        att_loaded = [sem(f"att_loaded{b}") for b in range(2)]
        att_high, att_low, att_tr, att_ev = sem("att_high"), sem("att_low"), sem("att_tr"), sem("att_ev")
        att_out = [sem(f"att_out{b}") for b in range(2)]
        sqrt_ask, sqrt_done = sem("sqrt_ask"), sem("sqrt_done")
        h_rows, tab_made, tab_out = sem("h_rows"), sem("tab_made"), sem("tab_out")
        w_in, w_high, w_ready = sem("w_in"), sem("w_high"), sem("w_ready")
        m_in = sem("m_in")
        at_in = [sem(f"at_in{b}") for b in range(UN)]
        meta_in = [sem(f"meta_in{b}") for b in range(UN)]
        gathered = [sem(f"gathered{b}") for b in range(4)]
        mm1, mm2, mm3 = sem("mm1"), sem("mm2"), sem("mm3")
        hid_high, hid_low, e_out = sem("hid_high"), sem("hid_low"), sem("e_out")
        msg_high, msg_low, picked, added = sem("msg_high"), sem("msg_low"), sem("picked"), sem("added")
        z_tr, z_ev0, z_ev1 = sem("z_tr"), sem("z_ev0"), sem("z_ev1")
        u_mm, u_ev, bn1_ready = sem("u_mm"), sem("u_ev"), sem("bn1_ready")
        v_made, z2_mm, z2_ev, bn2_ready = sem("v_made"), sem("z2_mm"), sem("z2_ev"), sem("bn2_ready")
        zn_made, zn_tr = sem("zn_made"), sem("zn_tr")
        xr_in, y_made, y_tr, y_ev0, y_ev1 = sem("xr_in"), sem("y_made"), sem("y_tr"), sem("y_ev0"), sem("y_ev1")
        lg_mm, lg_ev, ex_ask, ex_done, w_made = (sem("lg_mm"), sem("lg_ev"), sem("ex_ask"),
                                                 sem("ex_done"), sem("w_made"))
        a_mm, a_ev, d_mm, d_ev = sem("a_mm"), sem("a_ev"), sem("d_mm"), sem("d_ev")
        out_made, out_done = sem("out_made"), sem("out_done")

        def rsqrt(link, dve, var, rows, n, asked):
            a, b, y, t = (r[0:rows, 0:n] for r in (r_a, r_b, r_y, r_t))
            link(nc.vector.tensor_scalar(a, var, EPS, None, ALU.add))
            nc.vector.reciprocal(b, a).then_inc(sqrt_ask, 1)
            dve.wait_ge(sqrt_done, asked)
            link(nc.vector.tensor_tensor(t, y, y, ALU.mult))
            link(nc.vector.tensor_tensor(t, t, a, ALU.mult))
            link(nc.vector.tensor_scalar(t, t, -0.5, 1.5, ALU.mult, ALU.add))
            link(nc.vector.tensor_tensor(y, y, t, ALU.mult))
            return y

        def sqrt_for(act, rows, n, asked):
            act.wait_ge(sqrt_ask, asked)
            nc.scalar.activation(r_y[0:rows, 0:n], r_b[0:rows, 0:n], ACT.Sqrt).then_inc(sqrt_done, 1)

        def layer_norm(link, dve, a, o, asked, made):
            for t in range(NT):
                nc.vector.bn_stats(st_ln[0:TP, t, :], a[0:TP, t, :]).then_inc(link.sem, 1)
            link.n += NT
            dve.wait_ge(link.sem, link.base + link.n)
            for t in range(NT):
                nc.vector.bn_aggr(mv[0:TP, t, :], st_ln[0:TP, t, :]).then_inc(link.sem, 1)
            link.n += NT
            dve.wait_ge(link.sem, link.base + link.n)
            y = rsqrt(link, dve, mv[0:TP, :, 1], TP, NT, asked)
            for t in range(NT):
                nc.vector.tensor_scalar(o[0:TP, t, :], a[0:TP, t, :], mv[0:TP, t, 0:1], y[0:TP, t:t + 1],
                                        ALU.subtract, ALU.mult).then_inc(made, 1)

        ctx.enter_context(nc.allow_non_contiguous_dma(reason="small vectors and slot records"))

        with nc.Block() as block:
            @block.sync
            def _(sp):
                sp.dma_start(dst_i, dst.rearrange("(p c) -> p c", p=TP)).then_inc(edges_in, 16)
                sp.dma_start(src_i, src.rearrange("(p c) -> p c", p=TP)).then_inc(edges_in, 16)
                sp.dma_start(attr_raw, edge_attr.rearrange("(p c) w -> p c w", p=TP)).then_inc(edges_in, 16)
                sp.dma_start(h[0:TP, :, :], x.rearrange("(t p) d -> p t d", p=TP)).then_inc(x_in, 16)
                for l in range(L):
                    for col, k, a in ((V_B1, 4, mlp_b1), (V_G1, 4, bn1_g), (V_BB1, 4, bn1_b),
                                      (V_B2, 2, mlp_b2), (V_G2, 2, bn_g), (V_BB2, 2, bn_b)):
                        sp.dma_start(vec_all[:, l, col:col + k],
                                     a[l, :].rearrange("(f p) -> p f", p=128)).then_inc(vec_in, 16)
                sp.dma_start(vec_all[:, :, V_EPS], eps.unsqueeze(0).to_broadcast([128, L])).then_inc(vec_in, 16)
                moe = [(sW1_s[:, :, :], sW1.rearrange("(k p) f -> p k f", p=128)),
                       (sW2_s[:, :, :], sW2.rearrange("(k p) f -> p k f", p=128)),
                       (sW3_s[:, :], sW3),
                       (gW_s[:, :, :], gW.rearrange("(k p) e -> p k e", p=128)),
                       (gb_s[:, :], gb.unsqueeze(0).to_broadcast([128, NE])),
                       (sb1_s[:, :], sb1.rearrange("(f p) -> p f", p=128)),
                       (sb2_s[:, :], sb2.rearrange("(f p) -> p f", p=128)),
                       (eb1_s[:, :], eb1.rearrange("e p -> p e")),
                       (b_out[0:1, :], sb3.unsqueeze(0)),
                       (b_out[1:1 + NE, :], eb3)]
                for e in range(NE):
                    half = slice((e % 2) * EH2, (e % 2 + 1) * EH2)
                    moe += [(eW1_s[:, e, :, :], eW1[e, :, :].rearrange("(k p) f -> p k f", p=128)),
                            (eW2_s[:, e, half], eW2[e, :, :]),
                            (eW3_s[half, e // 2, :], eW3[e, :, :]),
                            (eb2_s[half, e // 2:e // 2 + 1], eb2[e, :].unsqueeze(1))]
                sp.wait_ge(zeros_made, 2)
                for o, i in moe:
                    sp.dma_start(o, i).then_inc(moe_in, 16)
                sp.wait_ge(vec_in, 16 * (6 * L + 1))
                sp.wait_ge(moe_in, 16 * len(moe))
                sp.wait_ge(scattered[0], 16 * SB * ((NSB + 1) // 2))
                sp.wait_ge(scattered[1], 16 * SB * (NSB // 2))

                def load_att(it, b):
                    sp.dma_start(att_in[:, b, :, :].rearrange("p (k j) w -> p k (j w)", k=PK),
                                 rec[ds(it * PK * GS, PK * GS), :]
                                 .rearrange("(k p j) w -> p k (j w)", k=PK, p=128)).then_inc(att_loaded[b], 16)

                def store_att(it, b):
                    sp.wait_ge(att_ev, it + 1)
                    for half in range(2):
                        sp.dma_start(attr_t[half * 2 * DE:(half + 1) * 2 * DE, ds(it * PK * GS, PK * GS)],
                                     att_t[:, b, :]).then_inc(att_out[b], 16)

                load_att(0, 0)
                load_att(1, 1)
                for b in range(2):
                    store_att(b, b)
                    load_att(b + 2, b)
                with sp.Fori(1, NPK // 2 - 1) as i:
                    for b in range(2):
                        store_att(2 * i + b, b)
                        load_att(2 * i + 2 + b, b)
                for b in range(2):
                    store_att(NPK - 2 + b, b)
                for b in range(2):
                    sp.wait_ge(att_out[b], 16 * NPK)

            @block.gpsimd
            def _(pool):
                gp = nc.gpsimd
                gp.memset(ident[:, :], 0.0).then_inc(pool_own, 1)
                gp.memset(lower[:, :], 1.0).then_inc(pool_own, 1)
                gp.memset(ones[:, :], 1.0).then_inc(pool_own, 1)
                gp.memset(sel[:, :, :], 0.0).then_inc(pool_own, 1)
                pool.wait_ge(pool_own, 4)
                gp.affine_select(out=ident[:, :], in_=ident[:, :], compare_op=ALU.not_equal, fill=1.0,
                                 base=0, pattern=[[-1, 128]], channel_multiplier=1).then_inc(consts, 1)
                gp.affine_select(out=lower[:, :], in_=lower[:, :], compare_op=ALU.is_gt, fill=0.0,
                                 base=0, pattern=[[1, 128]], channel_multiplier=-1).then_inc(consts, 1)
                gp.affine_select(out=sel[:, :, :].rearrange("p q (r c) -> p q r c", r=2),
                                 in_=sel[:, :, :].rearrange("p q (r c) -> p q r c", r=2),
                                 compare_op=ALU.not_equal, fill=1.0, base=1,
                                 pattern=[[2, 2], [1, 2], [0, EH2]], channel_multiplier=-1).then_inc(consts, 1)
                gp.iota(iota_n[:, :], pattern=[[1, TP]], base=0, channel_multiplier=0,
                        allow_small_or_imprecise_dtypes=True).then_inc(consts, 1)
                gp.iota(part_id[:, :], pattern=[[0, 1]], base=0, channel_multiplier=1,
                        allow_small_or_imprecise_dtypes=True).then_inc(consts, 1)
                gp.iota(g_iota[:, :], pattern=[[1, NG]], base=0, channel_multiplier=0,
                        allow_small_or_imprecise_dtypes=True).then_inc(consts, 1)
                pool.wait_ge(filled, 16 * NFILL)

                def scatter(k, b):
                    pool.wait_ge(staged, 4 * (k + 1))
                    pool.sem_inc(pool_pace)
                    for c in range(SB):
                        gp.indirect_dma_start(rec, bass.IndirectOffsetOnAxis(ap=stage_ix[0:TP, b, c:c + 1], axis=0),
                                              stage[0:TP, b, c, :], None).then_inc(scattered[b], 16)

                with pool.Fori(0, NSB // 2) as i:
                    scatter(2 * i, 0)
                    scatter(2 * i + 1, 1)
                scatter(NSB - 1, 0)

            @block.scalar
            def _(act):
                act.wait_ge(zeros_made, 2)
                fill = rec.rearrange("(c p r) w -> c p r w", c=NFILL, p=128)
                for c in range(NFILL):
                    act.dma_start(fill[c], clear[:, :, :]).then_inc(filled, 16)
                act.wait_ge(edges_in, 48)
                act.wait_ge(slots_made, 1)

                def stage_block(k, b):
                    cols = ds(k * SB, SB)
                    o = stage[0:TP, b, :, :]
                    nc.scalar.copy(o[:, :, ATT:RW], attr_raw[:, cols, :]).then_inc(staged, 1)
                    nc.scalar.copy(o[:, :, DLOC], dloc[:, cols]).then_inc(staged, 1)
                    nc.scalar.copy(o[:, :, SRC].bitcast(I32), src_i[:, cols]).then_inc(staged, 1)
                    nc.scalar.copy(stage_ix[0:TP, b, :], slot_i[:, cols]).then_inc(staged, 1)

                stage_block(0, 0)
                stage_block(1, 1)
                with act.Fori(1, NSB // 2) as i:
                    for b in range(2):
                        act.wait_ge(scattered[b], i * 16 * SB)
                        stage_block(2 * i + b, b)
                act.wait_ge(scattered[0], NSB // 2 * 16 * SB)
                stage_block(NSB - 1, 0)
                sqrt_for(act, TP, NT, 1)

                def high_part(it, b, turn, first):
                    act.wait_ge(att_loaded[b], turn * 16)
                    if not first:
                        act.wait_ge(att_tr, it - 1)
                    nc.scalar.copy(att_hl[:, b, :, 0:DE].bitcast(F32R), att_in[:, b, :, ATT:RW]).then_inc(att_high, 1)

                def evacuate(it, b, turn, first):
                    act.wait_ge(att_tr, it + 1)
                    if not first:
                        act.wait_ge(att_out[b], (turn - 1) * 32)
                    nc.scalar.copy(att_t[:, b, :], ps[0:2 * DE, 2 * b:2 * b + 2, :]
                                   .rearrange("p a c -> p (a c)")).then_inc(att_ev, 1)

                for b in range(2):
                    high_part(b, b, 1, True)
                    evacuate(b, b, 1, True)
                with act.Fori(1, NPK // 2) as i:
                    for b in range(2):
                        high_part(2 * i + b, b, i + 1, False)
                        evacuate(2 * i + b, b, i + 1, False)

            @block.vector
            def _(dve):
                vc = nc.vector
                link = Link(dve, d_pre)
                link(vc.memset(clear[:, :, :], 0.0))
                vc.memset(clear[:, :, DLOC], -1.0).then_inc(zeros_made, 1)
                vc.memset(eW2_s[:, :, :], 0.0).then_inc(zeros_made, 1)
                vc.memset(at[4 * DE:KA, :, :].bitcast(F32), 1.0).then_inc(d_pre, 1)
                vc.memset(ones_c, 1.0).then_inc(d_pre, 1)
                vc.memset(bucket, 0.0).then_inc(d_pre, 1)
                vc.memset(counts[:, :], 0.0).then_inc(d_pre, 1)
                link.n += 4
                dve.wait_ge(d_pre, link.n)
                dve.wait_ge(edges_in, 48)
                link(vc.tensor_copy(dst_f, dst_i))
                for b in range(1, NT):
                    link(vc.scalar_tensor_tensor(out=bucket, in0=dst_f, scalar=float(b * TP), in1=bucket,
                                                 op0=ALU.is_ge, op1=ALU.add))
                link(vc.scalar_tensor_tensor(out=dloc, in0=bucket, scalar=-float(TP), in1=dst_f,
                                             op0=ALU.mult, op1=ALU.add))
                link(vc.memset(rank, 0.0))
                for b in range(NT):
                    link(vc.tensor_scalar(mask, bucket, float(b), None, ALU.is_equal))
                    link(vc.tensor_tensor_scan(prefix, ones_c, mask, 0.0, ALU.mult, ALU.add))
                    link(vc.tensor_copy(counts[0:TP, b:b + 1], prefix[:, EC - 1:EC]))
                    link(vc.tensor_tensor(part, mask, prefix, ALU.mult))
                    last = vc.tensor_tensor(rank, rank, part, ALU.add)
                    if b < NT - 1:
                        link(last)
                last.then_inc(counts_made, 1)
                dve.wait_ge(sums_made, 1)
                link(vc.tensor_scalar(cnt_i[:, :], ps[:, 1, 0:NT], float(GS - 1), None, ALU.add))
                link(vc.tensor_scalar(cnt_i[:, :], cnt_i[:, :], GS.bit_length() - 1, None,
                                      ALU.logical_shift_right))
                link(vc.tensor_copy(groups[:, :], cnt_i[:, :]))
                link(vc.tensor_tensor_scan(groups_end[:, :], ones[:, 0:NT], groups[:, :], 0.0,
                                           ALU.mult, ALU.add))
                link(vc.tensor_tensor(offset[:, :], groups_end[:, :], groups[:, :], ALU.subtract))
                link(vc.tensor_scalar(offset[:, :], offset[:, :], float(GS), -1.0, ALU.mult, ALU.add))
                link(vc.tensor_tensor(offset[:, :], offset[:, :], ps[:, 0, 0:NT], ALU.add))
                for b in range(NT):
                    link(vc.tensor_scalar(part, bucket, float(b), offset[0:TP, b:b + 1], ALU.is_equal, ALU.mult))
                    link(vc.tensor_tensor(rank, rank, part, ALU.add))
                vc.tensor_copy(slot_i, rank).then_inc(slots_made, 1)
                link(vc.memset(gt_f[:, :], 0.0))
                for b in range(NT - 1):
                    link(vc.scalar_tensor_tensor(out=gt_f[:, :], in0=g_iota[:, :], scalar=groups_end[0:1, b:b + 1],
                                                 in1=gt_f[:, :], op0=ALU.is_ge, op1=ALU.add))
                link(vc.tensor_copy(group_tile[:, :], gt_f[:, :]))
                link(vc.tensor_scalar(w1_low[:, :], part_id[:, :], float(4 * DE), None, ALU.is_equal))
                link(vc.tensor_scalar(w1_high[:, :], part_id[:, :], float(2 * DE), None, ALU.is_lt))
                link(vc.tensor_tensor(w1_high[:, :], w1_high[:, :], w1_low[:, :], ALU.add))
                link(vc.tensor_scalar(w1_low[:, :], w1_high[:, :], -1.0, 1.0, ALU.mult, ALU.add))
                dve.wait_ge(vec_in, 16 * (6 * L + 1))
                link(vc.tensor_scalar(vec_all[:, :, V_EPS], vec_all[:, :, V_EPS], 1.0, None, ALU.add))
                link(vc.memset(vec_all[:, :, V_FLOOR], 0.0))
                link(vc.memset(vec_all[:, L - 1:L, V_FLOOR], -BIG))
                dve.wait_ge(x_in, 16)
                layer_norm(link, dve, h, h, 1, h_rows)

                def low_part(it, b):
                    dve.wait_ge(att_high, it + 1)
                    vc.tensor_tensor(att_hl[:, b, :, DE:2 * DE], att_in[:, b, :, ATT:RW], att_hl[:, b, :, 0:DE],
                                     ALU.subtract).then_inc(att_low, 1)

                with dve.Fori(0, NPK // 2) as i:
                    for b in range(2):
                        low_part(2 * i + b, b)

            @block.tensor
            def _(pe):
                pe.wait_ge(counts_made, 1)
                pe.wait_ge(consts, 6)
                nc.tensor.matmul(ps[:, 0, 0:NT], lower[:, :], counts[:, :], start=True, stop=True)
                nc.tensor.matmul(ps[:, 1, 0:NT], ones[:, :], counts[:, :], start=True, stop=True)\
                    .then_inc(sums_made, 1)
                pe.wait_ge(slots_made, 1)

                def transposes(it, b, first):
                    pe.wait_ge(att_low, it + 1)
                    if not first:
                        pe.wait_ge(att_ev, it - 1)
                    for q in range(2 * PK):
                        c = q * 128
                        last = nc.tensor.transpose(ps[0:2 * DE, 2 * b + c // 512, c % 512:c % 512 + 128],
                                                   att_hl[:, b, q, :], ident[:, :])
                    last.then_inc(att_tr, 1)

                for b in range(2):
                    transposes(b, b, True)
                with pe.Fori(1, NPK // 2) as i:
                    for b in range(2):
                        transposes(2 * i + b, b, False)

        def groups_loop(eng, step):
            for b in range(UN):
                step(b, 0, b)
            with eng.Fori(1, NIT - 1) as i:
                for b in range(UN):
                    step(i * UN + b, i, b)
            for b in range(UN):
                step((NIT - 1) * UN + b, NIT - 1, b)

        def is_past(g, k):
            return not isinstance(g, int) or g >= k

        def has(g, k):
            return not isinstance(g, int) or g + k < NG

        LAG, LAG_A = 4, 5
        GATHER_LAG = 3

        with nc.Block() as block:
            @block.sync
            def _(sp):
                with sp.Fori(0, L) as l:
                    sp.wait_ge(h_rows, (l + 1) * NT)
                    for k in range(4):
                        sp.dma_start(w1_raw[k * DE:(k + 1) * DE, :],
                                     ee_w1[ds(l, 1), :, :].rearrange("a k d -> (a k) d")).then_inc(w_in, 16)
                    for k in range(2):
                        sp.dma_start(w1_raw[4 * DE + k:4 * DE + k + 1, :], ee_b1[ds(l, 1), :]).then_inc(w_in, 16)
                    sp.dma_start(w2_raw[:, :, :], ee_w2[ds(l, 1), :, :].rearrange("a (k p) d -> p (a k) d", p=128))\
                        .then_inc(w_in, 16)
                    sp.dma_start(b2_all[:, :], ee_b2[ds(l, 1), :].to_broadcast([128, D])).then_inc(w_in, 16)

                    def attributes(g, i, b):
                        if is_past(g, UN):
                            sp.wait_ge(mm1, l * NG + g - (UN - 1))
                        sp.dma_start(at[0:4 * DE, b, :].bitcast(F32), attr_t[:, ds(g * GS, GS)]).then_inc(at_in[b], 16)

                    def slots(g, i, b):
                        if is_past(g, UN):
                            sp.wait_ge(picked, l * NG + g - (UN - 1))
                            sp.wait_ge(msg_high, l * NG + g - (UN - 1))
                        sp.dma_start(meta[:, b, :, :].bitcast(F32), rec[ds(g * GS, GS), 0:ATT]
                                     .rearrange("(p j) w -> p j w", j=2)).then_inc(meta_in[b], 16)

                    for b in range(UN):
                        attributes(b, 0, b)
                        slots(b, 0, b)
                    for k in range(2):
                        sp.dma_start(m1[:, k, :], mlp_w1[ds(l, 1), k * 128:(k + 1) * 128, :]
                                     .rearrange("a p f -> (a p) f")).then_inc(m_in, 16)
                    for k in range(4):
                        sp.dma_start(m2[:, k, :], mlp_w2[ds(l, 1), k * 128:(k + 1) * 128, :]
                                     .rearrange("a p f -> (a p) f")).then_inc(m_in, 16)
                    with sp.Fori(1, NIT) as i:
                        for b in range(UN):
                            attributes(i * UN + b, i, b)
                            slots(i * UN + b, i, b)

            @block.gpsimd
            def _(pool):
                with pool.Fori(0, L) as l:
                    pool.wait_ge(tab_out, (l + 1) * 16)
                    pool.sem_inc(pool_pace)

                    def gather(g, i, b):
                        pool.wait_ge(meta_in[b], (l * NIT + i + 1) * 16)
                        pool.wait_ge(e_out, l * NG + g + 1)
                        pool.sem_inc(pool_pace)
                        for j in range(2):
                            nc.gpsimd.indirect_dma_start(
                                e_sb[:, b % 4, j, :], None, table,
                                bass.IndirectOffsetOnAxis(ap=meta[:, b, j, SRC:SRC + 1], axis=0),
                                compute_op=ALU.add).then_inc(gathered[b % 4], 16)

                    with pool.Fori(0, NIT) as i:
                        for b in range(UN):
                            gather(i * UN + b, i, b)

            def z2_out(act, l, c):
                t0, nt = CH[c]
                n = nt * TP
                for f in range(2):
                    act.wait_ge(z2_mm, l * NCH * 2 + c * 2 + f + 1)
                    nc.scalar.activation(z2[:, f, t0 * TP:t0 * TP + n], ps[:, (c % 2) * 2 + f, 0:n], ACT.Identity,
                                         bias=vec[:, V_B2 + f:V_B2 + f + 1]).then_inc(z2_ev, 1)

            @block.scalar
            def _(act):
                with act.Fori(0, L) as l:
                    act.wait_ge(w_in, (l + 1) * 16 * 8)
                    nc.scalar.copy(w1_h[:, :], w1_raw[:, :]).then_inc(w_high, 1)
                    nc.scalar.copy(w2_h[:, :, :], w2_raw[:, :, :]).then_inc(w_high, 1)
                    act.wait_ge(tab_made, l + 1)
                    act.dma_start(table.rearrange("(t p) d -> p t d", p=TP), node_tab[0:TP, :, :])\
                        .then_inc(tab_out, 16)

                    def hidden_high(g, b):
                        act.wait_ge(mm1, l * NG + g + 1)
                        if is_past(g, 2):
                            act.wait_ge(mm2, l * NG + g - 1)
                        nc.scalar.activation(hid_h[:, b, :, :].rearrange("p a c -> p (a c)"), ps[:, b, :],
                                             ACT.Relu).then_inc(hid_high, 1)

                    def evacuate(g, i, b):
                        act.wait_ge(mm2, l * NG + g + 1)
                        if is_past(g, 4):
                            act.wait_ge(msg_low, l * NG + g - 3)
                        nc.scalar.copy(e_sb[:, b % 4, :, :].rearrange("p a c -> p (a c)"), ps[:, 2 + b % 2, :])\
                            .then_inc(e_out, 1)

                    def message_high(g, turn4, b):
                        act.wait_ge(gathered[b % 4], turn4 * 32)
                        if is_past(g, 2):
                            act.wait_ge(mm3, l * NG + g - 1)
                        nc.scalar.activation(msg_h[:, b % 2, :, :], e_sb[:, b % 4, :, :], ACT.Relu)\
                            .then_inc(msg_high, 1)

                    def turns4(g):
                        return l * (NG // 4) + g // 4 + 1

                    hidden_high(0, 0)

                    def step(g, i, b):
                        if has(g, 1):
                            hidden_high(g + 1, (b + 1) % 2)
                        if is_past(g, GATHER_LAG):
                            bb = (b - GATHER_LAG) % UN
                            back = 0 if b >= GATHER_LAG else 1
                            t4 = (turns4(g - GATHER_LAG) if isinstance(g, int)
                                  else l * (NG // 4) + (i - back) * 2 + bb // 4 + 1)
                            message_high(g - GATHER_LAG, t4, bb)
                        evacuate(g, i, b)

                    groups_loop(act, step)
                    for g in range(NG - GATHER_LAG, NG):
                        message_high(g, turns4(g), g % UN)

                    for c, (t0, nt) in enumerate(CH):
                        n = nt * TP
                        act.wait_ge(z_tr, l * NCH + c + 1)
                        if c >= 2:
                            act.wait_ge(u_mm, l * NCH * 4 + (c - 1) * 4)
                        nc.scalar.copy(zT[:, c % 2, 0, 0:n], ps[:, 6, 0:n]).then_inc(z_ev0, 1)
                        for f in range(4):
                            act.wait_ge(u_mm, l * NCH * 4 + c * 4 + f + 1)
                            nc.scalar.activation(u[:, f, t0 * TP:t0 * TP + n], ps[:, f, 0:n], ACT.Identity,
                                                 bias=vec[:, V_B1 + f:V_B1 + f + 1]).then_inc(u_ev, 1)
                    sqrt_for(act, 128, 4, l * 2 + 2)
                    act.wait_ge(bn1_ready, l + 1)
                    for c, (t0, nt) in enumerate(CH):
                        n = nt * TP
                        if c >= 2:
                            act.wait_ge(z2_mm, l * NCH * 2 + (c - 1) * 2)
                        for f in range(4):
                            nc.scalar.activation(v[:, c % 2, f, 0:n], u[:, f, t0 * TP:t0 * TP + n], ACT.Relu,
                                                 bias=r_o[:, f:f + 1], scale=r_s[:, f:f + 1]).then_inc(v_made, 1)
                        if c >= 1:
                            z2_out(act, l, c - 1)
                    z2_out(act, l, NCH - 1)
                    sqrt_for(act, 128, 2, l * 2 + 3)
                    act.wait_ge(bn2_ready, l + 1)
                    for c, (t0, nt) in enumerate(CH):
                        for f in range(2):
                            a = z2[:, f, t0 * TP:(t0 + nt) * TP]
                            nc.scalar.activation(a, a, ACT.Identity, bias=r_o[:, f:f + 1],
                                                 scale=r_s[:, f:f + 1]).then_inc(zn_made, 1)

            def bn_affine(link, dve, n, v_g, v_b, asked, ready):
                y = rsqrt(link, dve, mv[:, 0:n, 1], 128, n, asked)
                link(nc.vector.tensor_tensor(r_s[:, 0:n], y, vec[:, v_g:v_g + n], ALU.mult))
                link(nc.vector.tensor_tensor(r_t[:, 0:n], mv[:, 0:n, 0], r_s[:, 0:n], ALU.mult))
                nc.vector.tensor_tensor(r_o[:, 0:n], vec[:, v_b:v_b + n], r_t[:, 0:n], ALU.subtract)\
                    .then_inc(ready, 1)

            @block.vector
            def _(dve):
                vc = nc.vector
                with dve.Fori(0, L) as l:
                    CL = 1 + 14 + 4 + 4
                    link = Link(dve, d_lay, l * CL)
                    link(vc.tensor_copy(vec[:, :], vec_all[:, ds(l, 1), :].rearrange("p a v -> p (a v)")))
                    dve.wait_ge(w_in, (l + 1) * 16 * 8)
                    vc.tensor_tensor(node_tab[0:TP, :, :], h[0:TP, :, :],
                                     b2_all[0:TP, :].unsqueeze(1).to_broadcast([TP, NT, D]), ALU.add)\
                        .then_inc(tab_made, 1)
                    link(vc.tensor_scalar(agg[0:TP, :, :], h[0:TP, :, :], vec[0:TP, V_EPS:V_EPS + 1], None, ALU.mult))
                    dve.wait_ge(w_high, (l + 1) * 2)
                    link(vc.tensor_tensor(w1_l[:, :], w1_raw[:, :], w1_h[:, :].bitcast(F32), ALU.subtract))
                    link(vc.tensor_scalar(w1_raw[:, :], w1_h[:, :].bitcast(F32), w1_high[0:KA, :], None, ALU.mult))
                    link(vc.scalar_tensor_tensor(out=w1_s[:, :], in0=w1_l[:, :].bitcast(F32), scalar=w1_low[0:KA, :],
                                                 in1=w1_raw[:, :], op0=ALU.mult, op1=ALU.add))
                    vc.tensor_tensor(w2_l[:, :, :], w2_raw[:, :, :], w2_h[:, :, :].bitcast(F32),
                                     ALU.subtract).then_inc(w_ready, 1)

                    def hidden_low(g, b):
                        dve.wait_ge(hid_high, l * NG + g + 1)
                        vc.scalar_tensor_tensor(
                            out=hid_l[:, b, :, :].rearrange("p a c -> p (a c)"), in0=ps[:, b, :], scalar=0.0,
                            in1=hid_h[:, b, :, :].rearrange("p a c -> p (a c)").bitcast(F32), op0=ALU.max,
                            op1=ALU.subtract).then_inc(hid_low, 1)

                    def message_low(g, turn, b):
                        dve.wait_ge(meta_in[b], turn * 16)
                        if is_past(g, 2):
                            dve.wait_ge(mm3, l * NG + g - 1)
                        for j in range(2):
                            p = vc.tensor_scalar(pick[:, b % 2, j, 0:TP], iota_n[:, :],
                                                 meta_f[:, b, j, DLOC:DLOC + 1], None, ALU.is_equal)
                        p.then_inc(picked, 1)
                        dve.wait_ge(msg_high, l * NG + g + 1)
                        vc.scalar_tensor_tensor(
                            out=msg_l[:, b % 2, :, :].rearrange("p a c -> p (a c)"),
                            in0=e_sb[:, b % 4, :, :].rearrange("p a c -> p (a c)"), scalar=0.0,
                            in1=msg_h[:, b % 2, :, :].rearrange("p a c -> p (a c)").bitcast(F32), op0=ALU.max,
                            op1=ALU.subtract).then_inc(msg_low, 1)

                    def add_sums(g, b):
                        t = dve.value_load(group_tile[0:1, ds(g, 1)], min_val=0, max_val=NT - 1)
                        dve.wait_ge(mm3, l * NG + g + 1)
                        if is_past(g, 1):
                            dve.wait_ge(added, l * NG + g)
                        dst_tile = agg[0:TP, ds(t, 1), :].rearrange("p a d -> p (a d)")
                        vc.tensor_tensor(dst_tile, dst_tile, ps[0:TP, 4 + b % 2, 0:D], ALU.add).then_inc(added, 1)

                    hidden_low(0, 0)

                    def step(g, i, b):
                        if has(g, 1):
                            hidden_low(g + 1, (b + 1) % 2)
                        if is_past(g, GATHER_LAG):
                            bb = (b - GATHER_LAG) % UN
                            back = 0 if b >= GATHER_LAG else 1
                            message_low(g - GATHER_LAG, l * NIT + i - back + 1, bb)
                        if is_past(g, LAG_A):
                            add_sums(g - LAG_A, (b - LAG_A) % UN)

                    groups_loop(dve, step)
                    for k in range(NG - GATHER_LAG, NG + LAG_A - GATHER_LAG):
                        if k < NG:
                            message_low(k, l * NIT + NIT, k % UN)
                        k -= LAG_A - GATHER_LAG
                        add_sums(k, k % UN)

                    for c, (t0, nt) in enumerate(CH):
                        n = nt * TP
                        dve.wait_ge(z_tr, l * NCH + c + 1)
                        if c >= 2:
                            dve.wait_ge(u_mm, l * NCH * 4 + (c - 1) * 4)
                        vc.tensor_copy(zT[:, c % 2, 1, 0:n], ps[:, 7, 0:n]).then_inc(z_ev1, 1)
                        for f in range(4):
                            dve.wait_ge(u_ev, l * NCH * 4 + c * 4 + f + 1)
                            last = vc.bn_stats(st1[:, f, c, :], u[:, f, t0 * TP:t0 * TP + n])
                    link(last)
                    dve.sem_inc(dve_pace)
                    for f in range(4):
                        last = vc.bn_aggr(mv[:, f, :], st1[:, f, :, :].rearrange("p c s -> p (c s)"))
                    link(last)
                    bn_affine(link, dve, 4, V_G1, V_BB1, l * 2 + 2, bn1_ready)
                    for c, (t0, nt) in enumerate(CH):
                        for f in range(2):
                            dve.wait_ge(z2_ev, l * NCH * 2 + c * 2 + f + 1)
                            last = vc.bn_stats(st2[:, f, c, :], z2[:, f, t0 * TP:(t0 + nt) * TP])
                    link(last)
                    dve.sem_inc(dve_pace)
                    for f in range(2):
                        last = vc.bn_aggr(mv[:, f, :], st2[:, f, :, :].rearrange("p c s -> p (c s)"))
                    link(last)
                    bn_affine(link, dve, 2, V_G2, V_BB2, l * 2 + 3, bn2_ready)
                    for t in range(NT):
                        dve.wait_ge(zn_tr, l * NT + t + 1)
                        last = vc.scalar_tensor_tensor(out=h[0:TP, t, :], in0=ps[0:TP, t % 4, 0:D],
                                                       scalar=vec[0:TP, V_FLOOR:V_FLOOR + 1], in1=h[0:TP, t, :],
                                                       op0=ALU.max, op1=ALU.add)
                        last.then_inc(h_rows, 1)
                    dve.wait_ge(h_rows, (l + 2) * NT)
                    assert link.n == CL, link.n

            @block.tensor
            def _(pe):
                with pe.Fori(0, L) as l:
                    pe.wait_ge(w_ready, l + 1)

                    def hidden(g, turn, b):
                        pe.wait_ge(at_in[b], turn * 16)
                        if is_past(g, 2):
                            pe.wait_ge(hid_low, l * NG + g - 1)
                        for half in range(2):
                            last = nc.tensor.matmul(ps[:, b % 2, half * GS:(half + 1) * GS],
                                                    w1_s[:, half * 128:(half + 1) * 128], at[:, b, :],
                                                    start=True, stop=True)
                        last.then_inc(mm1, 1)

                    def edge_out(g, b):
                        pe.wait_ge(hid_low, l * NG + g + 1)
                        if is_past(g, 2):
                            pe.wait_ge(e_out, l * NG + g - 1)
                        s = b % 2
                        for j in range(2):
                            terms = [(a, w, k) for k in range(2)
                                     for a, w in ((hid_h, w2_h), (hid_h, w2_l), (hid_l, w2_h))]
                            for n, (a, w, k) in enumerate(terms):
                                last = nc.tensor.matmul(ps[:, 2 + s, j * D:(j + 1) * D],
                                                        a[:, s, k, j * 128:(j + 1) * 128], w[:, k, :],
                                                        start=(n == 0), stop=(n == len(terms) - 1))
                        last.then_inc(mm2, 1)

                    def sums(g, b):
                        pe.wait_ge(picked, l * NG + g + 1)
                        pe.wait_ge(msg_low, l * NG + g + 1)
                        if is_past(g, 2):
                            pe.wait_ge(added, l * NG + g - 1)
                        s = b % 2
                        for n, (j, m) in enumerate(((0, msg_h), (0, msg_l), (1, msg_h), (1, msg_l))):
                            last = nc.tensor.matmul(ps[0:TP, 4 + s, 0:D], pick[:, s, j, 0:TP], m[:, s, j, :],
                                                    start=(n == 0), stop=(n == 3))
                        last.then_inc(mm3, 1)

                    hidden(0, l * NIT + 1, 0)

                    def step(g, i, b):
                        if has(g, 1):
                            hidden(g + 1, l * NIT + i + 1 + (b + 1) // UN, (b + 1) % UN)
                        edge_out(g, b)
                        if is_past(g, LAG):
                            sums(g - LAG, b)

                    groups_loop(pe, step)
                    for k in range(NG - LAG, NG):
                        sums(k, k)

                    pe.wait_ge(added, (l + 1) * NG)
                    pe.wait_ge(m_in, (l + 1) * 16 * 6)
                    for c, (t0, nt) in enumerate(CH):
                        n = nt * TP
                        if c >= 1:
                            pe.wait_ge(z_ev0, l * NCH + c)
                            pe.wait_ge(z_ev1, l * NCH + c)
                        for half in range(2):
                            for t in range(nt):
                                last = nc.tensor.transpose(ps[:, 6 + half, t * TP:(t + 1) * TP],
                                                           agg[0:TP, t0 + t, half * 128:(half + 1) * 128],
                                                           ident[0:TP, 0:TP])
                        last.then_inc(z_tr, 1)
                        pe.wait_ge(z_ev0, l * NCH + c + 1)
                        pe.wait_ge(z_ev1, l * NCH + c + 1)
                        for f in range(4):
                            if c >= 1:
                                pe.wait_ge(u_ev, l * NCH * 4 + (c - 1) * 4 + f + 1)
                            for k in range(2):
                                last = nc.tensor.matmul(ps[:, f, 0:n], m1[:, k, f * 128:(f + 1) * 128],
                                                        zT[:, c % 2, k, 0:n], start=(k == 0), stop=(k == 1))
                            last.then_inc(u_mm, 1)
                    for c, (t0, nt) in enumerate(CH):
                        n = nt * TP
                        pe.wait_ge(v_made, l * NCH * 4 + c * 4 + 4)
                        if c >= 2:
                            pe.wait_ge(z2_ev, l * NCH * 2 + (c - 1) * 2)
                        for f in range(2):
                            for k in range(4):
                                last = nc.tensor.matmul(ps[:, (c % 2) * 2 + f, 0:n], m2[:, k, f * 128:(f + 1) * 128],
                                                        v[:, c % 2, k, 0:n], start=(k == 0), stop=(k == 3))
                            last.then_inc(z2_mm, 1)
                    for c, (t0, nt) in enumerate(CH):
                        pe.wait_ge(zn_made, l * NCH * 2 + c * 2 + 2)
                        for t in range(t0, t0 + nt):
                            if t >= 4:
                                pe.wait_ge(h_rows, (l + 1) * NT + t - 3)
                            for f in range(2):
                                last = nc.tensor.transpose(ps[0:TP, t % 4, f * 128:(f + 1) * 128],
                                                           z2[:, f, t * TP:(t + 1) * TP], ident[:, :])
                            last.then_inc(zn_tr, 1)

        with nc.Block() as block:
            @block.sync
            def _(sp):
                sp.dma_start(node_tab[0:TP, :, :], x.rearrange("(t p) d -> p t d", p=TP)).then_inc(xr_in, 16)
                for c, (t0, nt) in enumerate(CH):
                    sp.wait_ge(out_made, t0 + nt)
                    sp.dma_start(out.rearrange("(t p) d -> p t d", p=TP)[:, t0:t0 + nt, :],
                                 agg[0:TP, t0:t0 + nt, :]).then_inc(out_done, 16)
                sp.wait_ge(out_done, 16 * NCH)

            def h1_of(c):
                return zT[:, c % 2, :, :]

            def e1_of(c):
                return v[:, c % 2, :, :]

            h2_all = u_flat[:, 6400:7400].rearrange("p (s n) -> p s n", s=2)
            e2_all = u_flat[:, 7400:9400].rearrange("p (s q n) -> p s q n", s=2, q=2)

            def e2_of(c):
                return e2_all[:, c % 2, :, :]

            def units(c):
                t0, nt = CH[c]
                n = nt * TP
                y = [yT[:, k, t0 * TP:t0 * TP + n] for k in range(2)]
                got = [([(sW1_s[:, k, f * 128:(f + 1) * 128], y[k]) for k in range(2)],
                        sb1_s[:, f:f + 1], h1_of(c)[:, f, 0:n]) for f in range(2)]
                got += [([(eW1_s[:, e, k, :], y[k]) for k in range(2)],
                         eb1_s[:, e:e + 1], e1_of(c)[:, e, 0:n]) for e in range(NE)]
                got += [([(sW2_s[:, k, :], h1_of(c)[:, k, 0:n]) for k in range(2)],
                         sb2_s[:, 0:1], h2_all[:, c % 2, 0:n])]
                got += [([(eW2_s[:, 2 * q + r, :], e1_of(c)[:, 2 * q + r, 0:n]) for r in range(2)],
                         eb2_s[:, q:q + 1], e2_of(c)[:, q, 0:n]) for q in range(2)]
                return got

            @block.vector
            def _(dve):
                vc = nc.vector
                link = Link(dve, d_moe)
                dve.wait_ge(xr_in, 16)
                link(vc.tensor_tensor(h[0:TP, :, :], h[0:TP, :, :], node_tab[0:TP, :, :], ALU.add))
                layer_norm(link, dve, h, agg, 2 * L + 2, y_made)
                for c, (t0, nt) in enumerate(CH):
                    n = nt * TP
                    dve.wait_ge(y_tr, c + 1)
                    vc.tensor_copy(yT[:, 1, t0 * TP:t0 * TP + n], ps[:, 2 * (c % 2) + 1, 0:n]).then_inc(y_ev1, 1)
                    dve.wait_ge(lg_mm, c + 1)
                    vc.tensor_tensor(lg[0:TP, t0:t0 + nt, :],
                                     ps[0:TP, 4 + c % 2, 0:nt * NE].rearrange("p (t e) -> p t e", e=NE),
                                     gb_s[0:TP, :].unsqueeze(1).to_broadcast([TP, nt, NE]), ALU.add)\
                        .then_inc(lg_ev, 1)
                dve.wait_ge(lg_ev, NCH)
                mx, sm = r_a[0:TP, 0:NT], r_s[0:TP, 0:NT]

                def over(a):
                    return a.unsqueeze(2).to_broadcast([TP, NT, NE])

                g_, p_ = lg[0:TP, :, :], pr[0:TP, :, :]
                link(vc.tensor_reduce(mx, g_, AX, ALU.max))
                vc.tensor_tensor(g_, g_, over(mx), ALU.subtract).then_inc(ex_ask, 1)
                dve.wait_ge(ex_done, 1)
                link(vc.tensor_reduce(sm, p_, AX, ALU.add))
                link(vc.reciprocal(sm, sm))
                link(vc.tensor_tensor(p_, p_, over(sm), ALU.mult))
                link(vc.memset(rk[:, :, :], 0.0))
                for j in range(NE):
                    for k in range(j + 1, NE):
                        link(vc.tensor_tensor(cmp[0:TP, :], pr[0:TP, :, j], pr[0:TP, :, k], ALU.is_ge))
                        link(vc.tensor_tensor(rk[0:TP, k, :], rk[0:TP, k, :], cmp[0:TP, :], ALU.add))
                        link(vc.tensor_tensor(cmp[0:TP, :], pr[0:TP, :, k], pr[0:TP, :, j], ALU.is_gt))
                        link(vc.tensor_tensor(rk[0:TP, j, :], rk[0:TP, j, :], cmp[0:TP, :], ALU.add))
                link(vc.tensor_reduce(mx, p_, AX, ALU.max))
                vc.tensor_tensor(g_, p_, over(mx), ALU.subtract).then_inc(ex_ask, 1)
                dve.wait_ge(ex_done, 2)
                link(vc.scalar_tensor_tensor(out=p_, in0=rk[0:TP, :, :].rearrange("p e t -> p t e"), scalar=2.0,
                                             in1=p_, op0=ALU.is_lt, op1=ALU.mult))
                link(vc.tensor_reduce(sm, p_, AX, ALU.add))
                link(vc.reciprocal(sm, sm))
                link(vc.memset(w5[0:TP, :, 0:1], 1.0))
                vc.tensor_tensor(w5[0:TP, :, 1:1 + NE], p_, over(sm), ALU.mult).then_inc(w_made, 1)
                nd = 0
                for c, (t0, nt) in enumerate(CH):
                    n = nt * TP
                    nd += 1
                    dve.wait_ge(d_mm, nd)
                    vc.tensor_copy(wT[:, c % 2, 0:n], ps[0:1 + NE, 4 + (nd - 1) % 4, 0:n]).then_inc(d_ev, 1)
                    for q in range(2):
                        nd += 1
                        dve.wait_ge(d_mm, nd)
                        dve.wait_ge(a_ev, c * 9 + 8 + q)
                        e2 = e2_of(c)[:, q, 0:n]
                        vc.tensor_tensor(e2, e2, ps[:, 4 + (nd - 1) % 4, 0:n], ALU.mult).then_inc(d_ev, 1)
                    for t in range(t0, t0 + nt):
                        nd += 1
                        dve.wait_ge(d_mm, nd)
                        vc.tensor_tensor(agg[0:TP, t, :], ps[0:TP, 4 + (nd - 1) % 4, 0:D], h[0:TP, t, :],
                                         ALU.add).then_inc(out_made, 1)

            @block.scalar
            def _(act):
                sqrt_for(act, TP, NT, 2 * L + 2)
                for c, (t0, nt) in enumerate(CH):
                    n = nt * TP
                    act.wait_ge(y_tr, c + 1)
                    nc.scalar.copy(yT[:, 0, t0 * TP:t0 * TP + n], ps[:, 2 * (c % 2), 0:n]).then_inc(y_ev0, 1)
                for k in range(2):
                    act.wait_ge(ex_ask, k + 1)
                    nc.scalar.activation(pr[0:TP, :, :], lg[0:TP, :, :], ACT.Exp).then_inc(ex_done, 1)
                na = 0
                for c, (t0, nt) in enumerate(CH):
                    if c >= 2:
                        act.wait_ge(out_made, CH[c - 1][0])
                    for _, bias, where in units(c):
                        na += 1
                        act.wait_ge(a_mm, na)
                        nc.scalar.activation(where, ps[:, (na - 1) % 4, 0:nt * TP], ACT.Relu, bias=bias)\
                            .then_inc(a_ev, 1)

            @block.tensor
            def _(pe):
                pe.wait_ge(y_made, NT)
                for c, (t0, nt) in enumerate(CH):
                    n = nt * TP
                    if c >= 2:
                        pe.wait_ge(y_ev0, c - 1)
                        pe.wait_ge(y_ev1, c - 1)
                    for half in range(2):
                        for t in range(nt):
                            last = nc.tensor.transpose(ps[:, 2 * (c % 2) + half, t * TP:(t + 1) * TP],
                                                       agg[0:TP, t0 + t, half * 128:(half + 1) * 128],
                                                       ident[0:TP, 0:TP])
                    last.then_inc(y_tr, 1)
                    pe.wait_ge(y_ev0, c + 1)
                    pe.wait_ge(y_ev1, c + 1)
                    if c >= 2:
                        pe.wait_ge(lg_ev, c - 1)
                    for t in range(nt):
                        for k in range(2):
                            last = nc.tensor.matmul(ps[0:TP, 4 + c % 2, t * NE:(t + 1) * NE],
                                                    yT[:, k, (t0 + t) * TP:(t0 + t + 1) * TP], gW_s[:, k, :],
                                                    start=(k == 0), stop=(k == 1))
                    last.then_inc(lg_mm, 1)
                pe.wait_ge(w_made, 1)
                na, nd = 0, 0

                def bank_d():
                    nonlocal nd
                    if nd >= 4:
                        s, value = readers[nd - 4]
                        pe.wait_ge(s, value)
                    nd += 1
                    return 4 + (nd - 1) % 4

                readers = []
                for c, (t0, nt) in enumerate(CH):
                    readers += [(d_ev, 3 * c + k + 1) for k in range(3)]
                    readers += [(out_made, t + 1) for t in range(t0, t0 + nt)]
                for c, (t0, nt) in enumerate(CH):
                    n = nt * TP
                    for k, (terms, _, _) in enumerate(units(c)):
                        if k == 6:
                            pe.wait_ge(a_ev, 9 * c + 2)
                        if k == 7:
                            pe.wait_ge(a_ev, 9 * c + 6)
                        if na >= 4:
                            pe.wait_ge(a_ev, na - 3)
                        for m, (w, r) in enumerate(terms):
                            last = nc.tensor.matmul(ps[:, na % 4, 0:n], w, r, start=(m == 0),
                                                    stop=(m == len(terms) - 1))
                        last.then_inc(a_mm, 1)
                        na += 1
                        if k == 1:
                            b = bank_d()
                            for t in range(nt):
                                last = nc.tensor.transpose(ps[0:1 + NE, b, t * TP:(t + 1) * TP],
                                                           w5[0:TP, t0 + t, :], ident[0:TP, 0:TP])
                            last.then_inc(d_mm, 1)
                    pe.wait_ge(d_ev, 3 * c + 1)
                    for q in range(2):
                        b = bank_d()
                        nc.tensor.matmul(ps[:, b, 0:n], sel[:, q, :], wT[:, c % 2, 0:n], start=True, stop=True)\
                            .then_inc(d_mm, 1)
                    pe.wait_ge(a_ev, 9 * c + 7)
                    pe.wait_ge(d_ev, 3 * c + 3)
                    for t in range(nt):
                        cols = slice(t * TP, (t + 1) * TP)
                        b = bank_d()
                        terms = [(h2_all[:, c % 2, cols], sW3_s[:, :])]
                        terms += [(e2_of(c)[:, q, cols], eW3_s[:, q, :]) for q in range(2)]
                        terms += [(wT[:, c % 2, cols], b_out[:, :])]
                        for m, (w, r) in enumerate(terms):
                            last = nc.tensor.matmul(ps[0:TP, b, 0:D], w, r, start=(m == 0), stop=(m == 3))
                        last.then_inc(d_mm, 1)


_INS = ['x', 'src', 'dst', 'edge_attr_16', 'L0_gnn_ee_w1', 'L0_gnn_ee_b1', 'L0_gnn_ee_w2', 'L0_gnn_ee_b2',
        'L0_gnn_eps', 'L0_gnn_mlp_w1', 'L0_gnn_mlp_b1', 'L0_gnn_bn1_g', 'L0_gnn_bn1_b', 'L0_gnn_mlp_w2',
        'L0_gnn_mlp_b2', 'L0_gnn_bn_g', 'L0_gnn_bn_b', 'L0_ffn_sW1', 'L0_ffn_sb1', 'L0_ffn_sW2', 'L0_ffn_sb2',
        'L0_ffn_sW3', 'L0_ffn_sb3', 'L0_ffn_eW1', 'L0_ffn_eb1', 'L0_ffn_eW2', 'L0_ffn_eb2', 'L0_ffn_eW3',
        'L0_ffn_eb3', 'L0_ffn_gW', 'L0_ffn_gb']


def kernel(**inputs):
    import numpy as _np
    import concourse.bacc as _bacc
    from concourse import mybir as _mybir
    from concourse.bass_utils import run_bass_kernel_spmd as _run

    nc = _bacc.Bacc("TRN2", target_bir_lowering=False, num_devices=1)
    arrays, args = {}, []
    for name in _INS:
        a = _np.ascontiguousarray(inputs[name])
        arrays[f"in_{name}_dram"] = a
        args.append(nc.dram_tensor(f"in_{name}_dram", a.shape, _mybir.dt.from_np(a.dtype), kind="ExternalInput").ap())
    args.append(nc.dram_tensor("out_dram", (3125, 256), _mybir.dt.float32, kind="ExternalOutput").ap())
    gnn_moe_kernel(nc, *args)
    r = _run(nc, [arrays], core_ids=[0])
    return r.results[0]["out_dram"]
```

```python
import concourse.bass as bass
from concourse import mybir
from contextlib import ExitStack

F32 = mybir.dt.float32
F32R = mybir.dt.float32r
I32 = mybir.dt.int32
ALU = mybir.AluOpType
ACT = mybir.ActivationFunctionType
AX = mybir.AxisListType.X
ds = bass.ds

N, D, DE, L, E = 3125, 256, 16, 5, 53125
D2 = 2 * D
TP = 125
NT = N // TP
EC = E // TP
GS = 256
NG = (E + NT * (GS - 1)) // GS
UN = 8
NIT = NG // UN
assert NG % UN == 0 and N == NT * TP and E == EC * TP
RW = 2 + DE
SRC, DST, ATT = 0, 1, 2
EPS = 1e-5
BIG = 3.0e38
CH = [(t, min(4, NT - t)) for t in range(0, NT, 4)]
NCH = len(CH)
SB = 17
NSB = EC // SB
assert EC == SB * NSB and NSB % 2 == 1
TAIL = GS
Q = 4
BLK = 128 * Q
NBLK = -(-(E + TAIL) // (2 * BLK)) * 2
EP = NBLK * BLK
ATT_B = [(b, min(8, NBLK - b)) for b in range(0, NBLK, 8)]
FULL = E // BLK
FULL_P, REST = (E - FULL * BLK) // Q, E % Q
assert REST > 0
V_B1, V_G1, V_BB1, V_B2, V_G2, V_BB2, V_EPS, V_FLOOR, NV = 0, 4, 8, 12, 14, 16, 18, 19, 20
NE, EH1, EH2, SH1, SH2 = 4, 128, 64, 256, 128


class Link:

    def __init__(self, eng, sem, base=0):
        self.eng, self.sem, self.base, self.n = eng, sem, base, 0

    def __call__(self, ins):
        self.n += 1
        ins.then_inc(self.sem, 1)
        self.eng.wait_ge(self.sem, self.base + self.n)


def gnn_moe_kernel(nc, x, src, dst, edge_attr, ee_w1, ee_b1, ee_w2, ee_b2, eps, mlp_w1, mlp_b1,
                   bn1_g, bn1_b, mlp_w2, mlp_b2, bn_g, bn_b, sW1, sb1, sW2, sb2, sW3, sb3,
                   eW1, eb1, eW2, eb2, eW3, eb3, gW, gb, out):
    ctx = ExitStack()
    with ctx:
        def sb(name, shape, dt=F32):
            return ctx.enter_context(nc.sbuf_tensor(name, shape, dt))

        def sem(name):
            return ctx.enter_context(nc.semaphore(name))

        rec = nc.dram_tensor("edge_records", [E, RW], F32, kind="Internal").ap()
        ends_d = nc.dram_tensor("edge_ends", [E + TAIL, 2], F32, kind="Internal").ap()
        attr_t = nc.dram_tensor("attributes_t", [4 * DE, EP], F32, kind="Internal").ap()
        table = nc.dram_tensor("node_table", [N, D], F32, kind="Internal").ap()

        h = sb("h", [128, NT, D])
        agg = sb("agg", [128, NT, D])
        u = sb("u", [128, 4, N])
        u_flat = u[:, :, :].rearrange("p f n -> p (f n)")
        agg_flat = agg[:, :, :].rearrange("p t d -> p (t d)")
        z2 = agg_flat[:, 0:2 * N].rearrange("p (f n) -> p f n", f=2)
        node_tab = u_flat[:, 0:NT * D].rearrange("p (t d) -> p t d", d=D)
        yT = u_flat[:, 0:2 * N].rearrange("p (f n) -> p f n", f=2)
        ATT_W = NBLK * Q * DE
        att_all = u_flat[:, 0:ATT_W].rearrange("p (b q w) -> p b q w", q=Q, w=DE)
        scratch = [u_flat[0:TP, ATT_W + k * EC:ATT_W + (k + 1) * EC] for k in range(10)]
        dst_f, bucket, mask, prefix, rank, part, ones_c = scratch[:7]
        src_i, dst_i, place_i = (a.bitcast(I32) for a in scratch[7:])

        ident = sb("ident", [128, 128])
        iota_n = sb("iota_n", [128, TP])
        lower = sb("lower", [128, 128])
        ones = sb("ones", [128, 128])
        part_id = sb("part_id", [128, 1])
        w1_high = sb("w1_high", [128, 1])
        w1_low = sb("w1_low", [128, 1])
        vec_all = sb("vec_all", [128, L, NV])
        vec = sb("vec", [128, NV])
        upto = sb("upto", [128, NT])
        tile_part = sb("tile_part", [128, NT])
        dst_next = sb("dst_next", [128, 1], I32)
        dst_next_f = sb("dst_next_f", [128, 1])
        breaks = sb("breaks", [128, 2])
        unsorted = sb("unsorted", [1, 1], I32)
        cnt = sb("cnt", [NT, 1])
        cnt_i = sb("cnt_i", [NT, 1], I32)
        groups = sb("groups", [NT, 1])
        groups_end = sb("groups_end", [NT, 1])
        slack = sb("slack", [NT, 1])
        slack_b = sb("slack_b", [NT, 128])
        ended = sb("ended", [NT, NG])
        offset = sb("offset", [128, NT])
        g_iota = sb("g_iota", [128, NG])
        first_f = sb("first_f", [1, NG])
        first_edge = sb("first_edge", [1, NG], I32)
        tile_base = sb("tile_base", [128, NG])
        group_tile = sb("group_tile", [1, NG], I32)

        def carve(*shape):
            start, size = carve.at, 1
            for k in shape:
                size *= k
            carve.at = start + size
            assert carve.at <= NT * D
            letters = "abcde"[:len(shape)]
            return agg_flat[:, start:carve.at].rearrange(
                f"p ({' '.join(letters)}) -> p {' '.join(letters)}", **dict(zip(letters, shape)))

        carve.at = 0
        stage = carve(2, SB, RW)
        stage_ix = carve(2, SB).bitcast(I32)
        ends = carve(EC, 2)
        att_hl = carve(2, 4 * Q, 8 * DE)

        KA = 4 * DE + 2
        w1_raw = sb("w1_raw", [KA, D])
        w1_h = sb("w1_h", [KA, D], F32R)
        w1_l = sb("w1_l", [KA, D], F32R)
        w1_s = sb("w1_s", [KA, D], F32R)
        w2_raw = sb("w2_raw", [128, 2, D])
        w2_h = sb("w2_h", [128, 2, D], F32R)
        w2_l = sb("w2_l", [128, 2, D], F32R)
        b2_all = sb("b2_all", [128, D])
        m1 = sb("m1", [128, 2, D2])
        m2 = sb("m2", [128, 4, D])

        at = sb("at", [KA, UN, GS], F32R)
        meta = sb("meta", [128, UN, 2, 2], I32)
        meta_f = meta[:, :, :, :].bitcast(F32)
        hid_h = sb("hid_h", [128, 2, 2, GS], F32R)
        hid_l = sb("hid_l", [128, 2, 2, GS], F32R)
        e_sb = sb("e_sb", [128, 4, 2, D])
        msg_h = sb("msg_h", [128, 2, 2, D], F32R)
        msg_l = sb("msg_l", [128, 2, 2, D], F32R)
        pick = sb("pick", [128, 2, 2, TP + 1], F32R)

        zT = sb("zT", [128, 2, 2, 500])
        v = sb("v", [128, 2, 4, 500])
        st1 = sb("st1", [128, 4, NCH, 6])
        st2 = sb("st2", [128, 2, NCH, 6])
        mv = sb("mv", [128, NT, 2])
        st_ln = sb("st_ln", [128, NT, 6])
        r_a, r_b, r_y, r_t, r_s, r_o = (sb(f"r{k}", [128, NT]) for k in range(6))

        sW1_s = sb("sW1_s", [128, 2, SH1])
        sW2_s = sb("sW2_s", [128, 2, SH2])
        sW3_s = sb("sW3_s", [128, D])
        eW1_s = sb("eW1_s", [128, NE, 2, EH1])
        eW2_s = sb("eW2_s", [128, NE, 2 * EH2])
        eW3_s = sb("eW3_s", [128, 2, D])
        gW_s = sb("gW_s", [128, 2, NE])
        gb_s = sb("gb_s", [128, NE])
        sb1_s = sb("sb1_s", [128, 2])
        sb2_s = sb("sb2_s", [128, 1])
        eb1_s = sb("eb1_s", [128, NE])
        eb2_s = sb("eb2_s", [128, 2])
        b_out = sb("b_out", [1 + NE, D])
        lg = sb("lg", [128, NT, NE])
        pr = sb("pr", [128, NT, NE])
        rk = sb("rk", [128, NE, NT])
        cmp = sb("cmp", [128, NT])
        w5 = sb("w5", [128, NT, 1 + NE])
        sel = sb("sel", [1 + NE, 2, 128])
        wT = sb("wT", [1 + NE, 2, 500])

        att_t = [e_sb[:, :, :, :].rearrange("p a b c -> p (a b c)"),
                 v[:, :, :, :].rearrange("p a b c -> p (a b c)")]
        pad = v[0:1, :, :, :].rearrange("p a b c -> p (a b c)")[:, 2048:2048 + 2 * TAIL]            .rearrange("p (n w) -> p n w", w=2)

        ps = ctx.enter_context(nc.psum_tensor("ps", [128, 8, 512], F32))

        edges_in, x_in, vec_in, moe_in = sem("edges_in"), sem("x_in"), sem("vec_in"), sem("moe_in")
        consts, pool_own = sem("consts"), sem("pool_own")
        zeros_made, parts_made, parts_summed = sem("zeros_made"), sem("parts_made"), sem("parts_summed")
        flag_made, groups_made, groups_summed = sem("flag_made"), sem("groups_made"), sem("groups_summed")
        ended_made, ended_summed = sem("ended_made"), sem("ended_summed")
        ends_made, ends_out, places_made = sem("ends_made"), sem("ends_out"), sem("places_made")
        pool_pace, dve_pace, sp_pace = sem("pool_pace"), sem("dve_pace"), sem("sp_pace")
        staged, d_rank = sem("staged"), sem("d_rank")
        staged_att = [sem(f"staged_att{b}") for b in range(2)]
        scattered = [sem(f"scattered{b}") for b in range(2)]
        d_pre, d_lay, d_moe = sem("d_pre"), sem("d_lay"), sem("d_moe")
        att_loaded = [sem(f"att_loaded{k}") for k in range(len(ATT_B))]
        att_high, att_low, att_tr, att_ev = sem("att_high"), sem("att_low"), sem("att_tr"), sem("att_ev")
        att_out = [sem(f"att_out{b}") for b in range(2)]
        sqrt_ask, sqrt_done = sem("sqrt_ask"), sem("sqrt_done")
        h_rows, tab_made, tab_out = sem("h_rows"), sem("tab_made"), sem("tab_out")
        w_in, w_high, w_ready = sem("w_in"), sem("w_high"), sem("w_ready")
        m_in = sem("m_in")
        at_in = [sem(f"at_in{b}") for b in range(UN)]
        meta_in = [sem(f"meta_in{b}") for b in range(UN)]
        gathered = [sem(f"gathered{b}") for b in range(4)]
        mm1, mm2, mm3 = sem("mm1"), sem("mm2"), sem("mm3")
        hid_high, hid_low, e_out = sem("hid_high"), sem("hid_low"), sem("e_out")
        msg_high, msg_low, picked, added = sem("msg_high"), sem("msg_low"), sem("picked"), sem("added")
        z_tr, z_ev0, z_ev1 = sem("z_tr"), sem("z_ev0"), sem("z_ev1")
        u_mm, u_ev, bn1_ready = sem("u_mm"), sem("u_ev"), sem("bn1_ready")
        v_made, z2_mm, z2_ev, bn2_ready = sem("v_made"), sem("z2_mm"), sem("z2_ev"), sem("bn2_ready")
        zn_made, zn_tr = sem("zn_made"), sem("zn_tr")
        xr_in, y_made, y_tr, y_ev0, y_ev1 = sem("xr_in"), sem("y_made"), sem("y_tr"), sem("y_ev0"), sem("y_ev1")
        lg_mm, lg_ev, ex_ask, ex_done, w_made = (sem("lg_mm"), sem("lg_ev"), sem("ex_ask"),
                                                 sem("ex_done"), sem("w_made"))
        a_mm, a_ev, d_mm, d_ev = sem("a_mm"), sem("a_ev"), sem("d_mm"), sem("d_ev")
        out_made, out_done = sem("out_made"), sem("out_done")

        def rsqrt(link, dve, var, rows, n, asked):
            a, b, y, t = (r[0:rows, 0:n] for r in (r_a, r_b, r_y, r_t))
            link(nc.vector.tensor_scalar(a, var, EPS, None, ALU.add))
            nc.vector.reciprocal(b, a).then_inc(sqrt_ask, 1)
            dve.wait_ge(sqrt_done, asked)
            link(nc.vector.tensor_tensor(t, y, y, ALU.mult))
            link(nc.vector.tensor_tensor(t, t, a, ALU.mult))
            link(nc.vector.tensor_scalar(t, t, -0.5, 1.5, ALU.mult, ALU.add))
            link(nc.vector.tensor_tensor(y, y, t, ALU.mult))
            return y

        def sqrt_for(act, rows, n, asked):
            act.wait_ge(sqrt_ask, asked)
            nc.scalar.activation(r_y[0:rows, 0:n], r_b[0:rows, 0:n], ACT.Sqrt).then_inc(sqrt_done, 1)

        def layer_norm(link, dve, a, o, asked, made):
            for t in range(NT):
                nc.vector.bn_stats(st_ln[0:TP, t, :], a[0:TP, t, :]).then_inc(link.sem, 1)
            link.n += NT
            dve.wait_ge(link.sem, link.base + link.n)
            for t in range(NT):
                nc.vector.bn_aggr(mv[0:TP, t, :], st_ln[0:TP, t, :]).then_inc(link.sem, 1)
            link.n += NT
            dve.wait_ge(link.sem, link.base + link.n)
            y = rsqrt(link, dve, mv[0:TP, :, 1], TP, NT, asked)
            for t in range(NT):
                nc.vector.tensor_scalar(o[0:TP, t, :], a[0:TP, t, :], mv[0:TP, t, 0:1], y[0:TP, t:t + 1],
                                        ALU.subtract, ALU.mult).then_inc(made, 1)

        ctx.enter_context(nc.allow_non_contiguous_dma(reason="small vectors and slot records"))

        def is_unsorted(eng):
            eng.wait_ge(flag_made, 1)
            return eng.value_load(unsorted[0:1, 0:1], min_val=0, max_val=E) > 0

        def load_attributes(sp, a):
            for k, (b0, nb) in enumerate(ATT_B):
                for b in range(b0, min(b0 + nb, FULL)):
                    sp.dma_start(att_all[:, b, :, :], a[b * BLK:(b + 1) * BLK, :]
                                 .rearrange("(p q) w -> p q w", q=Q)).then_inc(att_loaded[k], 16)
                if b0 <= FULL < b0 + nb:
                    sp.dma_start(att_all[0:FULL_P, FULL, :, :], a[FULL * BLK:FULL * BLK + FULL_P * Q, :]
                                 .rearrange("(p q) w -> p q w", q=Q)).then_inc(att_loaded[k], 16)
                    sp.dma_start(att_all[FULL_P:FULL_P + 1, FULL, 0:REST, :], a[E - REST:E, :].unsqueeze(0))\
                        .then_inc(att_loaded[k], 16)

        def loads_of(k):
            b0, nb = ATT_B[k]
            return max(min(b0 + nb, FULL) - b0, 0) + (2 if b0 <= FULL < b0 + nb else 0)

        def raw_of(k, half):
            b0, nb = ATT_B[k]
            b0, nb = b0 + half * nb // 2, nb // 2
            return att_all[:, b0:b0 + nb, :, :].rearrange("p b q w -> p (b q) w").unsqueeze(2)\
                .to_broadcast([128, nb * Q, 2, DE])

        def hl_of(k, half):
            return att_hl[:, k % 2, 0:ATT_B[k][1] // 2 * Q, half * 4 * DE:(half + 1) * 4 * DE]\
                .rearrange("p k (a w) -> p k a w", a=2)

        with nc.Block() as block:
            @block.sync
            def _(sp):
                sp.dma_start(dst_i, dst.rearrange("(p c) -> p c", p=TP)).then_inc(edges_in, 16)
                sp.dma_start(dst_next[0:TP - 1, :], dst[EC:E].rearrange("(p c) -> p c", c=EC)[:, 0:1])\
                    .then_inc(edges_in, 16)
                sp.dma_start(src_i, src.rearrange("(p c) -> p c", p=TP)).then_inc(edges_in, 16)
                sp.dma_start(h[0:TP, :, :], x.rearrange("(t p) d -> p t d", p=TP)).then_inc(x_in, 16)
                sp.wait_ge(zeros_made, 3)
                branch = is_unsorted(sp)
                with sp.If(branch):
                    att_p = edge_attr.rearrange("(p c) w -> p c w", p=TP)

                    def stage_att(k, b):
                        sp.dma_start(stage[0:TP, b, :, ATT:RW], att_p[:, ds(k * SB, SB), :])\
                            .then_inc(staged_att[b], 16)

                    stage_att(0, 0)
                    stage_att(1, 1)
                    with sp.Fori(1, NSB // 2) as i:
                        for b in range(2):
                            sp.wait_ge(scattered[b], i * 16 * SB)
                            stage_att(2 * i + b, b)
                    sp.wait_ge(scattered[0], NSB // 2 * 16 * SB)
                    stage_att(NSB - 1, 0)
                    sp.wait_ge(scattered[0], 16 * SB * ((NSB + 1) // 2))
                    sp.wait_ge(scattered[1], 16 * SB * (NSB // 2))
                    sp.dma_start(ends_d[0:E, :], rec[:, 0:ATT]).then_inc(ends_out, 16)
                    load_attributes(sp, rec[:, ATT:RW])
                with sp.Else():
                    load_attributes(sp, edge_attr)
                for l in range(L):
                    for col, k, a in ((V_B1, 4, mlp_b1), (V_G1, 4, bn1_g), (V_BB1, 4, bn1_b),
                                      (V_B2, 2, mlp_b2), (V_G2, 2, bn_g), (V_BB2, 2, bn_b)):
                        sp.dma_start(vec_all[:, l, col:col + k],
                                     a[l, :].rearrange("(f p) -> p f", p=128)).then_inc(vec_in, 16)
                sp.dma_start(vec_all[:, :, V_EPS], eps.unsqueeze(0).to_broadcast([128, L])).then_inc(vec_in, 16)
                moe = [(sW1_s[:, :, :], sW1.rearrange("(k p) f -> p k f", p=128)),
                       (sW2_s[:, :, :], sW2.rearrange("(k p) f -> p k f", p=128)),
                       (sW3_s[:, :], sW3),
                       (gW_s[:, :, :], gW.rearrange("(k p) e -> p k e", p=128)),
                       (gb_s[:, :], gb.unsqueeze(0).to_broadcast([128, NE])),
                       (sb1_s[:, :], sb1.rearrange("(f p) -> p f", p=128)),
                       (sb2_s[:, :], sb2.rearrange("(f p) -> p f", p=128)),
                       (eb1_s[:, :], eb1.rearrange("e p -> p e")),
                       (b_out[0:1, :], sb3.unsqueeze(0)),
                       (b_out[1:1 + NE, :], eb3)]
                for e in range(NE):
                    half = slice((e % 2) * EH2, (e % 2 + 1) * EH2)
                    moe += [(eW1_s[:, e, :, :], eW1[e, :, :].rearrange("(k p) f -> p k f", p=128)),
                            (eW2_s[:, e, half], eW2[e, :, :]),
                            (eW3_s[half, e // 2, :], eW3[e, :, :]),
                            (eb2_s[half, e // 2:e // 2 + 1], eb2[e, :].unsqueeze(1))]
                for o, i in moe:
                    sp.dma_start(o, i).then_inc(moe_in, 16)
                sp.wait_ge(vec_in, 16 * (6 * L + 1))
                sp.wait_ge(moe_in, 16 * len(moe))
                for b in range(2):
                    sp.wait_ge(att_out[b], 32 * ((len(ATT_B) + 1 - b) // 2))
                sp.wait_ge(ends_out, 32)

            @block.gpsimd
            def _(pool):
                gp = nc.gpsimd
                gp.memset(lower[:, :], 1.0).then_inc(pool_own, 1)
                gp.memset(ones[:, :], 1.0).then_inc(pool_own, 1)
                gp.memset(ident[:, :], 0.0).then_inc(pool_own, 1)
                gp.memset(sel[:, :, :], 0.0).then_inc(pool_own, 1)
                pool.wait_ge(pool_own, 4)
                gp.affine_select(out=ident[:, :], in_=ident[:, :], compare_op=ALU.not_equal, fill=1.0,
                                 base=0, pattern=[[-1, 128]], channel_multiplier=1).then_inc(consts, 1)
                gp.affine_select(out=lower[:, :], in_=lower[:, :], compare_op=ALU.is_gt, fill=0.0,
                                 base=0, pattern=[[1, 128]], channel_multiplier=-1).then_inc(consts, 1)
                gp.affine_select(out=sel[:, :, :].rearrange("p q (r c) -> p q r c", r=2),
                                 in_=sel[:, :, :].rearrange("p q (r c) -> p q r c", r=2),
                                 compare_op=ALU.not_equal, fill=1.0, base=1,
                                 pattern=[[2, 2], [1, 2], [0, EH2]], channel_multiplier=-1).then_inc(consts, 1)
                gp.iota(iota_n[:, :], pattern=[[1, TP]], base=0, channel_multiplier=0,
                        allow_small_or_imprecise_dtypes=True).then_inc(consts, 1)
                gp.iota(part_id[:, :], pattern=[[0, 1]], base=0, channel_multiplier=1,
                        allow_small_or_imprecise_dtypes=True).then_inc(consts, 1)
                gp.iota(g_iota[:, :], pattern=[[1, NG]], base=0, channel_multiplier=0,
                        allow_small_or_imprecise_dtypes=True).then_inc(consts, 1)
                branch = is_unsorted(pool)
                with pool.If(branch):
                    def scatter(k, b, turn):
                        pool.wait_ge(staged, 3 * (k + 1))
                        pool.wait_ge(staged_att[b], 16 * turn)
                        pool.sem_inc(pool_pace)
                        for c in range(SB):
                            gp.indirect_dma_start(
                                rec, bass.IndirectOffsetOnAxis(ap=stage_ix[0:TP, b, c:c + 1], axis=0),
                                stage[0:TP, b, c, :], None).then_inc(scattered[b], 16)

                    with pool.Fori(0, NSB // 2) as i:
                        scatter(2 * i, 0, i + 1)
                        scatter(2 * i + 1, 1, i + 1)
                    scatter(NSB - 1, 0, NSB // 2 + 1)

            @block.scalar
            def _(act):
                act.wait_ge(zeros_made, 3)
                act.dma_start(ends_d[E:E + TAIL, :].unsqueeze(0), pad).then_inc(ends_out, 16)
                branch = is_unsorted(act)
                with act.If(branch):
                    act.wait_ge(places_made, 1)

                    def stage_block(k, b):
                        cols = ds(k * SB, SB)
                        o = stage[0:TP, b, :, :]
                        nc.scalar.copy(o[:, :, DST], dst_f[:, cols]).then_inc(staged, 1)
                        nc.scalar.copy(o[:, :, SRC].bitcast(I32), src_i[:, cols]).then_inc(staged, 1)
                        nc.scalar.copy(stage_ix[0:TP, b, :], place_i[:, cols]).then_inc(staged, 1)

                    stage_block(0, 0)
                    stage_block(1, 1)
                    with act.Fori(1, NSB // 2) as i:
                        for b in range(2):
                            act.wait_ge(scattered[b], i * 16 * SB)
                            stage_block(2 * i + b, b)
                    act.wait_ge(scattered[0], NSB // 2 * 16 * SB)
                    stage_block(NSB - 1, 0)
                with act.Else():
                    act.wait_ge(ends_made, 2)
                    act.dma_start(ends_d[0:E, :].rearrange("(p c) w -> p c w", p=TP), ends[0:TP, :, :])\
                        .then_inc(ends_out, 16)
                sqrt_for(act, TP, NT, 1)

                def high_part(k):
                    b0, nb = ATT_B[k]
                    act.wait_ge(att_loaded[k], 16 * loads_of(k))
                    if k >= 2:
                        act.wait_ge(att_tr, k - 1)
                    for half in range(2):
                        nc.scalar.copy(hl_of(k, half)[..., 0:DE].bitcast(F32R), raw_of(k, half)).then_inc(att_high, 1)

                def evacuate(k):
                    b, (b0, nb) = k % 2, ATT_B[k]
                    act.wait_ge(att_tr, k + 1)
                    if k >= 2:
                        act.wait_ge(att_out[b], k // 2 * 32)
                    nc.scalar.copy(att_t[b][:, 0:nb // 2 * BLK].rearrange("p (r c q) -> p r c q", c=128, q=Q),
                                   ps[:, 4 * b:4 * b + nb // 2, :].rearrange("p r (q c) -> p r c q", q=Q))\
                        .then_inc(att_ev, 1)
                    act.wait_ge(att_ev, k + 1)
                    for half in range(2):
                        start, width = (b0 + half * nb // 2) * BLK, nb // 2 * BLK
                        act.dma_start(attr_t[:, start:start + width],
                                      att_t[b][half * 64:(half + 1) * 64, 0:width]).then_inc(att_out[b], 16)

                high_part(0)
                for k in range(len(ATT_B)):
                    if k + 1 < len(ATT_B):
                        high_part(k + 1)
                    evacuate(k)

            @block.vector
            def _(dve):
                vc = nc.vector
                link = Link(dve, d_pre)
                vc.memset(eW2_s[:, :, :], 0.0).then_inc(zeros_made, 1)
                vc.memset(att_all[:, FULL:NBLK, :, :], 0.0).then_inc(zeros_made, 1)
                link(vc.memset(pad[:, :, SRC], 0.0))
                vc.memset(pad[:, :, DST], float(2 * N)).then_inc(zeros_made, 1)
                vc.memset(at[4 * DE:KA, :, :].bitcast(F32), 1.0).then_inc(d_pre, 1)
                vc.memset(breaks[:, :], 0.0).then_inc(d_pre, 1)
                vc.memset(tile_part[:, :], 0.0).then_inc(d_pre, 1)
                link.n += 3
                dve.wait_ge(d_pre, link.n)
                dve.wait_ge(edges_in, 48)
                vc.tensor_copy(dst_next_f[0:TP - 1, :], dst_next[0:TP - 1, :]).then_inc(d_pre, 1)
                link.n += 1
                link(vc.tensor_copy(dst_f, dst_i))
                link(vc.tensor_tensor(bucket[:, 0:EC - 1], dst_f[:, 0:EC - 1], dst_f[:, 1:EC], ALU.is_gt))
                vc.tensor_reduce(breaks[0:TP, 0:1], bucket[:, 0:EC - 1], AX, ALU.add).then_inc(d_pre, 1)
                vc.tensor_tensor(breaks[0:TP - 1, 1:2], dst_f[0:TP - 1, EC - 1:EC], dst_next_f[0:TP - 1, :],
                                 ALU.is_gt).then_inc(d_pre, 1)
                link.n += 2
                for b in range(NT):
                    m = (mask, prefix)[b % 2]
                    dve.wait_ge(d_pre, link.n - 1)
                    link.n += 1
                    vc.tensor_scalar(m, dst_f, float((b + 1) * TP), 0.0, ALU.is_lt, ALU.add,
                                     accum_out=upto[0:TP, b:b + 1]).then_inc(d_pre, 1)
                dve.wait_ge(d_pre, link.n)
                link(vc.tensor_tensor(breaks[:, 0:1], breaks[:, 0:1], breaks[:, 1:2], ALU.add))
                vc.tensor_copy(tile_part[0:TP, 0:1], upto[0:TP, 0:1]).then_inc(parts_made, 1)
                vc.tensor_tensor(tile_part[0:TP, 1:NT], upto[0:TP, 1:NT], upto[0:TP, 0:NT - 1],
                                 ALU.subtract).then_inc(parts_made, 1)
                vc.tensor_copy(ends[0:TP, :, DST], dst_f).then_inc(ends_made, 1)
                vc.tensor_copy(ends[0:TP, :, SRC].bitcast(I32), src_i).then_inc(ends_made, 1)
                dve.wait_ge(parts_summed, 1)
                vc.tensor_copy(unsorted[:, :], ps[0:1, 1, 0:1]).then_inc(flag_made, 1)
                link(vc.tensor_copy(cnt[:, :], ps[0:NT, 0, 0:1]))
                link(vc.tensor_scalar(cnt_i[:, :], cnt[:, :], float(GS - 1), None, ALU.add))
                link(vc.tensor_scalar(cnt_i[:, :], cnt_i[:, :], GS.bit_length() - 1, None,
                                      ALU.logical_shift_right))
                vc.tensor_copy(groups[:, :], cnt_i[:, :]).then_inc(groups_made, 1)
                dve.wait_ge(groups_made, 1)
                link(vc.scalar_tensor_tensor(out=slack[:, :], in0=groups[:, :], scalar=-float(GS), in1=cnt[:, :],
                                             op0=ALU.mult, op1=ALU.add))
                link(vc.tensor_scalar(slack_b[:, :], ones[0:NT, :], slack[:, 0:1], None, ALU.mult))
                dve.wait_ge(groups_summed, 1)
                link(vc.tensor_tensor(groups_end[:, :], groups[:, :], ps[0:NT, 3, 0:1], ALU.add))
                vc.tensor_scalar(ended[:, :], g_iota[0:NT, :], groups_end[:, 0:1], None, ALU.is_ge)\
                    .then_inc(ended_made, 1)
                dve.wait_ge(ended_summed, 1)
                link(vc.scalar_tensor_tensor(out=first_f[:, :], in0=g_iota[0:1, :], scalar=float(GS),
                                             in1=ps[0:1, 4, 0:NG], op0=ALU.mult, op1=ALU.add))
                link(vc.tensor_scalar(first_edge[:, :], first_f[:, :], float(E), None, ALU.min))
                link(vc.tensor_scalar(group_tile[:, :], ps[0:1, 5, 0:NG], float(NT - 1), None, ALU.min))
                link(vc.tensor_scalar(tile_base[:, :], ps[:, 5, 0:NG], float(NT - 1), -float(TP), ALU.min, ALU.mult))
                link(vc.tensor_scalar(w1_low[:, :], part_id[:, :], float(4 * DE), None, ALU.is_equal))
                link(vc.tensor_scalar(w1_high[:, :], part_id[:, :], float(2 * DE), None, ALU.is_lt))
                link(vc.tensor_tensor(w1_high[:, :], w1_high[:, :], w1_low[:, :], ALU.add))
                link(vc.tensor_scalar(w1_low[:, :], w1_high[:, :], -1.0, 1.0, ALU.mult, ALU.add))
                branch = is_unsorted(dve)
                with dve.If(branch):
                    chain = Link(dve, d_rank)
                    chain(vc.memset(ones_c, 1.0))
                    chain(vc.memset(bucket, 0.0))
                    chain(vc.memset(rank, 0.0))
                    for b in range(1, NT):
                        chain(vc.scalar_tensor_tensor(out=bucket, in0=dst_f, scalar=float(b * TP), in1=bucket,
                                                      op0=ALU.is_ge, op1=ALU.add))
                    chain(vc.memset(offset[:, :], -1.0))
                    chain(vc.tensor_tensor(offset[0:TP, :], offset[0:TP, :], ps[0:TP, 2, 0:NT], ALU.add))
                    chain(vc.tensor_tensor(offset[0:TP, 1:NT], offset[0:TP, 1:NT], ps[0:TP, 6, 0:NT - 1], ALU.add))
                    for b in range(NT):
                        chain(vc.tensor_scalar(mask, bucket, float(b), None, ALU.is_equal))
                        chain(vc.tensor_tensor_scan(prefix, ones_c, mask, 0.0, ALU.mult, ALU.add))
                        chain(vc.tensor_scalar(prefix, prefix, offset[0:TP, b:b + 1], None, ALU.add))
                        chain(vc.tensor_tensor(part, mask, prefix, ALU.mult))
                        chain(vc.tensor_tensor(rank, rank, part, ALU.add))
                    vc.tensor_copy(place_i, rank).then_inc(places_made, 1)
                dve.wait_ge(vec_in, 16 * (6 * L + 1))
                link(vc.tensor_scalar(vec_all[:, :, V_EPS], vec_all[:, :, V_EPS], 1.0, None, ALU.add))
                link(vc.memset(vec_all[:, :, V_FLOOR], 0.0))
                link(vc.memset(vec_all[:, L - 1:L, V_FLOOR], -BIG))
                dve.wait_ge(x_in, 16)
                layer_norm(link, dve, h, h, 1, h_rows)

                for k, (b0, nb) in enumerate(ATT_B):
                    for half in range(2):
                        dve.wait_ge(att_high, 2 * k + half + 1)
                        hl = hl_of(k, half)
                        vc.tensor_tensor(hl[..., DE:2 * DE], raw_of(k, half), hl[..., 0:DE], ALU.subtract)\
                            .then_inc(att_low, 1)

            @block.tensor
            def _(pe):
                pe.wait_ge(parts_made, 2)
                pe.wait_ge(consts, 6)
                nc.tensor.matmul(ps[0:NT, 0, 0:1], tile_part[0:TP, :], ones[0:TP, 0:1], start=True, stop=True)
                nc.tensor.matmul(ps[0:1, 1, 0:1], breaks[:, 0:1], ones[:, 0:1], start=True, stop=True)
                nc.tensor.matmul(ps[:, 2, 0:NT], lower[:, :], tile_part[:, :], start=True, stop=True)
                nc.tensor.matmul(ps[:, 6, 0:NT], ones[0:TP, :], upto[0:TP, :], start=True, stop=True)\
                    .then_inc(parts_summed, 1)
                pe.wait_ge(groups_made, 1)
                nc.tensor.matmul(ps[0:NT, 3, 0:1], lower[0:NT, 0:NT], groups[:, :], start=True, stop=True)\
                    .then_inc(groups_summed, 1)
                pe.wait_ge(ended_made, 1)
                nc.tensor.matmul(ps[:, 4, 0:NG], slack_b[:, :], ended[:, :], start=True, stop=True)
                nc.tensor.matmul(ps[:, 5, 0:NG], ones[0:NT, :], ended[:, :], start=True, stop=True)\
                    .then_inc(ended_summed, 1)

                for k, (b0, nb) in enumerate(ATT_B):
                    b = k % 2
                    pe.wait_ge(att_low, 2 * k + 2)
                    if k >= 2:
                        pe.wait_ge(att_ev, k - 1)
                    for r in range(nb // 2):
                        for q in range(Q):
                            last = nc.tensor.transpose(ps[:, 4 * b + r, q * 128:(q + 1) * 128],
                                                       att_hl[:, b, r * Q + q, :], ident[:, :])
                    last.then_inc(att_tr, 1)

        def groups_loop(eng, step):
            for b in range(UN):
                step(b, 0, b)
            with eng.Fori(1, NIT - 1) as i:
                for b in range(UN):
                    step(i * UN + b, i, b)
            for b in range(UN):
                step((NIT - 1) * UN + b, NIT - 1, b)

        def is_past(g, k):
            return not isinstance(g, int) or g >= k

        def has(g, k):
            return not isinstance(g, int) or g + k < NG

        LAG, LAG_A = 4, 5
        GATHER_LAG = 3

        with nc.Block() as block:
            @block.sync
            def _(sp):
                with sp.Fori(0, L) as l:
                    sp.wait_ge(h_rows, (l + 1) * NT)
                    for k in range(4):
                        sp.dma_start(w1_raw[k * DE:(k + 1) * DE, :],
                                     ee_w1[ds(l, 1), :, :].rearrange("a k d -> (a k) d")).then_inc(w_in, 16)
                    for k in range(2):
                        sp.dma_start(w1_raw[4 * DE + k:4 * DE + k + 1, :], ee_b1[ds(l, 1), :]).then_inc(w_in, 16)
                    sp.dma_start(w2_raw[:, :, :], ee_w2[ds(l, 1), :, :].rearrange("a (k p) d -> p (a k) d", p=128))\
                        .then_inc(w_in, 16)
                    sp.dma_start(b2_all[:, :], ee_b2[ds(l, 1), :].to_broadcast([128, D])).then_inc(w_in, 16)

                    def load_group(g, b):
                        if is_past(g, UN):
                            sp.wait_ge(mm1, l * NG + g - (UN - 1))
                            sp.wait_ge(picked, l * NG + g - (UN - 1))
                            sp.wait_ge(msg_high, l * NG + g - (UN - 1))
                            sp.sem_inc(sp_pace)
                        first = sp.value_load(first_edge[0:1, ds(g, 1)], min_val=0, max_val=E)
                        sp.dma_start(at[0:4 * DE, b, :].bitcast(F32), attr_t[:, ds(first, GS)]).then_inc(at_in[b], 16)
                        sp.dma_start(meta[:, b, :, :].bitcast(F32), ends_d[ds(first, GS), :]
                                     .rearrange("(j p) w -> p j w", j=2)).then_inc(meta_in[b], 16)

                    for b in range(UN):
                        load_group(b, b)
                    for k in range(2):
                        sp.dma_start(m1[:, k, :], mlp_w1[ds(l, 1), k * 128:(k + 1) * 128, :]
                                     .rearrange("a p f -> (a p) f")).then_inc(m_in, 16)
                    for k in range(4):
                        sp.dma_start(m2[:, k, :], mlp_w2[ds(l, 1), k * 128:(k + 1) * 128, :]
                                     .rearrange("a p f -> (a p) f")).then_inc(m_in, 16)
                    with sp.Fori(1, NIT) as i:
                        for b in range(UN):
                            load_group(i * UN + b, b)

            @block.gpsimd
            def _(pool):
                with pool.Fori(0, L) as l:
                    pool.wait_ge(tab_out, (l + 1) * 16)
                    pool.sem_inc(pool_pace)

                    def gather(g, i, b):
                        pool.wait_ge(meta_in[b], (l * NIT + i + 1) * 16)
                        pool.wait_ge(e_out, l * NG + g + 1)
                        pool.sem_inc(pool_pace)
                        for j in range(2):
                            nc.gpsimd.indirect_dma_start(
                                e_sb[:, b % 4, j, :], None, table,
                                bass.IndirectOffsetOnAxis(ap=meta[:, b, j, SRC:SRC + 1], axis=0),
                                compute_op=ALU.add).then_inc(gathered[b % 4], 16)

                    with pool.Fori(0, NIT) as i:
                        for b in range(UN):
                            gather(i * UN + b, i, b)

            def z2_out(act, l, c):
                t0, nt = CH[c]
                n = nt * TP
                for f in range(2):
                    act.wait_ge(z2_mm, l * NCH * 2 + c * 2 + f + 1)
                    nc.scalar.activation(z2[:, f, t0 * TP:t0 * TP + n], ps[:, (c % 2) * 2 + f, 0:n], ACT.Identity,
                                         bias=vec[:, V_B2 + f:V_B2 + f + 1]).then_inc(z2_ev, 1)

            @block.scalar
            def _(act):
                with act.Fori(0, L) as l:
                    act.wait_ge(w_in, (l + 1) * 16 * 8)
                    nc.scalar.copy(w1_h[:, :], w1_raw[:, :]).then_inc(w_high, 1)
                    nc.scalar.copy(w2_h[:, :, :], w2_raw[:, :, :]).then_inc(w_high, 1)
                    act.wait_ge(tab_made, l + 1)
                    act.dma_start(table.rearrange("(t p) d -> p t d", p=TP), node_tab[0:TP, :, :])\
                        .then_inc(tab_out, 16)

                    def hidden_high(g, b):
                        act.wait_ge(mm1, l * NG + g + 1)
                        if is_past(g, 2):
                            act.wait_ge(mm2, l * NG + g - 1)
                        nc.scalar.activation(hid_h[:, b, :, :].rearrange("p a c -> p (a c)"), ps[:, b, :],
                                             ACT.Relu).then_inc(hid_high, 1)

                    def evacuate(g, i, b):
                        act.wait_ge(mm2, l * NG + g + 1)
                        if is_past(g, 4):
                            act.wait_ge(msg_low, l * NG + g - 3)
                        nc.scalar.copy(e_sb[:, b % 4, :, :].rearrange("p a c -> p (a c)"), ps[:, 2 + b % 2, :])\
                            .then_inc(e_out, 1)

                    def message_high(g, turn4, b):
                        act.wait_ge(gathered[b % 4], turn4 * 32)
                        if is_past(g, 2):
                            act.wait_ge(mm3, l * NG + g - 1)
                        nc.scalar.activation(msg_h[:, b % 2, :, :], e_sb[:, b % 4, :, :], ACT.Relu)\
                            .then_inc(msg_high, 1)

                    def turns4(g):
                        return l * (NG // 4) + g // 4 + 1

                    hidden_high(0, 0)

                    def step(g, i, b):
                        if has(g, 1):
                            hidden_high(g + 1, (b + 1) % 2)
                        if is_past(g, GATHER_LAG):
                            bb = (b - GATHER_LAG) % UN
                            back = 0 if b >= GATHER_LAG else 1
                            t4 = (turns4(g - GATHER_LAG) if isinstance(g, int)
                                  else l * (NG // 4) + (i - back) * 2 + bb // 4 + 1)
                            message_high(g - GATHER_LAG, t4, bb)
                        evacuate(g, i, b)

                    groups_loop(act, step)
                    for g in range(NG - GATHER_LAG, NG):
                        message_high(g, turns4(g), g % UN)

                    for c, (t0, nt) in enumerate(CH):
                        n = nt * TP
                        act.wait_ge(z_tr, l * NCH + c + 1)
                        if c >= 2:
                            act.wait_ge(u_mm, l * NCH * 4 + (c - 1) * 4)
                        nc.scalar.copy(zT[:, c % 2, 0, 0:n], ps[:, 6, 0:n]).then_inc(z_ev0, 1)
                        for f in range(4):
                            act.wait_ge(u_mm, l * NCH * 4 + c * 4 + f + 1)
                            nc.scalar.activation(u[:, f, t0 * TP:t0 * TP + n], ps[:, f, 0:n], ACT.Identity,
                                                 bias=vec[:, V_B1 + f:V_B1 + f + 1]).then_inc(u_ev, 1)
                    sqrt_for(act, 128, 4, l * 2 + 2)
                    act.wait_ge(bn1_ready, l + 1)
                    for c, (t0, nt) in enumerate(CH):
                        n = nt * TP
                        if c >= 2:
                            act.wait_ge(z2_mm, l * NCH * 2 + (c - 1) * 2)
                        for f in range(4):
                            nc.scalar.activation(v[:, c % 2, f, 0:n], u[:, f, t0 * TP:t0 * TP + n], ACT.Relu,
                                                 bias=r_o[:, f:f + 1], scale=r_s[:, f:f + 1]).then_inc(v_made, 1)
                        if c >= 1:
                            z2_out(act, l, c - 1)
                    z2_out(act, l, NCH - 1)
                    sqrt_for(act, 128, 2, l * 2 + 3)
                    act.wait_ge(bn2_ready, l + 1)
                    for c, (t0, nt) in enumerate(CH):
                        for f in range(2):
                            a = z2[:, f, t0 * TP:(t0 + nt) * TP]
                            nc.scalar.activation(a, a, ACT.Identity, bias=r_o[:, f:f + 1],
                                                 scale=r_s[:, f:f + 1]).then_inc(zn_made, 1)

            def bn_affine(link, dve, n, v_g, v_b, asked, ready):
                y = rsqrt(link, dve, mv[:, 0:n, 1], 128, n, asked)
                link(nc.vector.tensor_tensor(r_s[:, 0:n], y, vec[:, v_g:v_g + n], ALU.mult))
                link(nc.vector.tensor_tensor(r_t[:, 0:n], mv[:, 0:n, 0], r_s[:, 0:n], ALU.mult))
                nc.vector.tensor_tensor(r_o[:, 0:n], vec[:, v_b:v_b + n], r_t[:, 0:n], ALU.subtract)\
                    .then_inc(ready, 1)

            @block.vector
            def _(dve):
                vc = nc.vector
                with dve.Fori(0, L) as l:
                    CL = 1 + 14 + 4 + 4
                    link = Link(dve, d_lay, l * CL)
                    link(vc.tensor_copy(vec[:, :], vec_all[:, ds(l, 1), :].rearrange("p a v -> p (a v)")))
                    dve.wait_ge(w_in, (l + 1) * 16 * 8)
                    vc.tensor_tensor(node_tab[0:TP, :, :], h[0:TP, :, :],
                                     b2_all[0:TP, :].unsqueeze(1).to_broadcast([TP, NT, D]), ALU.add)\
                        .then_inc(tab_made, 1)
                    link(vc.tensor_scalar(agg[0:TP, :, :], h[0:TP, :, :], vec[0:TP, V_EPS:V_EPS + 1], None, ALU.mult))
                    dve.wait_ge(w_high, (l + 1) * 2)
                    link(vc.tensor_tensor(w1_l[:, :], w1_raw[:, :], w1_h[:, :].bitcast(F32), ALU.subtract))
                    link(vc.tensor_scalar(w1_raw[:, :], w1_h[:, :].bitcast(F32), w1_high[0:KA, :], None, ALU.mult))
                    link(vc.scalar_tensor_tensor(out=w1_s[:, :], in0=w1_l[:, :].bitcast(F32), scalar=w1_low[0:KA, :],
                                                 in1=w1_raw[:, :], op0=ALU.mult, op1=ALU.add))
                    vc.tensor_tensor(w2_l[:, :, :], w2_raw[:, :, :], w2_h[:, :, :].bitcast(F32),
                                     ALU.subtract).then_inc(w_ready, 1)

                    def hidden_low(g, b):
                        dve.wait_ge(hid_high, l * NG + g + 1)
                        vc.scalar_tensor_tensor(
                            out=hid_l[:, b, :, :].rearrange("p a c -> p (a c)"), in0=ps[:, b, :], scalar=0.0,
                            in1=hid_h[:, b, :, :].rearrange("p a c -> p (a c)").bitcast(F32), op0=ALU.max,
                            op1=ALU.subtract).then_inc(hid_low, 1)

                    def message_low(g, turn, b):
                        dve.wait_ge(meta_in[b], turn * 16)
                        if is_past(g, 2):
                            dve.wait_ge(mm3, l * NG + g - 1)
                        for j in range(2):
                            p = vc.tensor_scalar(pick[:, b % 2, j, 0:TP], iota_n[:, :],
                                                 meta_f[:, b, j, DST:DST + 1], tile_base[:, ds(g, 1)],
                                                 ALU.subtract, ALU.is_equal)
                        p.then_inc(picked, 1)
                        dve.wait_ge(msg_high, l * NG + g + 1)
                        vc.scalar_tensor_tensor(
                            out=msg_l[:, b % 2, :, :].rearrange("p a c -> p (a c)"),
                            in0=e_sb[:, b % 4, :, :].rearrange("p a c -> p (a c)"), scalar=0.0,
                            in1=msg_h[:, b % 2, :, :].rearrange("p a c -> p (a c)").bitcast(F32), op0=ALU.max,
                            op1=ALU.subtract).then_inc(msg_low, 1)

                    def add_sums(g, b):
                        t = dve.value_load(group_tile[0:1, ds(g, 1)], min_val=0, max_val=NT - 1)
                        dve.wait_ge(mm3, l * NG + g + 1)
                        if is_past(g, 1):
                            dve.wait_ge(added, l * NG + g)
                        dst_tile = agg[0:TP, ds(t, 1), :].rearrange("p a d -> p (a d)")
                        vc.tensor_tensor(dst_tile, dst_tile, ps[0:TP, 4 + b % 2, 0:D], ALU.add).then_inc(added, 1)

                    hidden_low(0, 0)

                    def step(g, i, b):
                        if has(g, 1):
                            hidden_low(g + 1, (b + 1) % 2)
                        if is_past(g, GATHER_LAG):
                            bb = (b - GATHER_LAG) % UN
                            back = 0 if b >= GATHER_LAG else 1
                            message_low(g - GATHER_LAG, l * NIT + i - back + 1, bb)
                        if is_past(g, LAG_A):
                            add_sums(g - LAG_A, (b - LAG_A) % UN)

                    groups_loop(dve, step)
                    for k in range(NG - GATHER_LAG, NG + LAG_A - GATHER_LAG):
                        if k < NG:
                            message_low(k, l * NIT + NIT, k % UN)
                        k -= LAG_A - GATHER_LAG
                        add_sums(k, k % UN)

                    for c, (t0, nt) in enumerate(CH):
                        n = nt * TP
                        dve.wait_ge(z_tr, l * NCH + c + 1)
                        if c >= 2:
                            dve.wait_ge(u_mm, l * NCH * 4 + (c - 1) * 4)
                        vc.tensor_copy(zT[:, c % 2, 1, 0:n], ps[:, 7, 0:n]).then_inc(z_ev1, 1)
                        for f in range(4):
                            dve.wait_ge(u_ev, l * NCH * 4 + c * 4 + f + 1)
                            last = vc.bn_stats(st1[:, f, c, :], u[:, f, t0 * TP:t0 * TP + n])
                    link(last)
                    dve.sem_inc(dve_pace)
                    for f in range(4):
                        last = vc.bn_aggr(mv[:, f, :], st1[:, f, :, :].rearrange("p c s -> p (c s)"))
                    link(last)
                    bn_affine(link, dve, 4, V_G1, V_BB1, l * 2 + 2, bn1_ready)
                    for c, (t0, nt) in enumerate(CH):
                        for f in range(2):
                            dve.wait_ge(z2_ev, l * NCH * 2 + c * 2 + f + 1)
                            last = vc.bn_stats(st2[:, f, c, :], z2[:, f, t0 * TP:(t0 + nt) * TP])
                    link(last)
                    dve.sem_inc(dve_pace)
                    for f in range(2):
                        last = vc.bn_aggr(mv[:, f, :], st2[:, f, :, :].rearrange("p c s -> p (c s)"))
                    link(last)
                    bn_affine(link, dve, 2, V_G2, V_BB2, l * 2 + 3, bn2_ready)
                    for t in range(NT):
                        dve.wait_ge(zn_tr, l * NT + t + 1)
                        last = vc.scalar_tensor_tensor(out=h[0:TP, t, :], in0=ps[0:TP, t % 4, 0:D],
                                                       scalar=vec[0:TP, V_FLOOR:V_FLOOR + 1], in1=h[0:TP, t, :],
                                                       op0=ALU.max, op1=ALU.add)
                        last.then_inc(h_rows, 1)
                    dve.wait_ge(h_rows, (l + 2) * NT)
                    assert link.n == CL, link.n

            @block.tensor
            def _(pe):
                with pe.Fori(0, L) as l:
                    pe.wait_ge(w_ready, l + 1)

                    def hidden(g, turn, b):
                        pe.wait_ge(at_in[b], turn * 16)
                        if is_past(g, 2):
                            pe.wait_ge(hid_low, l * NG + g - 1)
                        for half in range(2):
                            last = nc.tensor.matmul(ps[:, b % 2, half * GS:(half + 1) * GS],
                                                    w1_s[:, half * 128:(half + 1) * 128], at[:, b, :],
                                                    start=True, stop=True)
                        last.then_inc(mm1, 1)

                    def edge_out(g, b):
                        pe.wait_ge(hid_low, l * NG + g + 1)
                        if is_past(g, 2):
                            pe.wait_ge(e_out, l * NG + g - 1)
                        s = b % 2
                        for j in range(2):
                            terms = [(a, w, k) for k in range(2)
                                     for a, w in ((hid_h, w2_h), (hid_h, w2_l), (hid_l, w2_h))]
                            for n, (a, w, k) in enumerate(terms):
                                last = nc.tensor.matmul(ps[:, 2 + s, j * D:(j + 1) * D],
                                                        a[:, s, k, j * 128:(j + 1) * 128], w[:, k, :],
                                                        start=(n == 0), stop=(n == len(terms) - 1))
                        last.then_inc(mm2, 1)

                    def sums(g, b):
                        pe.wait_ge(picked, l * NG + g + 1)
                        pe.wait_ge(msg_low, l * NG + g + 1)
                        if is_past(g, 2):
                            pe.wait_ge(added, l * NG + g - 1)
                        s = b % 2
                        for n, (j, m) in enumerate(((0, msg_h), (0, msg_l), (1, msg_h), (1, msg_l))):
                            last = nc.tensor.matmul(ps[0:TP, 4 + s, 0:D], pick[:, s, j, 0:TP], m[:, s, j, :],
                                                    start=(n == 0), stop=(n == 3))
                        last.then_inc(mm3, 1)

                    hidden(0, l * NIT + 1, 0)

                    def step(g, i, b):
                        if has(g, 1):
                            hidden(g + 1, l * NIT + i + 1 + (b + 1) // UN, (b + 1) % UN)
                        edge_out(g, b)
                        if is_past(g, LAG):
                            sums(g - LAG, b)

                    groups_loop(pe, step)
                    for k in range(NG - LAG, NG):
                        sums(k, k)

                    pe.wait_ge(added, (l + 1) * NG)
                    pe.wait_ge(m_in, (l + 1) * 16 * 6)
                    for c, (t0, nt) in enumerate(CH):
                        n = nt * TP
                        if c >= 1:
                            pe.wait_ge(z_ev0, l * NCH + c)
                            pe.wait_ge(z_ev1, l * NCH + c)
                        for half in range(2):
                            for t in range(nt):
                                last = nc.tensor.transpose(ps[:, 6 + half, t * TP:(t + 1) * TP],
                                                           agg[0:TP, t0 + t, half * 128:(half + 1) * 128],
                                                           ident[0:TP, 0:TP])
                        last.then_inc(z_tr, 1)
                        pe.wait_ge(z_ev0, l * NCH + c + 1)
                        pe.wait_ge(z_ev1, l * NCH + c + 1)
                        for f in range(4):
                            if c >= 1:
                                pe.wait_ge(u_ev, l * NCH * 4 + (c - 1) * 4 + f + 1)
                            for k in range(2):
                                last = nc.tensor.matmul(ps[:, f, 0:n], m1[:, k, f * 128:(f + 1) * 128],
                                                        zT[:, c % 2, k, 0:n], start=(k == 0), stop=(k == 1))
                            last.then_inc(u_mm, 1)
                    for c, (t0, nt) in enumerate(CH):
                        n = nt * TP
                        pe.wait_ge(v_made, l * NCH * 4 + c * 4 + 4)
                        if c >= 2:
                            pe.wait_ge(z2_ev, l * NCH * 2 + (c - 1) * 2)
                        for f in range(2):
                            for k in range(4):
                                last = nc.tensor.matmul(ps[:, (c % 2) * 2 + f, 0:n], m2[:, k, f * 128:(f + 1) * 128],
                                                        v[:, c % 2, k, 0:n], start=(k == 0), stop=(k == 3))
                            last.then_inc(z2_mm, 1)
                    for c, (t0, nt) in enumerate(CH):
                        pe.wait_ge(zn_made, l * NCH * 2 + c * 2 + 2)
                        for t in range(t0, t0 + nt):
                            if t >= 4:
                                pe.wait_ge(h_rows, (l + 1) * NT + t - 3)
                            for f in range(2):
                                last = nc.tensor.transpose(ps[0:TP, t % 4, f * 128:(f + 1) * 128],
                                                           z2[:, f, t * TP:(t + 1) * TP], ident[:, :])
                            last.then_inc(zn_tr, 1)

        with nc.Block() as block:
            @block.sync
            def _(sp):
                sp.dma_start(node_tab[0:TP, :, :], x.rearrange("(t p) d -> p t d", p=TP)).then_inc(xr_in, 16)
                for c, (t0, nt) in enumerate(CH):
                    sp.wait_ge(out_made, t0 + nt)
                    sp.dma_start(out.rearrange("(t p) d -> p t d", p=TP)[:, t0:t0 + nt, :],
                                 agg[0:TP, t0:t0 + nt, :]).then_inc(out_done, 16)
                sp.wait_ge(out_done, 16 * NCH)

            def h1_of(c):
                return zT[:, c % 2, :, :]

            def e1_of(c):
                return v[:, c % 2, :, :]

            h2_all = u_flat[:, 6400:7400].rearrange("p (s n) -> p s n", s=2)
            e2_all = u_flat[:, 7400:9400].rearrange("p (s q n) -> p s q n", s=2, q=2)

            def e2_of(c):
                return e2_all[:, c % 2, :, :]

            def units(c):
                t0, nt = CH[c]
                n = nt * TP
                y = [yT[:, k, t0 * TP:t0 * TP + n] for k in range(2)]
                got = [([(sW1_s[:, k, f * 128:(f + 1) * 128], y[k]) for k in range(2)],
                        sb1_s[:, f:f + 1], h1_of(c)[:, f, 0:n]) for f in range(2)]
                got += [([(eW1_s[:, e, k, :], y[k]) for k in range(2)],
                         eb1_s[:, e:e + 1], e1_of(c)[:, e, 0:n]) for e in range(NE)]
                got += [([(sW2_s[:, k, :], h1_of(c)[:, k, 0:n]) for k in range(2)],
                         sb2_s[:, 0:1], h2_all[:, c % 2, 0:n])]
                got += [([(eW2_s[:, 2 * q + r, :], e1_of(c)[:, 2 * q + r, 0:n]) for r in range(2)],
                         eb2_s[:, q:q + 1], e2_of(c)[:, q, 0:n]) for q in range(2)]
                return got

            @block.vector
            def _(dve):
                vc = nc.vector
                link = Link(dve, d_moe)
                dve.wait_ge(xr_in, 16)
                link(vc.tensor_tensor(h[0:TP, :, :], h[0:TP, :, :], node_tab[0:TP, :, :], ALU.add))
                layer_norm(link, dve, h, agg, 2 * L + 2, y_made)
                for c, (t0, nt) in enumerate(CH):
                    n = nt * TP
                    dve.wait_ge(y_tr, c + 1)
                    vc.tensor_copy(yT[:, 1, t0 * TP:t0 * TP + n], ps[:, 2 * (c % 2) + 1, 0:n]).then_inc(y_ev1, 1)
                    dve.wait_ge(lg_mm, c + 1)
                    vc.tensor_tensor(lg[0:TP, t0:t0 + nt, :],
                                     ps[0:TP, 4 + c % 2, 0:nt * NE].rearrange("p (t e) -> p t e", e=NE),
                                     gb_s[0:TP, :].unsqueeze(1).to_broadcast([TP, nt, NE]), ALU.add)\
                        .then_inc(lg_ev, 1)
                dve.wait_ge(lg_ev, NCH)
                mx, sm = r_a[0:TP, 0:NT], r_s[0:TP, 0:NT]

                def over(a):
                    return a.unsqueeze(2).to_broadcast([TP, NT, NE])

                g_, p_ = lg[0:TP, :, :], pr[0:TP, :, :]
                link(vc.tensor_reduce(mx, g_, AX, ALU.max))
                vc.tensor_tensor(g_, g_, over(mx), ALU.subtract).then_inc(ex_ask, 1)
                dve.wait_ge(ex_done, 1)
                link(vc.tensor_reduce(sm, p_, AX, ALU.add))
                link(vc.reciprocal(sm, sm))
                link(vc.tensor_tensor(p_, p_, over(sm), ALU.mult))
                link(vc.memset(rk[:, :, :], 0.0))
                for j in range(NE):
                    for k in range(j + 1, NE):
                        link(vc.tensor_tensor(cmp[0:TP, :], pr[0:TP, :, j], pr[0:TP, :, k], ALU.is_ge))
                        link(vc.tensor_tensor(rk[0:TP, k, :], rk[0:TP, k, :], cmp[0:TP, :], ALU.add))
                        link(vc.tensor_tensor(cmp[0:TP, :], pr[0:TP, :, k], pr[0:TP, :, j], ALU.is_gt))
                        link(vc.tensor_tensor(rk[0:TP, j, :], rk[0:TP, j, :], cmp[0:TP, :], ALU.add))
                link(vc.tensor_reduce(mx, p_, AX, ALU.max))
                vc.tensor_tensor(g_, p_, over(mx), ALU.subtract).then_inc(ex_ask, 1)
                dve.wait_ge(ex_done, 2)
                link(vc.scalar_tensor_tensor(out=p_, in0=rk[0:TP, :, :].rearrange("p e t -> p t e"), scalar=2.0,
                                             in1=p_, op0=ALU.is_lt, op1=ALU.mult))
                link(vc.tensor_reduce(sm, p_, AX, ALU.add))
                link(vc.reciprocal(sm, sm))
                link(vc.memset(w5[0:TP, :, 0:1], 1.0))
                vc.tensor_tensor(w5[0:TP, :, 1:1 + NE], p_, over(sm), ALU.mult).then_inc(w_made, 1)
                nd = 0
                for c, (t0, nt) in enumerate(CH):
                    n = nt * TP
                    nd += 1
                    dve.wait_ge(d_mm, nd)
                    vc.tensor_copy(wT[:, c % 2, 0:n], ps[0:1 + NE, 4 + (nd - 1) % 4, 0:n]).then_inc(d_ev, 1)
                    for q in range(2):
                        nd += 1
                        dve.wait_ge(d_mm, nd)
                        dve.wait_ge(a_ev, c * 9 + 8 + q)
                        e2 = e2_of(c)[:, q, 0:n]
                        vc.tensor_tensor(e2, e2, ps[:, 4 + (nd - 1) % 4, 0:n], ALU.mult).then_inc(d_ev, 1)
                    for t in range(t0, t0 + nt):
                        nd += 1
                        dve.wait_ge(d_mm, nd)
                        vc.tensor_tensor(agg[0:TP, t, :], ps[0:TP, 4 + (nd - 1) % 4, 0:D], h[0:TP, t, :],
                                         ALU.add).then_inc(out_made, 1)

            @block.scalar
            def _(act):
                sqrt_for(act, TP, NT, 2 * L + 2)
                for c, (t0, nt) in enumerate(CH):
                    n = nt * TP
                    act.wait_ge(y_tr, c + 1)
                    nc.scalar.copy(yT[:, 0, t0 * TP:t0 * TP + n], ps[:, 2 * (c % 2), 0:n]).then_inc(y_ev0, 1)
                for k in range(2):
                    act.wait_ge(ex_ask, k + 1)
                    nc.scalar.activation(pr[0:TP, :, :], lg[0:TP, :, :], ACT.Exp).then_inc(ex_done, 1)
                na = 0
                for c, (t0, nt) in enumerate(CH):
                    if c >= 2:
                        act.wait_ge(out_made, CH[c - 1][0])
                    for _, bias, where in units(c):
                        na += 1
                        act.wait_ge(a_mm, na)
                        nc.scalar.activation(where, ps[:, (na - 1) % 4, 0:nt * TP], ACT.Relu, bias=bias)\
                            .then_inc(a_ev, 1)

            @block.tensor
            def _(pe):
                pe.wait_ge(y_made, NT)
                for c, (t0, nt) in enumerate(CH):
                    n = nt * TP
                    if c >= 2:
                        pe.wait_ge(y_ev0, c - 1)
                        pe.wait_ge(y_ev1, c - 1)
                    for half in range(2):
                        for t in range(nt):
                            last = nc.tensor.transpose(ps[:, 2 * (c % 2) + half, t * TP:(t + 1) * TP],
                                                       agg[0:TP, t0 + t, half * 128:(half + 1) * 128],
                                                       ident[0:TP, 0:TP])
                    last.then_inc(y_tr, 1)
                    pe.wait_ge(y_ev0, c + 1)
                    pe.wait_ge(y_ev1, c + 1)
                    if c >= 2:
                        pe.wait_ge(lg_ev, c - 1)
                    for t in range(nt):
                        for k in range(2):
                            last = nc.tensor.matmul(ps[0:TP, 4 + c % 2, t * NE:(t + 1) * NE],
                                                    yT[:, k, (t0 + t) * TP:(t0 + t + 1) * TP], gW_s[:, k, :],
                                                    start=(k == 0), stop=(k == 1))
                    last.then_inc(lg_mm, 1)
                pe.wait_ge(w_made, 1)
                na, nd = 0, 0

                def bank_d():
                    nonlocal nd
                    if nd >= 4:
                        s, value = readers[nd - 4]
                        pe.wait_ge(s, value)
                    nd += 1
                    return 4 + (nd - 1) % 4

                readers = []
                for c, (t0, nt) in enumerate(CH):
                    readers += [(d_ev, 3 * c + k + 1) for k in range(3)]
                    readers += [(out_made, t + 1) for t in range(t0, t0 + nt)]
                for c, (t0, nt) in enumerate(CH):
                    n = nt * TP
                    for k, (terms, _, _) in enumerate(units(c)):
                        if k == 6:
                            pe.wait_ge(a_ev, 9 * c + 2)
                        if k == 7:
                            pe.wait_ge(a_ev, 9 * c + 6)
                        if na >= 4:
                            pe.wait_ge(a_ev, na - 3)
                        for m, (w, r) in enumerate(terms):
                            last = nc.tensor.matmul(ps[:, na % 4, 0:n], w, r, start=(m == 0),
                                                    stop=(m == len(terms) - 1))
                        last.then_inc(a_mm, 1)
                        na += 1
                        if k == 1:
                            b = bank_d()
                            for t in range(nt):
                                last = nc.tensor.transpose(ps[0:1 + NE, b, t * TP:(t + 1) * TP],
                                                           w5[0:TP, t0 + t, :], ident[0:TP, 0:TP])
                            last.then_inc(d_mm, 1)
                    pe.wait_ge(d_ev, 3 * c + 1)
                    for q in range(2):
                        b = bank_d()
                        nc.tensor.matmul(ps[:, b, 0:n], sel[:, q, :], wT[:, c % 2, 0:n], start=True, stop=True)\
                            .then_inc(d_mm, 1)
                    pe.wait_ge(a_ev, 9 * c + 7)
                    pe.wait_ge(d_ev, 3 * c + 3)
                    for t in range(nt):
                        cols = slice(t * TP, (t + 1) * TP)
                        b = bank_d()
                        terms = [(h2_all[:, c % 2, cols], sW3_s[:, :])]
                        terms += [(e2_of(c)[:, q, cols], eW3_s[:, q, :]) for q in range(2)]
                        terms += [(wT[:, c % 2, cols], b_out[:, :])]
                        for m, (w, r) in enumerate(terms):
                            last = nc.tensor.matmul(ps[0:TP, b, 0:D], w, r, start=(m == 0), stop=(m == 3))
                        last.then_inc(d_mm, 1)


_INS = ['x', 'src', 'dst', 'edge_attr_16', 'L0_gnn_ee_w1', 'L0_gnn_ee_b1', 'L0_gnn_ee_w2', 'L0_gnn_ee_b2',
        'L0_gnn_eps', 'L0_gnn_mlp_w1', 'L0_gnn_mlp_b1', 'L0_gnn_bn1_g', 'L0_gnn_bn1_b', 'L0_gnn_mlp_w2',
        'L0_gnn_mlp_b2', 'L0_gnn_bn_g', 'L0_gnn_bn_b', 'L0_ffn_sW1', 'L0_ffn_sb1', 'L0_ffn_sW2', 'L0_ffn_sb2',
        'L0_ffn_sW3', 'L0_ffn_sb3', 'L0_ffn_eW1', 'L0_ffn_eb1', 'L0_ffn_eW2', 'L0_ffn_eb2', 'L0_ffn_eW3',
        'L0_ffn_eb3', 'L0_ffn_gW', 'L0_ffn_gb']


def kernel(**inputs):
    import numpy as _np
    import concourse.bacc as _bacc
    from concourse import mybir as _mybir
    from concourse.bass_utils import run_bass_kernel_spmd as _run

    nc = _bacc.Bacc("TRN2", target_bir_lowering=False, num_devices=1)
    arrays, args = {}, []
    for name in _INS:
        a = _np.ascontiguousarray(inputs[name])
        arrays[f"in_{name}_dram"] = a
        args.append(nc.dram_tensor(f"in_{name}_dram", a.shape, _mybir.dt.from_np(a.dtype), kind="ExternalInput").ap())
    args.append(nc.dram_tensor("out_dram", (3125, 256), _mybir.dt.float32, kind="ExternalOutput").ap())
    gnn_moe_kernel(nc, *args)
    r = _run(nc, [arrays], core_ids=[0])
    return r.results[0]["out_dram"]
```

```python
import concourse.bass as bass
from concourse import mybir
from contextlib import ExitStack

F32 = mybir.dt.float32
F32R = mybir.dt.float32r
I32 = mybir.dt.int32
ALU = mybir.AluOpType
ACT = mybir.ActivationFunctionType
AX = mybir.AxisListType.X
ds = bass.ds

N, D, DE, L, E = 3125, 256, 16, 5, 53125
D2 = 2 * D
TP = 125
NT = N // TP
EC = E // TP
GS = 256
NG = (E + NT * (GS - 1)) // GS
UN = 8
NIT = NG // UN
assert NG % UN == 0 and N == NT * TP and E == EC * TP
RW = 2 + DE
SRC, DST, ATT = 0, 1, 2
EPS = 1e-5
BIG = 3.0e38
CH = [(t, min(4, NT - t)) for t in range(0, NT, 4)]
NCH = len(CH)
PAIRS = [(t, min(2, NT - t)) for t in range(0, NT, 2)]
NPAIR = len(PAIRS)
SB = 17
NSB = EC // SB
assert EC == SB * NSB and NSB % 2 == 1
TAIL = GS
Q = 4
BLK = 128 * Q
NBLK = -(-(E + TAIL) // (4 * BLK)) * 4
EP = NBLK * BLK
ATT_B = [(b, min(16, NBLK - b)) for b in range(0, NBLK, 16)]
FULL = E // BLK
FULL_P, REST = (E - FULL * BLK) // Q, E % Q
assert REST > 0
V_B1, V_G1, V_BB1, V_B2, V_G2, V_BB2, V_EPS, V_FLOOR, NV = 0, 4, 8, 12, 14, 16, 18, 19, 20
NE, EH1, EH2, SH1, SH2 = 4, 128, 64, 256, 128


class Link:

    def __init__(self, eng, sem, base=0):
        self.eng, self.sem, self.base, self.n = eng, sem, base, 0

    def __call__(self, ins):
        self.n += 1
        ins.then_inc(self.sem, 1)
        self.eng.wait_ge(self.sem, self.base + self.n)


def gnn_moe_kernel(nc, x, src, dst, edge_attr, ee_w1, ee_b1, ee_w2, ee_b2, eps, mlp_w1, mlp_b1,
                   bn1_g, bn1_b, mlp_w2, mlp_b2, bn_g, bn_b, sW1, sb1, sW2, sb2, sW3, sb3,
                   eW1, eb1, eW2, eb2, eW3, eb3, gW, gb, out):
    ctx = ExitStack()
    with ctx:
        def sb(name, shape, dt=F32):
            return ctx.enter_context(nc.sbuf_tensor(name, shape, dt))

        def sem(name):
            return ctx.enter_context(nc.semaphore(name))

        rec = nc.dram_tensor("edge_records", [E, RW], F32, kind="Internal").ap()
        ends_d = nc.dram_tensor("edge_ends", [E + TAIL, 2], F32, kind="Internal").ap()
        attr_t = nc.dram_tensor("attributes_t", [2 * DE, EP], F32, kind="Internal").ap()
        table = nc.dram_tensor("node_table", [N, D], F32, kind="Internal").ap()

        h = sb("h", [128, NT, D])
        agg = sb("agg", [128, NT, D])
        u = sb("u", [128, 4, N])
        u_flat = u[:, :, :].rearrange("p f n -> p (f n)")
        agg_flat = agg[:, :, :].rearrange("p t d -> p (t d)")
        z2 = agg_flat[:, 0:2 * N].rearrange("p (f n) -> p f n", f=2)
        node_tab = u_flat[:, 0:NT * D].rearrange("p (t d) -> p t d", d=D)
        yT = u_flat[:, 0:2 * N].rearrange("p (f n) -> p f n", f=2)
        assert len(ATT_B) == NCH
        ATT_W = NBLK * Q * DE
        att_all = u_flat[:, 0:ATT_W].rearrange("p (b q w) -> p b q w", q=Q, w=DE)
        scratch = [u_flat[0:TP, ATT_W + k * EC:ATT_W + (k + 1) * EC] for k in range(10)]
        dst_f, bucket, mask, prefix, rank, part, ones_c = scratch[:7]
        src_i, dst_i, place_i = (a.bitcast(I32) for a in scratch[7:])

        x_rest = u_flat[:, NT * D:]
        XT = (4 * N - NT * D) // D

        ident = sb("ident", [128, 128])
        iota_n = sb("iota_n", [128, TP])
        lower = sb("lower", [128, 128])
        ones = sb("ones", [128, 128])
        part_id = sb("part_id", [128, 1])
        w1_high = sb("w1_high", [128, 1])
        w1_low = sb("w1_low", [128, 1])
        vec_all = sb("vec_all", [128, L, NV])
        vec = sb("vec", [128, NV])
        upto = sb("upto", [128, NT])
        tile_part = sb("tile_part", [128, NT])
        dst_next = sb("dst_next", [128, 1], I32)
        dst_next_f = sb("dst_next_f", [128, 1])
        breaks = sb("breaks", [128, 2])
        unsorted = sb("unsorted", [1, 1], I32)
        cnt = sb("cnt", [NT, 1])
        cnt_i = sb("cnt_i", [NT, 1], I32)
        groups = sb("groups", [NT, 1])
        groups_end = sb("groups_end", [NT, 1])
        slack = sb("slack", [NT, 1])
        slack_b = sb("slack_b", [NT, 128])
        offset = sb("offset", [128, NT])
        first_edge = sb("first_edge", [1, NG], I32)
        tile_base = sb("tile_base", [128, NG])
        group_tile = sb("group_tile", [1, NG], I32)

        def carve(*shape):
            start, size = carve.at, 1
            for k in shape:
                size *= k
            carve.at = start + size
            assert carve.at <= NT * D
            letters = "abcde"[:len(shape)]
            return agg_flat[:, start:carve.at].rearrange(
                f"p ({' '.join(letters)}) -> p {' '.join(letters)}", **dict(zip(letters, shape)))

        carve.at = 0
        stage = carve(2, SB, RW)
        stage_ix = carve(2, SB).bitcast(I32)
        ends = carve(EC, 2)
        att_hl = carve(2, 4 * Q, 8 * DE)
        ended = carve(NG)[0:NT, :]
        g_iota, first_f = carve(NG), carve(NG)[0:1, :]

        KA = 4 * DE + 2
        w1_raw = sb("w1_raw", [KA, D])
        w1_s = sb("w1_s", [KA, D], F32R)
        w2_raw = sb("w2_raw", [128, 2, D])
        w2_h = sb("w2_h", [128, 2, D], F32R)
        w2_l = sb("w2_l", [128, 2, D], F32R)
        b2_all = sb("b2_all", [128, D])
        m1_raw = sb("m1_raw", [128, 2, D2])
        m1_h = sb("m1_h", [128, 2, D2], F32R)
        m1_l = sb("m1_l", [128, 2, D2], F32R)
        m2_raw = sb("m2_raw", [128, 4, D])
        m2_h = sb("m2_h", [128, 4, D], F32R)
        m2_l = sb("m2_l", [128, 4, D], F32R)

        at = sb("at", [KA, UN, GS], F32R)
        meta = sb("meta", [128, UN, 2, 2], I32)
        meta_f = meta[:, :, :, :].bitcast(F32)
        e_sb = sb("e_sb", [128, 4, 2, D])
        ring = sb("ring", [128, 4, 4 * GS], F32R)
        hid_h, hid_l, msg_h, msg_l = (ring[:, k, :].rearrange("p (s a c) -> p s a c", s=2, a=2) for k in range(4))
        w1_h, w1_l = (ring[0:KA, 0, k * D:(k + 1) * D] for k in range(2))
        pick = sb("pick", [128, 2, 2, TP + 1], F32R)

        z_h, z_l = (ring[:, 2 * k:2 * k + 2, :].rearrange("p a c -> p (a c)")[:, 0:2000]
                    .rearrange("p (s a c) -> p s a c", s=2, a=2) for k in range(2))
        v_h = sb("v_h", [128, 2, 4, 500], F32R)
        v_l = sb("v_l", [128, 2, 4, 500], F32R)
        st1 = sb("st1", [128, 4, NCH, 6])
        st2 = sb("st2", [128, 2, NCH, 6])
        mv = sb("mv", [128, NT, 2])
        st_ln = st1[:, :, :, :].rearrange("p f c s -> p (f c s)")[:, 0:NT * 6].rearrange("p (t s) -> p t s", s=6)
        r_a, r_b, r_y, r_t, r_s, r_o = (sb(f"r{k}", [128, NT]) for k in range(6))

        def in_u(start, *shape):
            size = 1
            for k in shape:
                size *= k
            in_u.end = start + size
            assert in_u.end <= 4 * N
            letters = "abc"[:len(shape)]
            return u_flat[:, start:in_u.end].rearrange(
                f"p ({' '.join(letters)}) -> p {' '.join(letters)}", **dict(zip(letters, shape)))

        sW1_s = in_u(9400, 2, SH1)
        sW2_s = in_u(in_u.end, 2, SH2)
        sW3_s = in_u(in_u.end, D)
        eW1_s = in_u(in_u.end, NE, 2, EH1)
        eW2_s = in_u(in_u.end, NE, 2 * EH2)
        eW3_s = in_u(in_u.end, 2, D)
        gW_s = sb("gW_s", [128, 2, NE])
        gb_s = sb("gb_s", [128, NE])
        sb1_s = sb("sb1_s", [128, 2])
        sb2_s = sb("sb2_s", [128, 1])
        eb1_s = sb("eb1_s", [128, NE])
        eb2_s = sb("eb2_s", [128, 2])
        b_out = m2_raw[0:1 + NE, 0, :]
        gate_mem = w2_raw[:, :, :].rearrange("p k d -> p (k d)")
        lg, pr = (gate_mem[:, k * NT * NE:(k + 1) * NT * NE].rearrange("p (t e) -> p t e", e=NE) for k in range(2))
        rk = gate_mem[:, 2 * NT * NE:3 * NT * NE].rearrange("p (e t) -> p e t", e=NE)
        w5 = gate_mem[:, 3 * NT * NE:3 * NT * NE + NT * (1 + NE)].rearrange("p (t e) -> p t e", e=1 + NE)
        cmp = gate_mem[:, 512 - NT:]
        sel = sb("sel", [1 + NE, 2, 128])
        wT = m1_raw[0:1 + NE, :, 0:500]

        x_parts = [(x_rest[0:TP, 0:XT * D].rearrange("p (t d) -> p t d", d=D), slice(0, XT)),
                   (e_sb[0:TP, :, :, :].rearrange("p s a c -> p (s a c)")[:, 0:(NT - XT) * D]
                    .rearrange("p (t d) -> p t d", d=D), slice(XT, NT))]
        att_t = [e_sb[:, :, :, :].rearrange("p a b c -> p (a b c)"),
                 v_h[:, :, :, :].rearrange("p a b c -> p (a b c)")]
        pad = u_flat[0:1, ATT_W + 10 * EC:ATT_W + 10 * EC + 2 * TAIL].rearrange("p (n w) -> p n w", w=2)

        ps = ctx.enter_context(nc.psum_tensor("ps", [128, 8, 512], F32))

        edges_in, x_in, vec_in, moe_in = sem("edges_in"), sem("x_in"), sem("vec_in"), sem("moe_in")
        consts, pool_own = sem("consts"), sem("pool_own")
        zeros_made, parts_made, parts_summed = sem("zeros_made"), sem("parts_made"), sem("parts_summed")
        flag_made, groups_made, groups_summed = sem("flag_made"), sem("groups_made"), sem("groups_summed")
        ended_made, ended_summed = sem("ended_made"), sem("ended_summed")
        ends_made, ends_out, places_made = sem("ends_made"), sem("ends_out"), sem("places_made")
        pool_pace, dve_pace, sp_pace = sem("pool_pace"), sem("dve_pace"), sem("sp_pace")
        staged, d_rank = sem("staged"), sem("d_rank")
        att_here, att_again = sem("att_here"), sem("att_again")
        staged_att = [sem(f"staged_att{b}") for b in range(2)]
        scattered = [sem(f"scattered{b}") for b in range(2)]
        d_pre, d_lay, d_moe = sem("d_pre"), sem("d_lay"), sem("d_moe")
        att_loaded = [sem(f"att_loaded{k}") for k in range(len(ATT_B))]
        att_high, att_low, att_tr, att_ev = sem("att_high"), sem("att_low"), sem("att_tr"), sem("att_ev")
        att_out = [sem(f"att_out{b}") for b in range(2)]
        sqrt_ask, sqrt_done = sem("sqrt_ask"), sem("sqrt_done")
        agg_set = sem("agg_set")
        tab_made = [sem(f"tab_made{c}") for c in range(NCH)]
        h_rows, tab_out = sem("h_rows"), sem("tab_out")
        w_in, w_high, w_ready = sem("w_in"), sem("w_high"), sem("w_ready")
        m_in, m1_high, m2_high, m1_low, m2_low = (sem("m_in"), sem("m1_high"), sem("m2_high"),
                                                  sem("m1_low"), sem("m2_low"))
        at_in = [sem(f"at_in{b}") for b in range(UN)]
        meta_in = [sem(f"meta_in{b}") for b in range(UN)]
        gathered = [sem(f"gathered{b}") for b in range(4)]
        mm1, mm2, mm3 = sem("mm1"), sem("mm2"), sem("mm3")
        hid_high, hid_low, e_out = sem("hid_high"), sem("hid_low"), sem("e_out")
        msg_high, msg_low, picked, added = sem("msg_high"), sem("msg_low"), sem("picked"), sem("added")
        z_tr, z_high, z_low = sem("z_tr"), sem("z_high"), sem("z_low")
        u_mm, u_ev, bn1_ready = sem("u_mm"), sem("u_ev"), sem("bn1_ready")
        v_high, v_high_d, v_low = sem("v_high"), sem("v_high_d"), sem("v_low")
        v_made, z2_mm, z2_ev, bn2_ready = sem("v_made"), sem("z2_mm"), sem("z2_ev"), sem("bn2_ready")
        zn_made, zn_tr = sem("zn_made"), sem("zn_tr")
        xr_in, y_made, y_tr, y_ev0, y_ev1 = sem("xr_in"), sem("y_made"), sem("y_tr"), sem("y_ev0"), sem("y_ev1")
        lg_mm, lg_ev, ex_ask, ex_done, w_made = (sem("lg_mm"), sem("lg_ev"), sem("ex_ask"),
                                                 sem("ex_done"), sem("w_made"))
        a_mm, a_ev, d_mm, d_ev = sem("a_mm"), sem("a_ev"), sem("d_mm"), sem("d_ev")
        small_in = sem("small_in")
        x_added, moe_here = sem("x_added"), sem("moe_here")
        out_made, out_done = sem("out_made"), sem("out_done")

        def rsqrt(link, dve, var, rows, n, asked, c0=0):
            a, b, y, t = (r[0:rows, c0:c0 + n] for r in (r_a, r_b, r_y, r_t))
            link(nc.vector.tensor_scalar(a, var, EPS, None, ALU.add))
            nc.vector.reciprocal(b, a).then_inc(sqrt_ask, 1)
            dve.wait_ge(sqrt_done, asked)
            link(nc.vector.tensor_tensor(t, y, y, ALU.mult))
            link(nc.vector.tensor_tensor(t, t, a, ALU.mult))
            link(nc.vector.tensor_scalar(t, t, -0.5, 1.5, ALU.mult, ALU.add))
            link(nc.vector.tensor_tensor(y, y, t, ALU.mult))
            return y

        def sqrt_for(act, rows, n, asked, c0=0):
            act.wait_ge(sqrt_ask, asked)
            nc.scalar.activation(r_y[0:rows, c0:c0 + n], r_b[0:rows, c0:c0 + n], ACT.Sqrt).then_inc(sqrt_done, 1)

        def norm_stats(link, a, t0, nt):
            for t in range(t0, t0 + nt):
                nc.vector.bn_stats(st_ln[0:TP, t, :], a[0:TP, t, :]).then_inc(link.sem, 1)
            link.n += nt

        def norm_scales(link, dve, t0, nt, asked):
            dve.wait_ge(link.sem, link.base + link.n)
            for t in range(t0, t0 + nt):
                nc.vector.bn_aggr(mv[0:TP, t, :], st_ln[0:TP, t, :]).then_inc(link.sem, 1)
            link.n += nt
            dve.wait_ge(link.sem, link.base + link.n)
            rsqrt(link, dve, mv[0:TP, t0:t0 + nt, 1], TP, nt, asked, t0)

        def norm_apply(a, o, t0, nt, made):
            for t in range(t0, t0 + nt):
                nc.vector.tensor_scalar(o[0:TP, t, :], a[0:TP, t, :], mv[0:TP, t, 0:1], r_y[0:TP, t:t + 1],
                                        ALU.subtract, ALU.mult).then_inc(made, 1)

        ctx.enter_context(nc.allow_non_contiguous_dma(reason="small vectors and slot records"))

        def is_unsorted(eng):
            eng.wait_ge(flag_made, 1)
            return eng.value_load(unsorted[0:1, 0:1], min_val=0, max_val=E) > 0

        def load_attributes(sp, a, loaded):
            for k, (b0, nb) in enumerate(ATT_B):
                whole = min(b0 + nb, FULL)
                if a is edge_attr:
                    sp.dma_start(att_all[:, b0:whole, :, :].rearrange("p b q w -> p b (q w)"),
                                 a[b0 * BLK:whole * BLK, :].rearrange("(b p q) w -> p b (q w)", p=128, q=Q))\
                        .then_inc(loaded(k), 16)
                else:
                    for b in range(b0, whole):
                        sp.dma_start(att_all[:, b, :, :], a[b * BLK:(b + 1) * BLK, :]
                                     .rearrange("(p q) w -> p q w", q=Q)).then_inc(loaded(k), 16)
                if b0 <= FULL < b0 + nb:
                    sp.dma_start(att_all[0:FULL_P, FULL, :, :], a[FULL * BLK:FULL * BLK + FULL_P * Q, :]
                                 .rearrange("(p q) w -> p q w", q=Q)).then_inc(loaded(k), 16)
                    sp.dma_start(att_all[FULL_P:FULL_P + 1, FULL, 0:REST, :], a[E - REST:E, :].unsqueeze(0))\
                        .then_inc(loaded(k), 16)
                    break

        def loads_of(k):
            b0, nb = ATT_B[k]
            return (1 if b0 < FULL else 0) + (2 if b0 <= FULL < b0 + nb else 0)

        def raw_of(k):
            b0, nb = ATT_B[k]
            return att_all[:, b0:b0 + nb, :, :].rearrange("p (h r) q w -> p h (r q) w", h=4)

        def parts_of(k, low):
            return att_hl[:, k % 2, 0:ATT_B[k][1] // 4 * Q, :]\
                .rearrange("p k (h a w) -> p a h k w", h=4, a=2)[:, low, :, :, :]

        TAB_VECTOR = (NCH // 2, NCH - 1)

        def make_table(engine, c):
            t0, nt = CH[c]
            engine.tensor_tensor(node_tab[0:TP, t0:t0 + nt, :], h[0:TP, t0:t0 + nt, :],
                                 b2_all[0:TP, :].unsqueeze(1).to_broadcast([TP, nt, D]), ALU.add)\
                .then_inc(tab_made[c], 1)

        def store_table(sp, l, c):
            t0, nt = CH[c]
            sp.wait_ge(tab_made[c], l + 1)
            sp.dma_start(table.rearrange("(t p) d -> p t d", p=TP)[:, t0:t0 + nt, :],
                         node_tab[0:TP, t0:t0 + nt, :]).then_inc(tab_out, 16)

        def load_slots(sp, g, b):
            first = sp.value_load(first_edge[0:1, ds(g, 1)], min_val=0, max_val=E)
            sp.dma_start(at[0:4 * DE, b, :].bitcast(F32),
                         attr_t[:, ds(first, GS)].unsqueeze(0).to_broadcast([2, 2 * DE, GS]))\
                .then_inc(at_in[b], 16)
            sp.dma_start(meta[:, b, :, :].bitcast(F32), ends_d[ds(first, GS), :]
                         .rearrange("(j p) w -> p j w", j=2)).then_inc(meta_in[b], 16)

        M_LOADS, W_LOADS = 6, 8
        EARLY = 3

        def load_node_weights(sp, l):
            for k in range(2):
                sp.dma_start(m1_raw[:, k, :], mlp_w1[ds(l, 1), k * 128:(k + 1) * 128, :]
                             .rearrange("a p f -> (a p) f")).then_inc(m_in, 16)
            for k in range(4):
                sp.dma_start(m2_raw[:, k, :], mlp_w2[ds(l, 1), k * 128:(k + 1) * 128, :]
                             .rearrange("a p f -> (a p) f")).then_inc(m_in, 16)

        VEC_IN = 16 * (4 * 3 + 2 * 3 + 1)

        def load_edge_weights(sp, l):
            for k in range(4):
                sp.dma_start(w1_raw[k * DE:(k + 1) * DE, :],
                             ee_w1[ds(l, 1), :, :].rearrange("a k d -> (a k) d")).then_inc(w_in, 16)
            for k in range(2):
                sp.dma_start(w1_raw[4 * DE + k:4 * DE + k + 1, :], ee_b1[ds(l, 1), :]).then_inc(w_in, 16)
            sp.dma_start(w2_raw[:, :, :], ee_w2[ds(l, 1), :, :].rearrange("a (k p) d -> p (a k) d", p=128))\
                .then_inc(w_in, 16)
            sp.dma_start(b2_all[:, :], ee_b2[ds(l, 1), :].to_broadcast([128, D])).then_inc(w_in, 16)

        def edge_weights_high(act, l):
            act.wait_ge(w_in, (l + 1) * 16 * W_LOADS)
            nc.scalar.copy(w1_h[:, :], w1_raw[:, :]).then_inc(w_high, 1)
            nc.scalar.copy(w2_h[:, :, :], w2_raw[:, :, :]).then_inc(w_high, 1)

        def node_weights_high(act, l, first=True, second=True):
            act.wait_ge(m_in, (l + 1) * 16 * M_LOADS)
            if first:
                nc.scalar.copy(m1_h[:, :, :], m1_raw[:, :, :]).then_inc(m1_high, 1)
            if second:
                nc.scalar.copy(m2_h[:, :, :], m2_raw[:, :, :]).then_inc(m2_high, 1)

        def low_of(dve, low, raw, high, ready, value, made):
            dve.wait_ge(ready, value)
            nc.vector.tensor_tensor(low[:, :, :], raw[:, :, :], high[:, :, :].bitcast(F32), ALU.subtract)\
                .then_inc(made, 1)

        def edge_weights_low(link, dve, l):
            vc = nc.vector
            dve.wait_ge(w_high, (l + 1) * 2)
            link(vc.tensor_tensor(w1_l[:, :], w1_raw[:, :], w1_h[:, :].bitcast(F32), ALU.subtract))
            link(vc.tensor_scalar(w1_raw[:, :], w1_h[:, :].bitcast(F32), w1_high[0:KA, :], None, ALU.mult))
            link(vc.scalar_tensor_tensor(out=w1_s[:, :], in0=w1_l[:, :].bitcast(F32), scalar=w1_low[0:KA, :],
                                         in1=w1_raw[:, :], op0=ALU.mult, op1=ALU.add))
            vc.tensor_tensor(w2_l[:, :, :], w2_raw[:, :, :], w2_h[:, :, :].bitcast(F32),
                             ALU.subtract).then_inc(w_ready, 1)

        with nc.Block() as block:
            @block.sync
            def _(sp):
                sp.dma_start(dst_i, dst.rearrange("(p c) -> p c", p=TP)).then_inc(edges_in, 16)
                sp.dma_start(dst_next[0:TP - 1, :], dst[EC:E].rearrange("(p c) -> p c", c=EC)[:, 0:1])\
                    .then_inc(edges_in, 16)
                sp.dma_start(src_i, src.rearrange("(p c) -> p c", p=TP)).then_inc(edges_in, 16)
                sp.wait_ge(zeros_made, 2)
                load_attributes(sp, edge_attr, lambda k: att_loaded[k])
                sp.dma_start(h[0:TP, :, :], x.rearrange("(t p) d -> p t d", p=TP)).then_inc(x_in, 16)
                load_edge_weights(sp, 0)
                load_node_weights(sp, 0)
                for col, k, a in ((V_B1, 4, mlp_b1), (V_G1, 4, bn1_g), (V_BB1, 4, bn1_b),
                                  (V_B2, 2, mlp_b2), (V_G2, 2, bn_g), (V_BB2, 2, bn_b)):
                    for f in range(k):
                        sp.dma_start(vec_all[:, :, col + f],
                                     a[:, f * 128:(f + 1) * 128].rearrange("l p -> p l")).then_inc(vec_in, 16)
                sp.dma_start(vec_all[:, :, V_EPS], eps.unsqueeze(0).to_broadcast([128, L])).then_inc(vec_in, 16)
                small = [(gW_s[:, :, :], gW.rearrange("(k p) e -> p k e", p=128)),
                         (gb_s[:, :], gb.unsqueeze(0).to_broadcast([128, NE])),
                         (sb1_s[:, :], sb1.rearrange("(f p) -> p f", p=128)),
                         (sb2_s[:, :], sb2.rearrange("(f p) -> p f", p=128)),
                         (eb1_s[:, :], eb1.rearrange("e p -> p e"))]
                small += [(eb2_s[(e % 2) * EH2:(e % 2 + 1) * EH2, e // 2:e // 2 + 1], eb2[e, :].unsqueeze(1))
                          for e in range(NE)]
                for o, i in small:
                    sp.dma_start(o, i).then_inc(small_in, 16)
                branch = is_unsorted(sp)
                with sp.If(branch):
                    att_p = edge_attr.rearrange("(p c) w -> p c w", p=TP)

                    def stage_att(k, b):
                        sp.dma_start(stage[0:TP, b, :, ATT:RW], att_p[:, ds(k * SB, SB), :])\
                            .then_inc(staged_att[b], 16)

                    stage_att(0, 0)
                    stage_att(1, 1)
                    with sp.Fori(1, NSB // 2) as i:
                        for b in range(2):
                            sp.wait_ge(scattered[b], i * 16 * SB)
                            stage_att(2 * i + b, b)
                    sp.wait_ge(scattered[0], NSB // 2 * 16 * SB)
                    stage_att(NSB - 1, 0)
                    sp.wait_ge(scattered[0], 16 * SB * ((NSB + 1) // 2))
                    sp.wait_ge(scattered[1], 16 * SB * (NSB // 2))
                    sp.dma_start(ends_d[0:E, :], rec[:, 0:ATT]).then_inc(ends_out, 16)
                    for k in range(len(ATT_B)):
                        sp.wait_ge(att_loaded[k], 16 * loads_of(k))
                    load_attributes(sp, rec[:, ATT:RW], lambda k: att_again)
                    sp.wait_ge(att_again, 16 * (FULL + 2))
                for k in range(len(ATT_B) + 2):
                    if k < len(ATT_B):
                        sp.wait_ge(att_loaded[k], 16 * loads_of(k))
                        sp.sem_inc(att_here)
                    if k >= 2:
                        b, (b0, nb) = k % 2, ATT_B[k - 2]
                        sp.wait_ge(att_ev, k - 1)
                        for quarter in range(4):
                            start, width = (b0 + quarter * nb // 4) * BLK, nb // 4 * BLK
                            sp.dma_start(attr_t[:, start:start + width],
                                         att_t[b][quarter * 32:(quarter + 1) * 32, 0:width].bitcast(F32))\
                                .then_inc(att_out[b], 16)
                for b in range(2):
                    sp.wait_ge(att_out[b], 64 * ((len(ATT_B) + 1 - b) // 2))
                sp.wait_ge(ends_out, 32)
                sp.sem_inc(sp_pace)
                for b in range(EARLY):
                    load_slots(sp, b, b)
                for c in range(NCH):
                    store_table(sp, 0, c)
                sp.wait_ge(small_in, 16 * len(small))
                sp.wait_ge(vec_in, VEC_IN)

            @block.gpsimd
            def _(pool):
                gp = nc.gpsimd
                gp.memset(lower[:, :], 1.0).then_inc(pool_own, 1)
                gp.memset(ones[:, :], 1.0).then_inc(pool_own, 1)
                gp.memset(ident[:, :], 0.0).then_inc(pool_own, 1)
                gp.memset(sel[:, :, :], 0.0).then_inc(pool_own, 1)
                pool.wait_ge(pool_own, 4)
                gp.affine_select(out=ident[:, :], in_=ident[:, :], compare_op=ALU.not_equal, fill=1.0,
                                 base=0, pattern=[[-1, 128]], channel_multiplier=1).then_inc(consts, 1)
                gp.affine_select(out=lower[:, :], in_=lower[:, :], compare_op=ALU.is_gt, fill=0.0,
                                 base=0, pattern=[[1, 128]], channel_multiplier=-1).then_inc(consts, 1)
                gp.affine_select(out=sel[:, :, :].rearrange("p q (r c) -> p q r c", r=2),
                                 in_=sel[:, :, :].rearrange("p q (r c) -> p q r c", r=2),
                                 compare_op=ALU.not_equal, fill=1.0, base=1,
                                 pattern=[[2, 2], [1, 2], [0, EH2]], channel_multiplier=-1).then_inc(consts, 1)
                gp.iota(iota_n[:, :], pattern=[[1, TP]], base=0, channel_multiplier=0,
                        allow_small_or_imprecise_dtypes=True).then_inc(consts, 1)
                gp.iota(part_id[:, :], pattern=[[0, 1]], base=0, channel_multiplier=1,
                        allow_small_or_imprecise_dtypes=True).then_inc(consts, 1)
                gp.iota(g_iota[:, :], pattern=[[1, NG]], base=0, channel_multiplier=0,
                        allow_small_or_imprecise_dtypes=True).then_inc(consts, 1)
                branch = is_unsorted(pool)
                with pool.If(branch):
                    def scatter(k, b, turn):
                        pool.wait_ge(staged, 3 * (k + 1))
                        pool.wait_ge(staged_att[b], 16 * turn)
                        pool.sem_inc(pool_pace)
                        for c in range(SB):
                            gp.indirect_dma_start(
                                rec, bass.IndirectOffsetOnAxis(ap=stage_ix[0:TP, b, c:c + 1], axis=0),
                                stage[0:TP, b, c, :], None).then_inc(scattered[b], 16)

                    with pool.Fori(0, NSB // 2) as i:
                        scatter(2 * i, 0, i + 1)
                        scatter(2 * i + 1, 1, i + 1)
                    scatter(NSB - 1, 0, NSB // 2 + 1)
                for c in range(NCH):
                    if c not in TAB_VECTOR:
                        pool.wait_ge(w_in, 16 * W_LOADS)
                        pool.wait_ge(h_rows, sum(CH[c]))
                        make_table(gp, c)

            @block.scalar
            def _(act):
                act.wait_ge(zeros_made, 2)
                act.dma_start(ends_d[E:E + TAIL, :].unsqueeze(0), pad).then_inc(ends_out, 16)
                branch = is_unsorted(act)
                with act.If(branch):
                    act.wait_ge(places_made, 1)

                    def stage_block(k, b):
                        cols = ds(k * SB, SB)
                        o = stage[0:TP, b, :, :]
                        nc.scalar.copy(o[:, :, DST], dst_f[:, cols]).then_inc(staged, 1)
                        nc.scalar.copy(o[:, :, SRC].bitcast(I32), src_i[:, cols]).then_inc(staged, 1)
                        nc.scalar.copy(stage_ix[0:TP, b, :], place_i[:, cols]).then_inc(staged, 1)

                    stage_block(0, 0)
                    stage_block(1, 1)
                    with act.Fori(1, NSB // 2) as i:
                        for b in range(2):
                            act.wait_ge(scattered[b], i * 16 * SB)
                            stage_block(2 * i + b, b)
                    act.wait_ge(scattered[0], NSB // 2 * 16 * SB)
                    stage_block(NSB - 1, 0)
                with act.Else():
                    act.wait_ge(ends_made, 2)
                    act.dma_start(ends_d[0:E, :].rearrange("(p c) w -> p c w", p=TP), ends[0:TP, :, :])\
                        .then_inc(ends_out, 16)

                def high_part(k):
                    b0, nb = ATT_B[k]
                    act.wait_ge(att_here, k + 1)
                    if k >= 2:
                        act.wait_ge(att_tr, k - 1)
                    nc.scalar.copy(parts_of(k, 0).bitcast(F32R), raw_of(k)).then_inc(att_high, 1)

                def evacuate(k):
                    b, (b0, nb) = k % 2, ATT_B[k]
                    act.wait_ge(att_tr, k + 1)
                    if k >= 2:
                        act.wait_ge(att_out[b], k // 2 * 64)
                    nc.scalar.copy(att_t[b][:, 0:nb // 4 * BLK].rearrange("p (r c q) -> p r c q", c=128, q=Q),
                                   ps[:, 4 * b:4 * b + nb // 4, :].rearrange("p r (q c) -> p r c q", q=Q))\
                        .then_inc(att_ev, 1)

                high_part(0)
                for k in range(len(ATT_B)):
                    if k + 1 < len(ATT_B):
                        high_part(k + 1)
                    evacuate(k)
                sqrt_for(act, TP, NT, 1)
                edge_weights_high(act, 0)
                node_weights_high(act, 0)

            @block.vector
            def _(dve):
                vc = nc.vector
                link = Link(dve, d_pre)
                vc.memset(att_all[:, FULL:NBLK, :, :], 0.0).then_inc(zeros_made, 1)
                link(vc.memset(pad[:, :, SRC], 0.0))
                vc.memset(pad[:, :, DST], float(2 * N)).then_inc(zeros_made, 1)
                vc.memset(at[4 * DE:KA, :, :].bitcast(F32), 1.0).then_inc(d_pre, 1)
                vc.memset(breaks[:, :], 0.0).then_inc(d_pre, 1)
                vc.memset(tile_part[:, :], 0.0).then_inc(d_pre, 1)
                link.n += 3
                dve.wait_ge(d_pre, link.n)
                dve.wait_ge(edges_in, 48)
                vc.tensor_copy(dst_next_f[0:TP - 1, :], dst_next[0:TP - 1, :]).then_inc(d_pre, 1)
                link.n += 1
                link(vc.tensor_copy(dst_f, dst_i))
                link(vc.tensor_tensor(bucket[:, 0:EC - 1], dst_f[:, 0:EC - 1], dst_f[:, 1:EC], ALU.is_gt))
                vc.tensor_reduce(breaks[0:TP, 0:1], bucket[:, 0:EC - 1], AX, ALU.add).then_inc(d_pre, 1)
                vc.tensor_tensor(breaks[0:TP - 1, 1:2], dst_f[0:TP - 1, EC - 1:EC], dst_next_f[0:TP - 1, :],
                                 ALU.is_gt).then_inc(d_pre, 1)
                link.n += 2
                for b in range(NT):
                    m = (mask, prefix)[b % 2]
                    dve.wait_ge(d_pre, link.n - 1)
                    link.n += 1
                    vc.tensor_scalar(m, dst_f, float((b + 1) * TP), 0.0, ALU.is_lt, ALU.add,
                                     accum_out=upto[0:TP, b:b + 1]).then_inc(d_pre, 1)
                dve.wait_ge(d_pre, link.n)
                link(vc.tensor_tensor(breaks[:, 0:1], breaks[:, 0:1], breaks[:, 1:2], ALU.add))
                vc.tensor_copy(tile_part[0:TP, 0:1], upto[0:TP, 0:1]).then_inc(parts_made, 1)
                vc.tensor_tensor(tile_part[0:TP, 1:NT], upto[0:TP, 1:NT], upto[0:TP, 0:NT - 1],
                                 ALU.subtract).then_inc(parts_made, 1)
                vc.tensor_copy(ends[0:TP, :, DST], dst_f).then_inc(ends_made, 1)
                vc.tensor_copy(ends[0:TP, :, SRC].bitcast(I32), src_i).then_inc(ends_made, 1)
                dve.wait_ge(parts_summed, 1)
                vc.tensor_copy(unsorted[:, :], ps[0:1, 1, 0:1]).then_inc(flag_made, 1)
                link(vc.tensor_copy(cnt[:, :], ps[0:NT, 0, 0:1]))
                link(vc.tensor_scalar(cnt_i[:, :], cnt[:, :], float(GS - 1), None, ALU.add))
                link(vc.tensor_scalar(cnt_i[:, :], cnt_i[:, :], GS.bit_length() - 1, None,
                                      ALU.logical_shift_right))
                vc.tensor_copy(groups[:, :], cnt_i[:, :]).then_inc(groups_made, 1)
                dve.wait_ge(groups_made, 1)
                link(vc.scalar_tensor_tensor(out=slack[:, :], in0=groups[:, :], scalar=-float(GS), in1=cnt[:, :],
                                             op0=ALU.mult, op1=ALU.add))
                link(vc.tensor_scalar(slack_b[:, :], ones[0:NT, :], slack[:, 0:1], None, ALU.mult))
                dve.wait_ge(groups_summed, 1)
                link(vc.tensor_tensor(groups_end[:, :], groups[:, :], ps[0:NT, 3, 0:1], ALU.add))
                vc.tensor_scalar(ended[:, :], g_iota[0:NT, :], groups_end[:, 0:1], None, ALU.is_ge)\
                    .then_inc(ended_made, 1)
                dve.wait_ge(ended_summed, 1)
                link(vc.scalar_tensor_tensor(out=first_f[:, :], in0=g_iota[0:1, :], scalar=float(GS),
                                             in1=ps[0:1, 4, 0:NG], op0=ALU.mult, op1=ALU.add))
                link(vc.tensor_scalar(first_edge[:, :], first_f[:, :], float(E), None, ALU.min))
                link(vc.tensor_scalar(group_tile[:, :], ps[0:1, 5, 0:NG], float(NT - 1), None, ALU.min))
                link(vc.tensor_scalar(tile_base[:, :], ps[:, 5, 0:NG], float(NT - 1), -float(TP), ALU.min, ALU.mult))
                link(vc.tensor_scalar(w1_low[:, :], part_id[:, :], float(4 * DE), None, ALU.is_equal))
                link(vc.tensor_scalar(w1_high[:, :], part_id[:, :], float(2 * DE), None, ALU.is_lt))
                link(vc.tensor_tensor(w1_high[:, :], w1_high[:, :], w1_low[:, :], ALU.add))
                link(vc.tensor_scalar(w1_low[:, :], w1_high[:, :], -1.0, 1.0, ALU.mult, ALU.add))
                branch = is_unsorted(dve)
                with dve.If(branch):
                    chain = Link(dve, d_rank)
                    chain(vc.memset(ones_c, 1.0))
                    chain(vc.memset(bucket, 0.0))
                    chain(vc.memset(rank, 0.0))
                    for b in range(1, NT):
                        chain(vc.scalar_tensor_tensor(out=bucket, in0=dst_f, scalar=float(b * TP), in1=bucket,
                                                      op0=ALU.is_ge, op1=ALU.add))
                    chain(vc.memset(offset[:, :], -1.0))
                    chain(vc.tensor_tensor(offset[0:TP, :], offset[0:TP, :], ps[0:TP, 2, 0:NT], ALU.add))
                    chain(vc.tensor_tensor(offset[0:TP, 1:NT], offset[0:TP, 1:NT], ps[0:TP, 6, 0:NT - 1], ALU.add))
                    for b in range(NT):
                        chain(vc.tensor_scalar(mask, bucket, float(b), None, ALU.is_equal))
                        chain(vc.tensor_tensor_scan(prefix, ones_c, mask, 0.0, ALU.mult, ALU.add))
                        chain(vc.tensor_scalar(prefix, prefix, offset[0:TP, b:b + 1], None, ALU.add))
                        chain(vc.tensor_tensor(part, mask, prefix, ALU.mult))
                        chain(vc.tensor_tensor(rank, rank, part, ALU.add))
                    vc.tensor_copy(place_i, rank).then_inc(places_made, 1)

                def low_parts(k):
                    dve.wait_ge(att_high, k + 1)
                    vc.tensor_tensor(parts_of(k, 1), raw_of(k), parts_of(k, 0), ALU.subtract).then_inc(att_low, 1)

                def first_table(c):
                    norm_apply(h, h, *CH[c], h_rows)
                    if c in TAB_VECTOR:
                        dve.wait_ge(w_in, 16 * W_LOADS)
                        dve.wait_ge(h_rows, sum(CH[c]))
                        make_table(vc, c)

                for k in range(len(ATT_B)):
                    low_parts(k)
                    if k == 0:
                        dve.wait_ge(x_in, 16)
                    norm_stats(link, h, *CH[k])
                norm_scales(link, dve, 0, NT, 1)
                for c in range(NCH):
                    first_table(c)
                edge_weights_low(link, dve, 0)
                low_of(dve, m1_l, m1_raw, m1_h, m1_high, 1, m1_low)
                dve.wait_ge(vec_in, VEC_IN)
                link(vc.tensor_scalar(vec_all[:, :, V_EPS], vec_all[:, :, V_EPS], 1.0, None, ALU.add))
                link(vc.memset(vec_all[:, :, V_FLOOR], 0.0))
                link(vc.memset(vec_all[:, L - 1:L, V_FLOOR], -BIG))

            @block.tensor
            def _(pe):
                pe.wait_ge(parts_made, 2)
                pe.wait_ge(consts, 6)
                nc.tensor.matmul(ps[0:NT, 0, 0:1], tile_part[0:TP, :], ones[0:TP, 0:1], start=True, stop=True)
                nc.tensor.matmul(ps[0:1, 1, 0:1], breaks[:, 0:1], ones[:, 0:1], start=True, stop=True)
                nc.tensor.matmul(ps[:, 2, 0:NT], lower[:, :], tile_part[:, :], start=True, stop=True)
                nc.tensor.matmul(ps[:, 6, 0:NT], ones[0:TP, :], upto[0:TP, :], start=True, stop=True)\
                    .then_inc(parts_summed, 1)
                pe.wait_ge(groups_made, 1)
                nc.tensor.matmul(ps[0:NT, 3, 0:1], lower[0:NT, 0:NT], groups[:, :], start=True, stop=True)\
                    .then_inc(groups_summed, 1)
                pe.wait_ge(ended_made, 1)
                nc.tensor.matmul(ps[:, 4, 0:NG], slack_b[:, :], ended[:, :], start=True, stop=True)
                nc.tensor.matmul(ps[:, 5, 0:NG], ones[0:NT, :], ended[:, :], start=True, stop=True)\
                    .then_inc(ended_summed, 1)

                for k, (b0, nb) in enumerate(ATT_B):
                    b = k % 2
                    pe.wait_ge(att_low, k + 1)
                    if k >= 2:
                        pe.wait_ge(att_ev, k - 1)
                    for r in range(nb // 4):
                        for q in range(Q):
                            last = nc.tensor.transpose(ps[:, 4 * b + r, q * 128:(q + 1) * 128],
                                                       att_hl[:, b, r * Q + q, :], ident[:, :])
                    last.then_inc(att_tr, 1)

        def even(n):
            return n + n % 2

        def groups_loop(eng, step):
            for b in range(UN):
                step(b, 0, b)
            with eng.Fori(1, NIT - 1) as i:
                for b in range(UN):
                    step(i * UN + b, i, b)
            for b in range(UN):
                step((NIT - 1) * UN + b, NIT - 1, b)

        def is_past(g, k):
            return not isinstance(g, int) or g >= k

        def has(g, k):
            return not isinstance(g, int) or g + k < NG

        LAG, LAG_A = 4, 5
        GATHER_LAG = 3
        IDLE_PRODUCTS = 24

        with nc.Block() as block:
            @block.sync
            def _(sp):
                for b in range(EARLY, UN):
                    load_slots(sp, b, b)
                with sp.Fori(0, L) as l:
                    with sp.Fori(1, NIT) as i:
                        for b in range(UN):
                            g = i * UN + b
                            sp.wait_ge(mm1, l * NG + g - (UN - 1))
                            sp.wait_ge(picked, l * NG + g - (UN - 1))
                            sp.wait_ge(msg_high, l * NG + g - (UN - 1))
                            sp.sem_inc(sp_pace)
                            load_slots(sp, g, b)
                    sp.wait_ge(w_ready, l + 1)
                    sp.sem_inc(sp_pace)
                    load_edge_weights(sp, (l + 1) % L)
                    sp.wait_ge(m1_low, l + 1)
                    sp.wait_ge(m2_low, l + 1)
                    sp.sem_inc(sp_pace)
                    load_node_weights(sp, (l + 1) % L)
                    sp.wait_ge(mm1, (l + 1) * NG)
                    sp.wait_ge(picked, (l + 1) * NG)
                    sp.wait_ge(msg_high, (l + 1) * NG)
                    sp.sem_inc(sp_pace)
                    for b in range(UN):
                        load_slots(sp, b, b)
                    with sp.If(l < L - 1):
                        for c in range(NCH):
                            store_table(sp, l + 1, c)
                    with sp.Else():
                        sp.wait_ge(v_low, L * NCH * 4)
                        for rows, tiles in x_parts:
                            sp.dma_start(rows, x.rearrange("(t p) d -> p t d", p=TP)[:, tiles, :])\
                                .then_inc(xr_in, 16)

            @block.gpsimd
            def _(pool):
                with pool.Fori(0, L) as l:
                    pool.wait_ge(tab_out, (l + 1) * 16 * NCH)
                    pool.sem_inc(pool_pace)

                    def gather(g, i, b):
                        pool.wait_ge(meta_in[b], (l * NIT + i + 1) * 16)
                        pool.wait_ge(e_out, l * NG + g + 1)
                        pool.sem_inc(pool_pace)
                        for j in range(2):
                            nc.gpsimd.indirect_dma_start(
                                e_sb[:, b % 4, j, :], None, table,
                                bass.IndirectOffsetOnAxis(ap=meta[:, b, j, SRC:SRC + 1], axis=0),
                                compute_op=ALU.add).then_inc(gathered[b % 4], 16)

                    with pool.Fori(0, NIT) as i:
                        for b in range(UN):
                            gather(i * UN + b, i, b)
                    with pool.If(l < L - 1):
                        for c, (t0, nt) in enumerate(CH):
                            if c not in TAB_VECTOR:
                                pool.wait_ge(w_in, (l + 2) * 16 * W_LOADS)
                                pool.wait_ge(h_rows, (l + 1) * NT + t0 + nt)
                                make_table(nc.gpsimd, c)

            def z2_out(act, l, c):
                t0, nt = CH[c]
                n = nt * TP
                for f in range(2):
                    act.wait_ge(z2_mm, l * NCH * 2 + c * 2 + f + 1)
                    nc.scalar.activation(z2[:, f, t0 * TP:t0 * TP + n], ps[:, (c % 2) * 2 + f, 0:n], ACT.Identity,
                                         bias=vec[:, V_B2 + f:V_B2 + f + 1]).then_inc(z2_ev, 1)

            @block.scalar
            def _(act):
                with act.Fori(0, L) as l:
                    def hidden_high(g, b):
                        act.wait_ge(mm1, l * NG + g + 1)
                        if is_past(g, 2):
                            act.wait_ge(mm2, l * NG + g - 1)
                        nc.scalar.activation(hid_h[:, b, :, :].rearrange("p a c -> p (a c)"), ps[:, b, :],
                                             ACT.Relu).then_inc(hid_high, 1)

                    def evacuate(g, i, b):
                        act.wait_ge(mm2, l * NG + g + 1)
                        if is_past(g, 4):
                            act.wait_ge(msg_low, l * NG + g - 3)
                        nc.scalar.copy(e_sb[:, b % 4, :, :].rearrange("p a c -> p (a c)"), ps[:, 2 + b % 2, :])\
                            .then_inc(e_out, 1)

                    def message_high(g, turn4, b):
                        act.wait_ge(gathered[b % 4], turn4 * 32)
                        if is_past(g, 2):
                            act.wait_ge(mm3, l * NG + g - 1)
                        nc.scalar.activation(msg_h[:, b % 2, :, :], e_sb[:, b % 4, :, :], ACT.Relu)\
                            .then_inc(msg_high, 1)

                    def turns4(g):
                        return l * (NG // 4) + g // 4 + 1

                    hidden_high(0, 0)

                    def step(g, i, b):
                        if has(g, 1):
                            hidden_high(g + 1, (b + 1) % 2)
                        if is_past(g, GATHER_LAG):
                            bb = (b - GATHER_LAG) % UN
                            back = 0 if b >= GATHER_LAG else 1
                            t4 = (turns4(g - GATHER_LAG) if isinstance(g, int)
                                  else l * (NG // 4) + (i - back) * 2 + bb // 4 + 1)
                            message_high(g - GATHER_LAG, t4, bb)
                        evacuate(g, i, b)

                    groups_loop(act, step)
                    for g in range(NG - GATHER_LAG, NG):
                        message_high(g, turns4(g), g % UN)

                    def z_out(c):
                        n = CH[c][1] * TP
                        act.wait_ge(z_tr, l * NCH + c + 1)
                        if c >= 2:
                            act.wait_ge(u_mm, l * NCH * 4 + (c - 1) * 4)
                        nc.scalar.copy(z_h[:, c % 2, :, 0:n], ps[:, 6:8, 0:n]).then_inc(z_high, 1)

                    z_out(0)
                    for c, (t0, nt) in enumerate(CH):
                        n = nt * TP
                        if c + 1 < NCH:
                            z_out(c + 1)
                        for f in range(4):
                            act.wait_ge(u_mm, l * NCH * 4 + c * 4 + f + 1)
                            nc.scalar.activation(u[:, f, t0 * TP:t0 * TP + n], ps[:, f, 0:n], ACT.Identity,
                                                 bias=vec[:, V_B1 + f:V_B1 + f + 1]).then_inc(u_ev, 1)
                    sqrt_for(act, 128, 4, l * 2 + 2)
                    edge_weights_high(act, l + 1)
                    act.wait_ge(bn1_ready, l + 1)
                    for c, (t0, nt) in enumerate(CH):
                        n = nt * TP
                        def v_out(f):
                            cols = u[:, f, t0 * TP:t0 * TP + n]
                            nc.scalar.activation(cols, cols, ACT.Relu, bias=r_o[:, f:f + 1],
                                                 scale=r_s[:, f:f + 1]).then_inc(v_made, 1)

                        def v_out_high(f):
                            act.wait_ge(v_made, l * NCH * 4 + c * 4 + f + 1)
                            if c >= 2:
                                act.wait_ge(z2_mm, l * NCH * 2 + (c - 1) * 2)
                            nc.scalar.copy(v_h[:, c % 2, f, 0:n], u[:, f, t0 * TP:t0 * TP + n])\
                                .then_inc(v_high, 1)

                        v_out(0)
                        if c == 0:
                            v_out_high(0)
                        v_out(1)
                        if c > 0:
                            v_out_high(0)
                        v_out_high(1)
                        v_out(2)
                        v_out(3)
                        if c >= 1:
                            z2_out(act, l, c - 1)
                    z2_out(act, l, NCH - 1)
                    sqrt_for(act, 128, 2, l * 2 + 3)
                    node_weights_high(act, l + 1, second=False)
                    act.wait_ge(bn2_ready, l + 1)
                    for c, (t0, nt) in enumerate(CH):
                        for f in range(2):
                            a = z2[:, f, t0 * TP:(t0 + nt) * TP]
                            nc.scalar.activation(a, a, ACT.Identity, bias=r_o[:, f:f + 1],
                                                 scale=r_s[:, f:f + 1]).then_inc(zn_made, 1)
                    node_weights_high(act, l + 1, first=False)

            def bn_affine(link, dve, n, v_g, v_b, asked, ready):
                y = rsqrt(link, dve, mv[:, 0:n, 1], 128, n, asked)
                link(nc.vector.tensor_tensor(r_s[:, 0:n], y, vec[:, v_g:v_g + n], ALU.mult))
                link(nc.vector.tensor_tensor(r_t[:, 0:n], mv[:, 0:n, 0], r_s[:, 0:n], ALU.mult))
                nc.vector.tensor_tensor(r_o[:, 0:n], vec[:, v_b:v_b + n], r_t[:, 0:n], ALU.subtract)\
                    .then_inc(ready, 1)

            @block.vector
            def _(dve):
                vc = nc.vector
                with dve.Fori(0, L) as l:
                    CL = 1 + 14 + 4 + 3
                    link = Link(dve, d_lay, l * CL)
                    link(vc.tensor_copy(vec[:, :], vec_all[:, ds(l, 1), :].rearrange("p a v -> p (a v)")))

                    def hidden_low(g, b):
                        dve.wait_ge(hid_high, l * NG + g + 1)
                        vc.scalar_tensor_tensor(
                            out=hid_l[:, b, :, :].rearrange("p a c -> p (a c)"), in0=ps[:, b, :], scalar=0.0,
                            in1=hid_h[:, b, :, :].rearrange("p a c -> p (a c)").bitcast(F32), op0=ALU.max,
                            op1=ALU.subtract).then_inc(hid_low, 1)

                    def message_low(g, turn, b):
                        dve.wait_ge(meta_in[b], turn * 16)
                        if is_past(g, 2):
                            dve.wait_ge(mm3, l * NG + g - 1)
                        for j in range(2):
                            p = vc.tensor_scalar(pick[:, b % 2, j, 0:TP], iota_n[:, :],
                                                 meta_f[:, b, j, DST:DST + 1], tile_base[:, ds(g, 1)],
                                                 ALU.subtract, ALU.is_equal)
                        p.then_inc(picked, 1)
                        dve.wait_ge(msg_high, l * NG + g + 1)
                        vc.scalar_tensor_tensor(
                            out=msg_l[:, b % 2, :, :].rearrange("p a c -> p (a c)"),
                            in0=e_sb[:, b % 4, :, :].rearrange("p a c -> p (a c)"), scalar=0.0,
                            in1=msg_h[:, b % 2, :, :].rearrange("p a c -> p (a c)").bitcast(F32), op0=ALU.max,
                            op1=ALU.subtract).then_inc(msg_low, 1)

                    def add_sums(g, b):
                        t = dve.value_load(group_tile[0:1, ds(g, 1)], min_val=0, max_val=NT - 1)
                        dve.wait_ge(mm3, l * NG + g + 1)
                        if is_past(g, 1):
                            dve.wait_ge(added, l * NG + g)
                        else:
                            dve.wait_ge(agg_set, (l + 1) * 3)
                        dst_tile = agg[0:TP, ds(t, 1), :].rearrange("p a d -> p (a d)")
                        vc.tensor_tensor(dst_tile, dst_tile, ps[0:TP, 4 + b % 2, 0:D], ALU.add).then_inc(added, 1)

                    hidden_low(0, 0)

                    def step(g, i, b):
                        if has(g, 1):
                            hidden_low(g + 1, (b + 1) % 2)
                        if isinstance(g, int) and g < 3:
                            third = slice(g * NT // 3, (g + 1) * NT // 3)
                            vc.tensor_scalar(agg[0:TP, third, :], h[0:TP, third, :], vec[0:TP, V_EPS:V_EPS + 1],
                                             None, ALU.mult).then_inc(agg_set, 1)
                        if isinstance(g, int) and g == 3:
                            low_of(dve, m2_l, m2_raw, m2_h, m2_high, l + 1, m2_low)
                        if is_past(g, GATHER_LAG):
                            bb = (b - GATHER_LAG) % UN
                            back = 0 if b >= GATHER_LAG else 1
                            message_low(g - GATHER_LAG, l * NIT + i - back + 1, bb)
                        if is_past(g, LAG_A):
                            add_sums(g - LAG_A, (b - LAG_A) % UN)

                    groups_loop(dve, step)
                    for k in range(NG - GATHER_LAG, NG + LAG_A - GATHER_LAG):
                        if k < NG:
                            message_low(k, l * NIT + NIT, k % UN)
                        k -= LAG_A - GATHER_LAG
                        add_sums(k, k % UN)

                    def z_out(c):
                        n = CH[c][1] * TP
                        dve.wait_ge(z_high, l * NCH + c + 1)
                        vc.tensor_tensor(z_l[:, c % 2, :, 0:n], ps[:, 6:8, 0:n],
                                         z_h[:, c % 2, :, 0:n].bitcast(F32), ALU.subtract).then_inc(z_low, 1)

                    z_out(0)
                    for c, (t0, nt) in enumerate(CH):
                        n = nt * TP
                        if c + 1 < NCH:
                            z_out(c + 1)
                        for f in range(4):
                            dve.wait_ge(u_ev, l * NCH * 4 + c * 4 + f + 1)
                            last = vc.bn_stats(st1[:, f, c, :], u[:, f, t0 * TP:t0 * TP + n])
                    link(last)
                    dve.sem_inc(dve_pace)
                    for f in range(4):
                        last = vc.bn_aggr(mv[:, f, :], st1[:, f, :, :].rearrange("p c s -> p (c s)"))
                    link(last)
                    bn_affine(link, dve, 4, V_G1, V_BB1, l * 2 + 2, bn1_ready)

                    def v_out(c):
                        t0, nt = CH[c]
                        n = nt * TP

                        def cols(f):
                            return u[:, f, t0 * TP:t0 * TP + n]

                        def low(f):
                            vc.tensor_tensor(v_l[:, c % 2, f, 0:n], cols(f), v_h[:, c % 2, f, 0:n].bitcast(F32),
                                             ALU.subtract).then_inc(v_low, 1)

                        for f in range(2):
                            dve.wait_ge(v_high, l * NCH * 2 + c * 2 + f + 1)
                            low(f)
                        for f in range(2, 4):
                            dve.wait_ge(v_made, l * NCH * 4 + c * 4 + f + 1)
                            vc.tensor_copy(v_h[:, c % 2, f, 0:n], cols(f)).then_inc(v_high_d, 1)
                        for f in range(2, 4):
                            dve.wait_ge(v_high_d, l * NCH * 2 + c * 2 + f - 1)
                            low(f)

                    v_out(0)
                    edge_weights_low(link, dve, l + 1)
                    for c, (t0, nt) in enumerate(CH):
                        if c + 1 < NCH:
                            v_out(c + 1)
                        for f in range(2):
                            dve.wait_ge(z2_ev, l * NCH * 2 + c * 2 + f + 1)
                            last = vc.bn_stats(st2[:, f, c, :], z2[:, f, t0 * TP:(t0 + nt) * TP])
                    link(last)
                    dve.sem_inc(dve_pace)
                    for f in range(2):
                        last = vc.bn_aggr(mv[:, f, :], st2[:, f, :, :].rearrange("p c s -> p (c s)"))
                    link(last)
                    bn_affine(link, dve, 2, V_G2, V_BB2, l * 2 + 3, bn2_ready)
                    low_of(dve, m1_l, m1_raw, m1_h, m1_high, l + 2, m1_low)
                    for k, (t0, nt) in enumerate(PAIRS):
                        dve.wait_ge(zn_tr, l * NPAIR + k + 1)
                        rows = h[0:TP, t0:t0 + nt, :].rearrange("p t d -> p (t d)")
                        vc.scalar_tensor_tensor(out=rows, in0=ps[0:TP, k % 4, 0:nt * D],
                                                scalar=vec[0:TP, V_FLOOR:V_FLOOR + 1], in1=rows,
                                                op0=ALU.max, op1=ALU.add).then_inc(h_rows, nt)
                        for c in TAB_VECTOR:
                            if t0 == min(sum(CH[c]), NT - 1):
                                dve.wait_ge(w_in, (l + 2) * 16 * W_LOADS)
                                dve.wait_ge(h_rows, (l + 1) * NT + sum(CH[c]))
                                make_table(vc, c)
                    dve.wait_ge(h_rows, (l + 2) * NT)
                    assert link.n == CL, link.n

            @block.tensor
            def _(pe):
                with pe.Fori(0, L) as l:
                    pe.wait_ge(w_ready, l + 1)
                    pe.wait_ge(h_rows, (l + 1) * NT)

                    def hidden(g, turn, b):
                        pe.wait_ge(at_in[b], turn * 16)
                        if is_past(g, 2):
                            pe.wait_ge(hid_low, l * NG + g - 1)
                        for half in range(2):
                            last = nc.tensor.matmul(ps[:, b % 2, half * GS:(half + 1) * GS],
                                                    w1_s[:, half * 128:(half + 1) * 128], at[:, b, :],
                                                    start=True, stop=True)
                        last.then_inc(mm1, 1)

                    def edge_out(g, b):
                        pe.wait_ge(hid_low, l * NG + g + 1)
                        if is_past(g, 2):
                            pe.wait_ge(e_out, l * NG + g - 1)
                        s = b % 2
                        for j in range(2):
                            terms = [(a, w, k) for k in range(2)
                                     for a, w in ((hid_h, w2_h), (hid_h, w2_l), (hid_l, w2_h))]
                            for n, (a, w, k) in enumerate(terms):
                                last = nc.tensor.matmul(ps[:, 2 + s, j * D:(j + 1) * D],
                                                        a[:, s, k, j * 128:(j + 1) * 128], w[:, k, :],
                                                        start=(n == 0), stop=(n == len(terms) - 1))
                        last.then_inc(mm2, 1)

                    def sums(g, b):
                        pe.wait_ge(picked, l * NG + g + 1)
                        pe.wait_ge(msg_low, l * NG + g + 1)
                        if is_past(g, 2):
                            pe.wait_ge(added, l * NG + g - 1)
                        s = b % 2
                        for n, (j, m) in enumerate(((0, msg_h), (0, msg_l), (1, msg_h), (1, msg_l))):
                            last = nc.tensor.matmul(ps[0:TP, 4 + s, 0:D], pick[:, s, j, 0:TP], m[:, s, j, :],
                                                    start=(n == 0), stop=(n == 3))
                        last.then_inc(mm3, 1)

                    hidden(0, l * NIT + 1, 0)

                    def step(g, i, b):
                        if has(g, 1):
                            hidden(g + 1, l * NIT + i + 1 + (b + 1) // UN, (b + 1) % UN)
                        edge_out(g, b)
                        if is_past(g, LAG):
                            sums(g - LAG, b)

                    groups_loop(pe, step)
                    for k in range(NG - LAG, NG):
                        sums(k, k)

                    pe.wait_ge(added, (l + 1) * NG)
                    pe.wait_ge(m1_low, l + 1)
                    def z_transposed(c):
                        t0, nt = CH[c]
                        for half in range(2):
                            for t in range(nt):
                                last = nc.tensor.transpose(ps[:, 6 + half, t * TP:(t + 1) * TP],
                                                           agg[0:TP, t0 + t, half * 128:(half + 1) * 128],
                                                           ident[0:TP, 0:TP])
                        last.then_inc(z_tr, 1)

                    z_transposed(0)
                    for c, (t0, nt) in enumerate(CH):
                        n = nt * TP
                        pe.wait_ge(z_low, l * NCH + c + 1)
                        if c + 1 < NCH:
                            z_transposed(c + 1)
                        for f in range(4):
                            if c >= 1:
                                pe.wait_ge(u_ev, l * NCH * 4 + (c - 1) * 4 + f + 1)
                            terms = [(w, a, k) for k in range(2)
                                     for w, a in ((m1_h, z_h), (m1_h, z_l), (m1_l, z_h))]
                            for i, (w, a, k) in enumerate(terms):
                                last = nc.tensor.matmul(ps[:, f, 0:even(n)], w[:, k, f * 128:(f + 1) * 128],
                                                        a[:, c % 2, k, 0:even(n)], start=(i == 0),
                                                        stop=(i == len(terms) - 1))
                            last.then_inc(u_mm, 1)
                    for _ in range(IDLE_PRODUCTS):
                        nc.tensor.matmul(ps[:, 4, 0:500], m1_h[:, 0, 0:128], z_l[:, 1, 0, :], start=True, stop=True)
                    for c, (t0, nt) in enumerate(CH):
                        n = nt * TP
                        if c == 0:
                            pe.wait_ge(m2_low, l + 1)
                        if c >= 2:
                            pe.wait_ge(z2_ev, l * NCH * 2 + (c - 1) * 2)
                        for k in range(4):
                            pe.wait_ge(v_low, l * NCH * 4 + c * 4 + k + 1)
                            for f in range(2):
                                for i, (w, a) in enumerate(((m2_h, v_h), (m2_h, v_l), (m2_l, v_h))):
                                    last = nc.tensor.matmul(ps[:, (c % 2) * 2 + f, 0:even(n)],
                                                            w[:, k, f * 128:(f + 1) * 128],
                                                            a[:, c % 2, k, 0:even(n)],
                                                            start=(k == 0 and i == 0), stop=(k == 3 and i == 2))
                                if k == 3:
                                    last.then_inc(z2_mm, 1)
                    for _ in range(IDLE_PRODUCTS):
                        nc.tensor.matmul(ps[:, 4, 0:500], w2_h[:, 0, 0:128], v_l[:, 1, 0, :], start=True, stop=True)
                    for c, (t0, nt) in enumerate(CH):
                        pe.wait_ge(zn_made, l * NCH * 2 + c * 2 + 2)
                        for t in range(t0, t0 + nt):
                            if t % 2 == 0 and t >= 8:
                                pe.wait_ge(h_rows, (l + 1) * NT + t - 6)
                            for f in range(2):
                                at_col = t % 2 * D + f * 128
                                last = nc.tensor.transpose(ps[0:TP, t // 2 % 4, at_col:at_col + 128],
                                                           z2[:, f, t * TP:(t + 1) * TP], ident[:, :])
                            if t % 2 == 1 or t == NT - 1:
                                last.then_inc(zn_tr, 1)

        with nc.Block() as block:
            @block.sync
            def _(sp):
                for b in range(UN):
                    sp.wait_ge(at_in[b], 16 * (L * NIT + 1))
                    sp.wait_ge(meta_in[b], 16 * (L * NIT + 1))
                sp.wait_ge(w_in, 16 * W_LOADS * (L + 1))
                sp.wait_ge(m_in, 16 * M_LOADS * (L + 1))
                sp.wait_ge(tab_out, 16 * NCH * L)
                big = [(sW1_s[:, :, :], sW1.rearrange("(k p) f -> p k f", p=128)),
                       (sW2_s[:, :, :], sW2.rearrange("(k p) f -> p k f", p=128)),
                       (sW3_s[:, :], sW3)]
                for e in range(NE):
                    half = slice((e % 2) * EH2, (e % 2 + 1) * EH2)
                    big += [(eW1_s[:, e, :, :], eW1[e, :, :].rearrange("(k p) f -> p k f", p=128)),
                            (eW2_s[:, e, half], eW2[e, :, :]),
                            (eW3_s[half, e // 2, :], eW3[e, :, :])]
                for o, i in ((b_out[0:1, :], sb3.unsqueeze(0)), (b_out[1:1 + NE, :], eb3)):
                    sp.dma_start(o, i).then_inc(moe_in, 16)
                sp.wait_ge(x_added, 3)
                for o, i in big:
                    sp.dma_start(o, i).then_inc(moe_in, 16)
                sp.wait_ge(moe_in, 16 * (len(big) + 2))
                sp.sem_inc(moe_here)
                for c, (t0, nt) in enumerate(CH):
                    sp.wait_ge(out_made, t0 + nt)
                    sp.dma_start(out.rearrange("(t p) d -> p t d", p=TP)[:, t0:t0 + nt, :],
                                 h[0:TP, t0:t0 + nt, :]).then_inc(out_done, 16)
                sp.wait_ge(out_done, 16 * NCH)

            X_HALF = NT // 2 + 4

            e1_all = agg_flat[:, 0:4000].rearrange("p (s e c) -> p s e c", s=2, e=NE)
            h1_all = e_sb[:, :, :, :].rearrange("p a b c -> p (a b c)")[:, 0:2000]\
                .rearrange("p (s a c) -> p s a c", s=2, a=2)

            def h1_of(c):
                return h1_all[:, c % 2, :, :]

            def e1_of(c):
                return e1_all[:, c % 2, :, :]

            h2_all = u_flat[:, 6400:7400].rearrange("p (s n) -> p s n", s=2)
            e2_all = u_flat[:, 7400:9400].rearrange("p (s q n) -> p s q n", s=2, q=2)

            def e2_of(c):
                return e2_all[:, c % 2, :, :]

            def units(c):
                t0, nt = CH[c]
                n = nt * TP
                y = [yT[:, k, t0 * TP:t0 * TP + n] for k in range(2)]
                got = [([(sW1_s[:, k, f * 128:(f + 1) * 128], y[k]) for k in range(2)],
                        sb1_s[:, f:f + 1], h1_of(c)[:, f, 0:n]) for f in range(2)]
                got += [([(eW1_s[:, e, k, :], y[k]) for k in range(2)],
                         eb1_s[:, e:e + 1], e1_of(c)[:, e, 0:n]) for e in range(NE)]
                got += [([(sW2_s[:, k, :], h1_of(c)[:, k, 0:n]) for k in range(2)],
                         sb2_s[:, 0:1], h2_all[:, c % 2, 0:n])]
                got += [([(eW2_s[:, 2 * q + r, :], e1_of(c)[:, 2 * q + r, 0:n]) for r in range(2)],
                         eb2_s[:, q:q + 1], e2_of(c)[:, q, 0:n]) for q in range(2)]
                return got

            @block.vector
            def _(dve):
                vc = nc.vector
                link = Link(dve, d_moe)
                dve.wait_ge(xr_in, 32)
                dve.wait_ge(tab_out, 16 * NCH * L)
                link(vc.tensor_tensor(h[0:TP, 0:X_HALF, :], h[0:TP, 0:X_HALF, :], x_parts[0][0][:, 0:X_HALF, :],
                                      ALU.add))
                norm_stats(link, h, 0, X_HALF)
                dve.wait_ge(x_added, 2)
                vc.memset(eW2_s[:, :, :], 0.0).then_inc(x_added, 1)
                norm_stats(link, h, X_HALF, NT - X_HALF)
                norm_scales(link, dve, 0, NT, 2 * L + 2)

                def y_out(c):
                    t0, nt = CH[c]
                    dve.wait_ge(y_tr, c + 1)
                    vc.tensor_copy(yT[:, 1, t0 * TP:(t0 + nt) * TP], ps[:, 2 * (c % 2) + 1, 0:nt * TP])\
                        .then_inc(y_ev1, 1)

                norm_apply(h, agg, *CH[0], y_made)
                norm_apply(h, agg, *CH[1], y_made)
                y_out(0)
                for c, (t0, nt) in enumerate(CH):
                    if c + 2 < NCH:
                        norm_apply(h, agg, *CH[c + 2], y_made)
                    if c + 1 < NCH:
                        y_out(c + 1)
                    dve.wait_ge(lg_mm, c + 1)
                    vc.tensor_tensor(lg[0:TP, t0:t0 + nt, :],
                                     ps[0:TP, 4 + c % 2, 0:nt * NE].rearrange("p (t e) -> p t e", e=NE),
                                     gb_s[0:TP, :].unsqueeze(1).to_broadcast([TP, nt, NE]), ALU.add)\
                        .then_inc(lg_ev, 1)
                dve.wait_ge(lg_ev, NCH)
                mx, sm = r_a[0:TP, 0:NT], r_s[0:TP, 0:NT]

                def over(a):
                    return a.unsqueeze(2).to_broadcast([TP, NT, NE])

                g_, p_ = lg[0:TP, :, :], pr[0:TP, :, :]
                link(vc.tensor_reduce(mx, g_, AX, ALU.max))
                vc.tensor_tensor(g_, g_, over(mx), ALU.subtract).then_inc(ex_ask, 1)
                dve.wait_ge(ex_done, 1)
                link(vc.tensor_reduce(sm, p_, AX, ALU.add))
                link(vc.reciprocal(sm, sm))
                link(vc.tensor_tensor(p_, p_, over(sm), ALU.mult))
                link(vc.memset(rk[:, :, :], 0.0))
                for j in range(NE):
                    for k in range(j + 1, NE):
                        link(vc.tensor_tensor(cmp[0:TP, :], pr[0:TP, :, j], pr[0:TP, :, k], ALU.is_ge))
                        link(vc.tensor_tensor(rk[0:TP, k, :], rk[0:TP, k, :], cmp[0:TP, :], ALU.add))
                        link(vc.tensor_tensor(cmp[0:TP, :], pr[0:TP, :, k], pr[0:TP, :, j], ALU.is_gt))
                        link(vc.tensor_tensor(rk[0:TP, j, :], rk[0:TP, j, :], cmp[0:TP, :], ALU.add))
                link(vc.tensor_reduce(mx, p_, AX, ALU.max))
                vc.tensor_tensor(g_, p_, over(mx), ALU.subtract).then_inc(ex_ask, 1)
                dve.wait_ge(ex_done, 2)
                link(vc.scalar_tensor_tensor(out=p_, in0=rk[0:TP, :, :].rearrange("p e t -> p t e"), scalar=2.0,
                                             in1=p_, op0=ALU.is_lt, op1=ALU.mult))
                link(vc.tensor_reduce(sm, p_, AX, ALU.add))
                link(vc.reciprocal(sm, sm))
                link(vc.memset(w5[0:TP, :, 0:1], 1.0))
                vc.tensor_tensor(w5[0:TP, :, 1:1 + NE], p_, over(sm), ALU.mult).then_inc(w_made, 1)
                nd = 0
                for c, (t0, nt) in enumerate(CH):
                    n = nt * TP
                    nd += 1
                    dve.wait_ge(d_mm, nd)
                    vc.tensor_copy(wT[:, c % 2, 0:n], ps[0:1 + NE, 4 + (nd - 1) % 4, 0:n]).then_inc(d_ev, 1)
                    for q in range(2):
                        nd += 1
                        dve.wait_ge(d_mm, nd)
                        dve.wait_ge(a_ev, c * 9 + 8 + q)
                        e2 = e2_of(c)[:, q, 0:n]
                        vc.tensor_tensor(e2, e2, ps[:, 4 + (nd - 1) % 4, 0:n], ALU.mult).then_inc(d_ev, 1)
                    for t in range(t0, t0 + nt):
                        nd += 1
                        dve.wait_ge(d_mm, nd)
                        vc.tensor_tensor(h[0:TP, t, :], ps[0:TP, 4 + (nd - 1) % 4, 0:D], h[0:TP, t, :],
                                         ALU.add).then_inc(out_made, 1)

            @block.gpsimd
            def _(pool):
                pool.wait_ge(xr_in, 32)
                for (rows, tiles), first in zip(x_parts, (X_HALF, XT)):
                    o = h[0:TP, first:tiles.stop, :]
                    nc.gpsimd.tensor_tensor(o, o, rows[:, first - tiles.start:, :], ALU.add).then_inc(x_added, 1)

            @block.scalar
            def _(act):
                sqrt_for(act, TP, NT, 2 * L + 2)
                act.wait_ge(tab_out, 16 * NCH * L)
                for c, (t0, nt) in enumerate(CH):
                    n = nt * TP
                    act.wait_ge(y_tr, c + 1)
                    nc.scalar.copy(yT[:, 0, t0 * TP:t0 * TP + n], ps[:, 2 * (c % 2), 0:n]).then_inc(y_ev0, 1)

                def exp_for(k):
                    act.wait_ge(ex_ask, k)
                    nc.scalar.activation(pr[0:TP, :, :], lg[0:TP, :, :], ACT.Exp).then_inc(ex_done, 1)

                exp_for(1)
                na = 0
                for c, (t0, nt) in enumerate(CH):
                    if c >= 2:
                        act.wait_ge(out_made, CH[c - 1][0])
                    for _, bias, where in units(c):
                        if na == 4:
                            exp_for(2)
                        na += 1
                        act.wait_ge(a_mm, na)
                        nc.scalar.activation(where, ps[:, (na - 1) % 4, 0:nt * TP], ACT.Relu, bias=bias)\
                            .then_inc(a_ev, 1)

            @block.tensor
            def _(pe):
                def y_transposed(c):
                    t0, nt = CH[c]
                    pe.wait_ge(y_made, t0 + nt)
                    if c >= 2:
                        pe.wait_ge(y_ev0, c - 1)
                        pe.wait_ge(y_ev1, c - 1)
                    for half in range(2):
                        for t in range(nt):
                            last = nc.tensor.transpose(ps[:, 2 * (c % 2) + half, t * TP:(t + 1) * TP],
                                                       agg[0:TP, t0 + t, half * 128:(half + 1) * 128],
                                                       ident[0:TP, 0:TP])
                    last.then_inc(y_tr, 1)

                y_transposed(0)
                for c, (t0, nt) in enumerate(CH):
                    n = nt * TP
                    if c + 1 < NCH:
                        y_transposed(c + 1)
                    pe.wait_ge(y_ev0, c + 1)
                    pe.wait_ge(y_ev1, c + 1)
                    if c >= 2:
                        pe.wait_ge(lg_ev, c - 1)
                    for t in range(nt):
                        for k in range(2):
                            last = nc.tensor.matmul(ps[0:TP, 4 + c % 2, t * NE:(t + 1) * NE],
                                                    yT[:, k, (t0 + t) * TP:(t0 + t + 1) * TP], gW_s[:, k, :],
                                                    start=(k == 0), stop=(k == 1))
                    last.then_inc(lg_mm, 1)
                pe.wait_ge(moe_here, 1)
                na, nd = 0, 0

                def bank_d():
                    nonlocal nd
                    if nd >= 4:
                        s, value = readers[nd - 4]
                        pe.wait_ge(s, value)
                    nd += 1
                    return 4 + (nd - 1) % 4

                readers = []
                for c, (t0, nt) in enumerate(CH):
                    readers += [(d_ev, 3 * c + k + 1) for k in range(3)]
                    readers += [(out_made, t + 1) for t in range(t0, t0 + nt)]

                def hidden_of(c):
                    nonlocal na
                    n = CH[c][1] * TP
                    for k, (terms, _, _) in enumerate(units(c)):
                        if k == 6:
                            pe.wait_ge(a_ev, 9 * c + 2)
                        if k == 7:
                            pe.wait_ge(a_ev, 9 * c + 6)
                        if na >= 4:
                            pe.wait_ge(a_ev, na - 3)
                        for m, (w, r) in enumerate(terms):
                            last = nc.tensor.matmul(ps[:, na % 4, 0:n], w, r, start=(m == 0),
                                                    stop=(m == len(terms) - 1))
                        last.then_inc(a_mm, 1)
                        na += 1
                        if c >= 1 and k == 4:
                            gates_of(c - 1)
                        if c >= 1 and k == 6:
                            spread_gates_of(c - 1)

                def gates_of(c):
                    t0, nt = CH[c]
                    if c == 0:
                        pe.wait_ge(w_made, 1)
                    b = bank_d()
                    for t in range(nt):
                        last = nc.tensor.transpose(ps[0:1 + NE, b, t * TP:(t + 1) * TP],
                                                   w5[0:TP, t0 + t, :], ident[0:TP, 0:TP])
                    last.then_inc(d_mm, 1)

                def spread_gates_of(c):
                    n = CH[c][1] * TP
                    pe.wait_ge(d_ev, 3 * c + 1)
                    for q in range(2):
                        b = bank_d()
                        nc.tensor.matmul(ps[:, b, 0:n], sel[:, q, :], wT[:, c % 2, 0:n], start=True, stop=True)\
                            .then_inc(d_mm, 1)

                def outputs_of(c):
                    t0, nt = CH[c]
                    pe.wait_ge(a_ev, 9 * c + 7)
                    pe.wait_ge(d_ev, 3 * c + 3)
                    for t in range(nt):
                        cols = slice(t * TP, (t + 1) * TP)
                        b = bank_d()
                        terms = [(h2_all[:, c % 2, cols], sW3_s[:, :])]
                        terms += [(e2_of(c)[:, q, cols], eW3_s[:, q, :]) for q in range(2)]
                        terms += [(wT[:, c % 2, cols], b_out[:, :])]
                        for m, (w, r) in enumerate(terms):
                            last = nc.tensor.matmul(ps[0:TP, b, 0:D], w, r, start=(m == 0), stop=(m == 3))
                        last.then_inc(d_mm, 1)

                hidden_of(0)
                for c in range(NCH):
                    if c + 1 < NCH:
                        hidden_of(c + 1)
                    else:
                        gates_of(c)
                        spread_gates_of(c)
                    outputs_of(c)


_INS = ['x', 'src', 'dst', 'edge_attr_16', 'L0_gnn_ee_w1', 'L0_gnn_ee_b1', 'L0_gnn_ee_w2', 'L0_gnn_ee_b2',
        'L0_gnn_eps', 'L0_gnn_mlp_w1', 'L0_gnn_mlp_b1', 'L0_gnn_bn1_g', 'L0_gnn_bn1_b', 'L0_gnn_mlp_w2',
        'L0_gnn_mlp_b2', 'L0_gnn_bn_g', 'L0_gnn_bn_b', 'L0_ffn_sW1', 'L0_ffn_sb1', 'L0_ffn_sW2', 'L0_ffn_sb2',
        'L0_ffn_sW3', 'L0_ffn_sb3', 'L0_ffn_eW1', 'L0_ffn_eb1', 'L0_ffn_eW2', 'L0_ffn_eb2', 'L0_ffn_eW3',
        'L0_ffn_eb3', 'L0_ffn_gW', 'L0_ffn_gb']


def kernel(**inputs):
    import numpy as _np
    import concourse.bacc as _bacc
    from concourse import mybir as _mybir
    from concourse.bass_utils import run_bass_kernel_spmd as _run

    nc = _bacc.Bacc("TRN2", target_bir_lowering=False, num_devices=1)
    arrays, args = {}, []
    for name in _INS:
        a = _np.ascontiguousarray(inputs[name])
        arrays[f"in_{name}_dram"] = a
        args.append(nc.dram_tensor(f"in_{name}_dram", a.shape, _mybir.dt.from_np(a.dtype), kind="ExternalInput").ap())
    args.append(nc.dram_tensor("out_dram", (3125, 256), _mybir.dt.float32, kind="ExternalOutput").ap())
    gnn_moe_kernel(nc, *args)
    r = _run(nc, [arrays], core_ids=[0])
    return r.results[0]["out_dram"]
```
